# Optimizing a Trainium2 kernel written in Bass

```python
import numpy as np
import jax
import jax.numpy as jnp

def _softmax(x, axis=-1):
    return jax.nn.softmax(x, axis=axis)

def _gelu(x):
    return jax.nn.gelu(x, approximate=True)

def _silu(x):
    return jax.nn.silu(x)

def _sigmoid(x):
    return jax.nn.sigmoid(x)

def _layernorm(x, axis=-1, eps=1e-05):
    m = jnp.mean(x, axis=axis, keepdims=True)
    v = jnp.var(x, axis=axis, keepdims=True)
    return (x - m) / jnp.sqrt(v + eps)

def _scatter_add(tgt, idx, src, axis=0):
    return tgt.at[idx].add(src)

def _segment_sum(src, seg, n):
    return jax.ops.segment_sum(src, seg, n)
kernel_name = 'mk_early_fusion_embed_d2_tok_img768_r4_526050'

def setup_inputs(seed: int=0):
    np.random.seed(seed)
    _w = jnp.asarray

    def _rec_inputs():
        import jax
        import jax.numpy as jnp
        _rk = jax.random.key(seed)
        x = -0.000137204 + 0.999937 * jax.random.normal(jax.random.fold_in(_rk, 1), (4, 3, 224, 224), jnp.float32)
        x_txt = jax.random.randint(jax.random.fold_in(_rk, 51), (4, 512), 0, 12564, jnp.int32)
        return (x, x_txt)
    x, x_txt = _rec_inputs()

    def _L0_tok_setup():
        import jax, jax.numpy as jnp
        import numpy as np
        B, C, H, W_IMG = (128, 3, 224, 224)
        N_PATCH, EMBED = (256, 192)
        GRID = 32
        key = jax.random.key(seed)
        k1, k2, k3, k4 = jax.random.split(key, 4)
        x = jax.random.normal(k1, (B, C, H, W_IMG), dtype=jnp.float32)
        curve = jax.random.randint(k2, (N_PATCH, 2), 0, GRID, dtype=jnp.int32)
        proj_w = jax.random.normal(k3, (EMBED, C), dtype=jnp.float32) * 0.02
        proj_b = jax.random.normal(k4, (EMBED,), dtype=jnp.float32) * 0.02
        return {'x': x, 'curve': curve, 'proj_w': proj_w, 'proj_b': proj_b}
    _L0_tok_all = _L0_tok_setup()
    _L0_tok_in = {k: v for k, v in _L0_tok_all.items() if k in ('curve', 'proj_w', 'proj_b')}
    del _L0_tok_all

    def _L0_txt_setup():
        import jax, jax.numpy as jnp
        import numpy as np
        EMBED_DIM_LIST = (192, 96, 144, 192)
        MAX_EMBED_DIM = 192
        VOCAB = 50257
        BATCH, SEQ = (8, 512)
        key = jax.random.key(seed)
        k1, k2, k3 = jax.random.split(key, 3)
        x = jax.random.randint(k1, (BATCH, SEQ), 0, VOCAB, dtype=jnp.int64)
        weights = jax.random.uniform(k2, (len(EMBED_DIM_LIST),), dtype=jnp.float32)
        emb_weight = jax.random.normal(k3, (VOCAB, MAX_EMBED_DIM), dtype=jnp.float32) * 0.02
        return {'x': x, 'weights': weights, 'emb_weight': emb_weight}
    _L0_txt_all = _L0_txt_setup()
    _L0_txt_in = {k: v for k, v in _L0_txt_all.items() if k in ('weights', 'emb_weight')}
    del _L0_txt_all

    def _L0_attn_setup():
        import jax, jax.numpy as jnp
        import numpy as np
        H = 12
        BETA = 0.5
        LN_EPS = 1e-12

        def layer_norm(x, g, b):
            mu = x.mean(-1, keepdims=True)
            var = ((x - mu) ** 2).mean(-1, keepdims=True)
            return (x - mu) * jax.lax.rsqrt(var + LN_EPS) * g + b
        key = jax.random.key(seed)
        B, S, D, F, L = (16, 128, 192, 768, 4)
        ks = jax.random.split(key, 9)
        w = lambda k, shape: jax.random.normal(k, shape, jnp.float32) * 0.02
        return {'hidden_states': jax.random.normal(ks[0], (B, S, D), jnp.float32), 'Wq': w(ks[1], (L, D, D)), 'bq': jnp.zeros((L, D), jnp.float32), 'Wk': w(ks[2], (L, D, D)), 'bk': jnp.zeros((L, D), jnp.float32), 'Wv': w(ks[3], (L, D, D)), 'bv': jnp.zeros((L, D), jnp.float32), 'Wc': w(ks[4], (L, D, D)), 'bc': jnp.zeros((L, D), jnp.float32), 'Wo': w(ks[5], (L, D, D)), 'bo': jnp.zeros((L, D), jnp.float32), 'g1': jnp.ones((L, D), jnp.float32), 'b1': jnp.zeros((L, D), jnp.float32), 'Wi': w(ks[6], (L, D, F)), 'bi': jnp.zeros((L, F), jnp.float32), 'Wo2': w(ks[7], (L, F, D)), 'bo2': jnp.zeros((L, D), jnp.float32), 'g2': jnp.ones((L, D), jnp.float32), 'b2': jnp.zeros((L, D), jnp.float32)}
    _L0_attn_all = _L0_attn_setup()
    _L0_attn_in = {k: v for k, v in _L0_attn_all.items() if k in ('Wq', 'bq', 'Wk', 'bk', 'Wv', 'bv', 'Wc', 'bc', 'Wo', 'bo', 'g1', 'b1', 'Wi', 'bi', 'Wo2', 'bo2', 'g2', 'b2')}
    del _L0_attn_all

    def _L0_ffn_setup():
        import jax, jax.numpy as jnp
        import numpy as np
        HIDDEN = 192
        INNER = 128
        EPS = 1e-05
        key = jax.random.key(seed)
        ks = jax.random.split(key, 6)
        B, S = (8, 1024)
        x = jax.random.normal(ks[0], (B, S, HIDDEN), dtype=jnp.float32)
        W1 = jax.random.normal(ks[1], (INNER, HIDDEN), dtype=jnp.float32) * 0.02
        b1 = jnp.zeros((INNER,), dtype=jnp.float32)
        W2 = jax.random.normal(ks[2], (HIDDEN, INNER), dtype=jnp.float32) * 0.02
        b2 = jnp.zeros((HIDDEN,), dtype=jnp.float32)
        bound = 1.0 / np.sqrt(HIDDEN)
        Wo = jax.random.uniform(ks[3], (HIDDEN, HIDDEN), minval=-bound, maxval=bound, dtype=jnp.float32)
        bo = jax.random.uniform(ks[4], (HIDDEN,), minval=-bound, maxval=bound, dtype=jnp.float32)
        gamma = jnp.ones((HIDDEN,), dtype=jnp.float32)
        beta = jnp.zeros((HIDDEN,), dtype=jnp.float32)
        return {'x': x, 'W1': W1, 'b1': b1, 'W2': W2, 'b2': b2, 'Wo': Wo, 'bo': bo, 'gamma': gamma, 'beta': beta}
    _L0_ffn_all = _L0_ffn_setup()
    _L0_ffn_in = {k: v for k, v in _L0_ffn_all.items() if k in ('W1', 'b1', 'W2', 'b2', 'Wo', 'bo', 'gamma', 'beta')}
    del _L0_ffn_all

    def _L1_attn_setup():
        import jax, jax.numpy as jnp
        import numpy as np
        D_MODEL = 192
        NHEAD = 12
        HEAD_DIM = D_MODEL // NHEAD
        MAX_REL = 16
        B, T = (4, 256)
        key = jax.random.key(seed)
        ks = jax.random.split(key, 6)
        s = 0.02
        return {'x': jax.random.normal(ks[0], (B, T, D_MODEL), dtype=jnp.float32), 'qkv_w': jax.random.normal(ks[1], (3 * D_MODEL, D_MODEL), dtype=jnp.float32) * s, 'qkv_b': jax.random.normal(ks[2], (3 * D_MODEL,), dtype=jnp.float32) * s, 'out_w': jax.random.normal(ks[3], (D_MODEL, D_MODEL), dtype=jnp.float32) * s, 'out_b': jax.random.normal(ks[4], (D_MODEL,), dtype=jnp.float32) * s, 'rel_pos_emb': jax.random.normal(ks[5], (2 * MAX_REL + 1, HEAD_DIM), dtype=jnp.float32)}
    _L1_attn_all = _L1_attn_setup()
    _L1_attn_in = {k: v for k, v in _L1_attn_all.items() if k in ('qkv_w', 'qkv_b', 'out_w', 'out_b', 'rel_pos_emb')}
    del _L1_attn_all

    def _L1_ffn_setup():
        import jax, jax.numpy as jnp
        import numpy as np
        E = 8
        TOP_K = 2
        CAP_RATIO = 1.2
        key = jax.random.key(seed)
        k1, k2, k3, k4 = jax.random.split(key, 4)
        B, L, D, H = (2, 512, 192, 512)
        x = jax.random.normal(k1, (B, L, D), dtype=jnp.float32)
        Wg = jax.random.normal(k2, (D, E), dtype=jnp.float32) * 0.02
        W1 = jax.random.normal(k3, (E, D, 2 * H), dtype=jnp.float32) * 0.02
        W2 = jax.random.normal(k4, (E, H, D), dtype=jnp.float32) * 0.02
        return {'x': x, 'Wg': Wg, 'W1': W1, 'W2': W2}
    _L1_ffn_all = _L1_ffn_setup()
    _L1_ffn_in = {k: v for k, v in _L1_ffn_all.items() if k in ('Wg', 'W1', 'W2')}
    del _L1_ffn_all
    return {'x': x, 'x_txt': x_txt, 'L0_tok_curve': _L0_tok_in['curve'], 'L0_tok_proj_w': _L0_tok_in['proj_w'], 'L0_tok_proj_b': _L0_tok_in['proj_b'], 'L0_txt_weights': _L0_txt_in['weights'], 'L0_txt_emb_weight': _L0_txt_in['emb_weight'], 'L0_attn_Wq': _L0_attn_in['Wq'], 'L0_attn_bq': _L0_attn_in['bq'], 'L0_attn_Wk': _L0_attn_in['Wk'], 'L0_attn_bk': _L0_attn_in['bk'], 'L0_attn_Wv': _L0_attn_in['Wv'], 'L0_attn_bv': _L0_attn_in['bv'], 'L0_attn_Wc': _L0_attn_in['Wc'], 'L0_attn_bc': _L0_attn_in['bc'], 'L0_attn_Wo': _L0_attn_in['Wo'], 'L0_attn_bo': _L0_attn_in['bo'], 'L0_attn_g1': _L0_attn_in['g1'], 'L0_attn_b1': _L0_attn_in['b1'], 'L0_attn_Wi': _L0_attn_in['Wi'], 'L0_attn_bi': _L0_attn_in['bi'], 'L0_attn_Wo2': _L0_attn_in['Wo2'], 'L0_attn_bo2': _L0_attn_in['bo2'], 'L0_attn_g2': _L0_attn_in['g2'], 'L0_attn_b2': _L0_attn_in['b2'], 'L0_ffn_W1': _L0_ffn_in['W1'], 'L0_ffn_b1': _L0_ffn_in['b1'], 'L0_ffn_W2': _L0_ffn_in['W2'], 'L0_ffn_b2': _L0_ffn_in['b2'], 'L0_ffn_Wo': _L0_ffn_in['Wo'], 'L0_ffn_bo': _L0_ffn_in['bo'], 'L0_ffn_gamma': _L0_ffn_in['gamma'], 'L0_ffn_beta': _L0_ffn_in['beta'], 'L1_attn_qkv_w': _L1_attn_in['qkv_w'], 'L1_attn_qkv_b': _L1_attn_in['qkv_b'], 'L1_attn_out_w': _L1_attn_in['out_w'], 'L1_attn_out_b': _L1_attn_in['out_b'], 'L1_attn_rel_pos_emb': _L1_attn_in['rel_pos_emb'], 'L1_ffn_Wg': _L1_ffn_in['Wg'], 'L1_ffn_W1': _L1_ffn_in['W1'], 'L1_ffn_W2': _L1_ffn_in['W2']}

def reference(x, x_txt, L0_tok_curve, L0_tok_proj_w, L0_tok_proj_b, L0_txt_weights, L0_txt_emb_weight, L0_attn_Wq, L0_attn_bq, L0_attn_Wk, L0_attn_bk, L0_attn_Wv, L0_attn_bv, L0_attn_Wc, L0_attn_bc, L0_attn_Wo, L0_attn_bo, L0_attn_g1, L0_attn_b1, L0_attn_Wi, L0_attn_bi, L0_attn_Wo2, L0_attn_bo2, L0_attn_g2, L0_attn_b2, L0_ffn_W1, L0_ffn_b1, L0_ffn_W2, L0_ffn_b2, L0_ffn_Wo, L0_ffn_bo, L0_ffn_gamma, L0_ffn_beta, L1_attn_qkv_w, L1_attn_qkv_b, L1_attn_out_w, L1_attn_out_b, L1_attn_rel_pos_emb, L1_ffn_Wg, L1_ffn_W1, L1_ffn_W2):
    import jax
    import jax.numpy as jnp

    def _L0_tok_ref(x, curve, proj_w, proj_b):
        import jax, jax.numpy as jnp
        import numpy as np
        B, C, H, W_IMG = (128, 3, 224, 224)
        N_PATCH, EMBED = (256, 192)
        GRID = 32
        gathered = x[:, :, curve[:, 1], curve[:, 0]]
        return jnp.einsum('bcn,ec->bne', gathered, proj_w) + proj_b

    def _L0_txt_ref(x, weights, emb_weight):
        import jax, jax.numpy as jnp
        import numpy as np
        EMBED_DIM_LIST = (192, 96, 144, 192)
        MAX_EMBED_DIM = 192
        VOCAB = 50257
        BATCH, SEQ = (8, 512)
        dims = jnp.asarray(EMBED_DIM_LIST)
        col = jnp.arange(MAX_EMBED_DIM)
        mask = (col[None, :] < dims[:, None]).astype(weights.dtype)
        col_scale = weights @ mask
        embedding_mixture = emb_weight * col_scale[None, :]
        out = embedding_mixture[x]
        return out

    def _L0_attn_ref(hidden_states, Wq, bq, Wk, bk, Wv, bv, Wc, bc, Wo, bo, g1, b1, Wi, bi, Wo2, bo2, g2, b2):
        import jax, jax.numpy as jnp
        import numpy as np
        H = 12
        BETA = 0.5
        LN_EPS = 1e-12

        def layer_norm(x, g, b):
            mu = x.mean(-1, keepdims=True)
            var = ((x - mu) ** 2).mean(-1, keepdims=True)
            return (x - mu) * jax.lax.rsqrt(var + LN_EPS) * g + b
        B, S, D = hidden_states.shape
        Dh = D // H
        L = Wq.shape[0]
        eye = jnp.eye(S, dtype=hidden_states.dtype)
        scale = 1.0 / np.sqrt(Dh).astype(np.float32)

        def heads(t):
            return t.reshape(B, S, H, Dh).transpose(0, 2, 1, 3)
        x = hidden_states
        for i in range(L):
            q = heads(x @ Wq[i] + bq[i])
            k = heads(x @ Wk[i] + bk[i])
            v = heads(x @ Wv[i] + bv[i])
            c = heads(x @ Wc[i] + bc[i])
            cn = jnp.linalg.norm(c, axis=-1, keepdims=True)
            denom = cn * jnp.swapaxes(cn, -1, -2)
            s1 = 1.0 - jnp.einsum('bhld,bhrd->bhlr', c, c) / denom + eye
            p1 = jax.nn.softmax(s1, axis=-1)
            s2 = jnp.einsum('bhld,bhrd->bhlr', q, k) * scale
            p2 = jax.nn.softmax(s2, axis=-1)
            p = BETA * p1 + (1.0 - BETA) * p2
            ctx = jnp.einsum('bhlr,bhrd->bhld', p, v)
            ctx = ctx.transpose(0, 2, 1, 3).reshape(B, S, D)
            attn_out = layer_norm(ctx @ Wo[i] + bo[i] + x, g1[i], b1[i])
            h = jax.nn.gelu(attn_out @ Wi[i] + bi[i], approximate=False)
            x = layer_norm(h @ Wo2[i] + bo2[i] + attn_out, g2[i], b2[i])
        return x

    def _L0_ffn_ref(x, W1, b1, W2, b2, Wo, bo, gamma, beta):
        import jax, jax.numpy as jnp
        import numpy as np
        HIDDEN = 192
        INNER = 128
        EPS = 1e-05
        h = jax.nn.relu(jnp.einsum('bsd,id->bsi', x, W1) + b1)
        pred = jnp.einsum('bsi,di->bsd', h, W2) + b2
        out = jnp.einsum('bsd,ed->bse', pred, Wo) + bo
        mu = jnp.mean(out, axis=-1, keepdims=True)
        var = jnp.mean(jnp.square(out - mu), axis=-1, keepdims=True)
        out = (out - mu) * jax.lax.rsqrt(var + EPS) * gamma + beta
        return out

    def _L1_attn_ref(x, qkv_w, qkv_b, out_w, out_b, rel_pos_emb):
        import jax, jax.numpy as jnp
        import numpy as np
        D_MODEL = 192
        NHEAD = 12
        HEAD_DIM = D_MODEL // NHEAD
        MAX_REL = 16
        B, T = (4, 256)
        Bx, Tx, _ = x.shape
        scale = HEAD_DIM ** (-0.5)
        qkv = x @ qkv_w.T + qkv_b
        qkv = qkv.reshape(Bx, Tx, 3, NHEAD, HEAD_DIM)
        q = qkv[:, :, 0].transpose(0, 2, 1, 3)
        k = qkv[:, :, 1].transpose(0, 2, 1, 3)
        v = qkv[:, :, 2].transpose(0, 2, 1, 3)
        attn_scores = jnp.einsum('bhtd,bhsd->bhts', q, k)
        rng = jnp.arange(Tx)
        rel_pos = jnp.clip(rng[None, :] - rng[:, None], -MAX_REL, MAX_REL) + MAX_REL
        rel_emb = rel_pos_emb[rel_pos]
        rel_scores = jnp.einsum('bhtd,tsd->bhts', q, rel_emb)
        attn = jax.nn.softmax((attn_scores + rel_scores) * scale, axis=-1)
        out = jnp.einsum('bhts,bhsd->bhtd', attn, v)
        out = out.transpose(0, 2, 1, 3).reshape(Bx, Tx, D_MODEL)
        return out @ out_w.T + out_b

    def _L1_ffn_ref(x, Wg, W1, W2):
        import jax, jax.numpy as jnp
        import numpy as np
        E = 8
        TOP_K = 2
        CAP_RATIO = 1.2
        B, L, D = x.shape
        H = W2.shape[1]
        xf = x.reshape(-1, D)
        N = xf.shape[0]
        capacity = int(CAP_RATIO * N / E)
        logits = xf @ Wg
        scores, idx = jax.lax.top_k(logits, TOP_K)
        weights = jax.nn.softmax(scores, axis=-1)
        xpad = jnp.concatenate([xf, jnp.zeros((1, D), xf.dtype)], axis=0)
        wpad_zero = jnp.zeros((1,), weights.dtype)
        out = jnp.zeros((N, D), x.dtype)
        for k in range(TOP_K):
            ik = idx[:, k]
            onehot = ik[:, None] == jnp.arange(E)[None, :]
            pos = jnp.cumsum(onehot, axis=0) - 1
            posk = jnp.take_along_axis(pos, ik[:, None], axis=1)[:, 0]
            keep = posk < capacity
            buf = jnp.full((E, capacity), N, dtype=jnp.int32)
            buf = buf.at[ik, posk].set(jnp.arange(N, dtype=jnp.int32), mode='drop')
            xg = xpad[buf]
            h = jnp.einsum('ecd,edh->ech', xg, W1)
            act = h[..., :H] * jax.nn.silu(h[..., H:])
            ye = jnp.einsum('ech,ehd->ecd', act, W2)
            wk = jnp.where(keep, weights[:, k], 0.0)
            w_buf = jnp.concatenate([wk, wpad_zero])[buf]
            out = out.at[buf.reshape(-1)].add((w_buf[..., None] * ye).reshape(E * capacity, D), mode='drop')
        return out.reshape(B, L, D)
    h = _L0_tok_ref(x, L0_tok_curve, L0_tok_proj_w, L0_tok_proj_b)
    h = jnp.concatenate([h, _L0_txt_ref(x_txt, L0_txt_weights, L0_txt_emb_weight)], axis=1)
    h = h + _L0_attn_ref(_layernorm(h, axis=-1), L0_attn_Wq, L0_attn_bq, L0_attn_Wk, L0_attn_bk, L0_attn_Wv, L0_attn_bv, L0_attn_Wc, L0_attn_bc, L0_attn_Wo, L0_attn_bo, L0_attn_g1, L0_attn_b1, L0_attn_Wi, L0_attn_bi, L0_attn_Wo2, L0_attn_bo2, L0_attn_g2, L0_attn_b2)
    h = h + _L0_ffn_ref(_layernorm(h, axis=-1), L0_ffn_W1, L0_ffn_b1, L0_ffn_W2, L0_ffn_b2, L0_ffn_Wo, L0_ffn_bo, L0_ffn_gamma, L0_ffn_beta)
    h = h + _L1_attn_ref(_layernorm(h, axis=-1), L1_attn_qkv_w, L1_attn_qkv_b, L1_attn_out_w, L1_attn_out_b, L1_attn_rel_pos_emb)
    h = h + _L1_ffn_ref(_layernorm(h, axis=-1), L1_ffn_Wg, L1_ffn_W1, L1_ffn_W2)
    return h

_drawn_inputs = setup_inputs


def setup_inputs(seed=0):
    import zlib

    import numpy as np

    out = dict(_drawn_inputs(seed))
    spreads = {'L0_attn_bq': (0.0, 0.8),
     'L0_attn_bk': (0.0, 0.8),
     'L0_attn_bv': (0.0, 0.1),
     'L0_attn_bc': (0.0, 0.8),
     'L0_attn_bo': (0.0, 0.1),
     'L0_attn_g1': (1.0, 0.2),
     'L0_attn_b1': (0.0, 0.1),
     'L0_attn_bi': (0.0, 0.1),
     'L0_attn_bo2': (0.0, 0.1),
     'L0_attn_g2': (1.0, 0.2),
     'L0_attn_b2': (0.0, 0.1),
     'L0_ffn_b1': (0.0, 0.1),
     'L0_ffn_b2': (0.0, 0.1),
     'L0_ffn_gamma': (1.0, 0.2),
     'L0_ffn_beta': (0.0, 0.1)}
    factors = {'L0_attn_Wq': 8.0,
     'L0_attn_Wk': 8.0,
     'L0_attn_Wc': 8.0,
     'L1_attn_qkv_b': 8.0,
     'L1_attn_out_b': 4.384,
     'L1_attn_rel_pos_emb': 8.0,
     'L1_ffn_Wg': 8.0,
     'L1_ffn_W1': 8.0,
     'L1_ffn_W2': 8.0}
    for name, (base, spread) in spreads.items():
        noise = np.random.default_rng([zlib.crc32(name.encode()), seed]).standard_normal(out[name].shape)
        drawn = base * np.exp(spread * noise) if base else spread * noise
        out[name] = jnp.asarray(drawn.astype(out[name].dtype))
    for name, factor in factors.items():
        out[name] = (out[name] * factor).astype(out[name].dtype)
    return out
```

```python
import concourse.bass as bass
from concourse import mybir
from concourse.alu_op_type import AluOpType as ALU
from contextlib import ExitStack

F32 = mybir.dt.float32
BF16 = mybir.dt.bfloat16
I32 = mybir.dt.int32
U32 = mybir.dt.uint32
ACT = mybir.ActivationFunctionType
AX = mybir.AxisListType

P = 128
B, NPATCH, NTXT = 4, 256, 512
S = NPATCH + NTXT
NT = S // P
D, H, DH = 192, 12, 16
L = 4
FC = D // 2
HALF = S // 2
FF = 768
NM = FF // P
BANK = 512
G = 4
NG = H // G
PLANE = 224 * 224
VOCAB = 50257
MAXREL = 16
NREL = 2 * MAXREL + 1
WIN = 192
XL = WIN + P - 1
FILL = (XL - NREL) // 2
E_, TOPK, HID = 8, 2, 512
N = B * S
CAP = int(1.2 * N / E_)
CP, CC = 115, 4
NBLK = TOPK * E_
SLOTS = NBLK * CAP

KEY_PARTS = (0, 0, 0, 1, 1, 2)
QRY_PARTS = (0, 1, 2, 0, 1, 0)
CORE = len(KEY_PARTS) * DH
MROWS = 3
RROWS = 3 * NT


LSTEP, TSTEP = 76, 120


class Counts:

    def __init__(self, nc, ctx, prefix, per):
        self.per, self.prefix = per, prefix
        self.sem = {k: ctx.enter_context(nc.semaphore(prefix + k)) for k in per}

    def on(self, eng, passes):
        return View(self, eng, passes)


class View:

    def __init__(self, counts, eng, passes):
        self.c, self.eng, self.passes, self.links = counts, eng, passes, {}

    def wait(self, name, k):
        if isinstance(self.passes, int) and self.passes * self.c.per[name] + k <= 0:
            return
        self.eng.wait_ge(self.c.sem[name], self.passes * self.c.per[name] + k)

    def inc(self, ins, name, by=1):
        ins.then_inc(self.c.sem[name], by)

    def link(self, ins, name="dve_step"):
        self.links[name] = self.links.get(name, 0) + 1
        ins.then_inc(self.c.sem[name], 1)
        self.wait(name, self.links[name])

    def close(self, name="dve_step"):
        assert self.links.get(name, 0) == self.c.per[name], (self.c.prefix, self.links.get(name, 0))


def attention_order(has_max):
    job = 0
    ended = None
    blocks = NG * NT
    for n in range(blocks + 1):
        for j in range(G):
            if n < blocks:
                yield "unit", n, j
                if has_max:
                    for _ in range(2):
                        yield "max", job, 0
                        job += 1
            if n and j % 2:
                yield "av", n - 1, j // 2
        if ended is not None:
            yield "norm", ended, 0
            yield "norm", ended, 1
            ended = None
        if n and (n - 1) % NT == NT - 1:
            ended = (n - 1) // NT
            yield "evac", ended, 0
    yield "norm", ended, 0
    yield "norm", ended, 1


def embed(nc, a, H0, XG):
    with ExitStack() as ctx:
        sb = lambda n, s, d: ctx.enter_context(nc.sbuf_tensor(n, s, d))
        sem = lambda n: ctx.enter_context(nc.semaphore(n))
        ids = sb("ids", [P, B * 4], I32)
        cur = sb("cur", [P, 2, 2], I32)
        curf = sb("curf", [P, 2, 2], F32)
        pixf = sb("pixf", [P, 2], F32)
        pix = sb("pix", [P, 2], I32)
        pw = sb("pw", [P, 4, D], F32)
        wt = sb("wt", [P, 4], F32)
        mask = sb("mask", [P, 4, D], F32)
        cs = sb("cs", [P, D], F32)
        gim = sb("gim", [P, 2, 3 * B], F32)
        hs = sb("hs", [P, B, NT, D], F32)
        zero = sb("zero", [CP, 8 * D], F32)
        loaded, pix_ready = sem("emb_loaded"), sem("pix_ready")
        img_in, txt_in, step = sem("img_in"), sem("txt_in"), sem("emb_step")
        h_ready, stored, zeroed, zset = sem("h_ready"), sem("h_stored"), sem("xg_zeroed"), sem("zero_set")
        nload = 6

        with nc.Block() as block:
            @block.sync
            def _(sp):
                sp.dma_start(ids[:], a["ids"]).then_inc(loaded, 16)
                sp.dma_start(cur[:], a["curve"]).then_inc(loaded, 16)
                sp.dma_start(pw[:, 0:3], a["tok_w"].partition_broadcast(P)).then_inc(loaded, 16)
                sp.dma_start(pw[:, 3], a["tok_b"].partition_broadcast(P)).then_inc(loaded, 16)
                sp.dma_start(wt[:], a["txt_w"].partition_broadcast(P)).then_inc(loaded, 16)
                sp.dma_start(mask[:], a["colmask"].partition_broadcast(P)).then_inc(loaded, 16)
                sp.wait_ge(zset, 1)
                for i in range(8):
                    sp.dma_start(XG[i * SLOTS // 8:(i + 1) * SLOTS // 8, :].rearrange("(p c) d -> p (c d)", p=CP),
                                 zero[:]).then_inc(zeroed, 16)
                sp.wait_ge(h_ready, 1)
                sp.dma_start(H0[0:B].rearrange("b p t d -> p b t d"), hs[:]).then_inc(stored, 16)
                sp.dma_start(H0[B], hs[:, 0]).then_inc(stored, 16)
                sp.wait_ge(stored, 32)
                sp.wait_ge(zeroed, 8 * 16)

            @block.gpsimd
            def _(pool):
                pool.wait_ge(loaded, 16 * nload)
                for b in range(B):
                    for t in range(4):
                        pool.indirect_dma_start(
                            out=hs[:, b, 2 + t, :], out_offset=None, in_=a["emb"],
                            in_offset=bass.IndirectOffsetOnAxis(ap=ids[:, b * 4 + t:b * 4 + t + 1], axis=0)
                        ).then_inc(txt_in, 16)
                pool.wait_ge(pix_ready, 1)
                for t in range(2):
                    for c in range(3 * B):
                        pool.indirect_dma_start(
                            out=gim[:, t, c:c + 1], out_offset=None, in_=a["img"],
                            in_offset=bass.IndirectOffsetOnAxis(ap=pix[:, t:t + 1], axis=0),
                            element_offset=c * PLANE).then_inc(img_in, 16)

            @block.vector
            def _(dve):
                links = [0]

                def link(ins):
                    links[0] += 1
                    ins.then_inc(step, 1)
                    dve.wait_ge(step, links[0])

                dve.memset(zero[:], 0.0).then_inc(zset, 1)
                dve.wait_ge(loaded, 16 * nload)
                link(dve.tensor_copy(curf[:], cur[:]))
                link(dve.scalar_tensor_tensor(out=pixf[:], in0=curf[:, :, 1], scalar=224.0, in1=curf[:, :, 0],
                                              op0=ALU.mult, op1=ALU.add))
                dve.tensor_copy(pix[:], pixf[:]).then_inc(pix_ready, 1)
                link(dve.tensor_scalar(cs[:], mask[:, 0], wt[:, 0:1], None, ALU.mult))
                for i in range(1, 4):
                    link(dve.scalar_tensor_tensor(out=cs[:], in0=mask[:, i], scalar=wt[:, i:i + 1], in1=cs[:],
                                                  op0=ALU.mult, op1=ALU.add))
                dve.wait_ge(txt_in, 16 * 16)
                link(dve.tensor_tensor(hs[:, :, 2:NT, :], hs[:, :, 2:NT, :],
                                       cs[:].unsqueeze(1).unsqueeze(1).broadcast_to([P, B, 4, D]), ALU.mult))
                dve.wait_ge(img_in, 16 * 2 * 3 * B)
                last = None
                for c in range(3):
                    for b in range(B):
                        for t in range(2):
                            prev = pw[:, 3] if c == 0 else hs[:, b, t]
                            last = dve.scalar_tensor_tensor(out=hs[:, b, t], in0=pw[:, c],
                                                            scalar=gim[:, t, 3 * b + c:3 * b + c + 1], in1=prev,
                                                            op0=ALU.mult, op1=ALU.add)
                    if c < 2:
                        link(last)
                last.then_inc(h_ready, 1)


def layers(nc, a, H0, H1, XF, LG, PD, MD, RD, XD):
    with ExitStack() as ctx:
        sb = lambda n, s, d: ctx.enter_context(nc.sbuf_tensor(n, s, d))
        sem = lambda n: ctx.enter_context(nc.semaphore(n))

        X = sb("X", [P, NT, D], F32)
        HR = sb("HR", [P, NT, D], F32)
        A1 = sb("A1", [P, NT, D], F32)
        XT = sb("XT", [FC, 2, S], F32)
        PARTS = sb("PARTS", [P, 3 * 3 * 2 * S], BF16)
        parts = PARTS[0:FC, :].rearrange("p (o k c t) -> p o k c t", o=3, k=3, c=2)
        pf = PARTS[:].bitcast(F32)
        OS = pf[:, 0:S]
        T2, CTX = (pf[:, S + i * NT * D:S + (i + 1) * NT * D].rearrange("p (t d) -> p t d", t=NT)
                   for i in range(2))
        AQ = sb("AQ", [P, H, S], BF16)
        AK = sb("AK", [P, H, S], BF16)
        CL = sb("CL", [P, H, S], BF16)
        CR = sb("CR", [P, H, S], BF16)
        XS = AQ[:].rearrange("p h s -> p (h s)").bitcast(F32)[:, 0:H * XL].rearrange("p (h x) -> p h x", h=H)
        DWH = [w[:].rearrange("p h s -> p (h s)").bitcast(F32).rearrange("p (r t x) -> p r t x", r=4, t=NT)
               for w in (AQ, AK)]
        window = lambda i: DWH[(i % 8) // 4][:, i % 4]
        HT = AQ[:].rearrange("p h s -> p (h s)").bitcast(F32).rearrange("p (m s) -> p m s", m=NM)
        VP = sb("VP", [P, NT, H, 2 * DH], F32)
        E = sb("E", [P, 8, S], F32)
        Fc, Fk, Fq, SQ = (E[0:FC, 2 * i:2 * i + 2, :] for i in range(4))
        REM = sb("REM", [FC, 2, S], F32)
        MX = sb("MX", [P, 2, H * NT], F32)
        NMX = sb("NMX", [P, H * NT], F32)
        NMR = sb("NMR", [P, H * NT], F32)
        NMP = sb("NMP", [P, 3, H * NT], BF16)
        MT = sb("MT", [H * NT, 3, P], BF16)
        RZ = sb("RZ", [P, 3, G], F32)
        TP = sb("TP", [P, 3, G, DH], F32)
        ST = sb("ST", [P, NT, 6], F32)
        MV = sb("MV", [P, NT, 2], F32)
        SD = sb("SD", [P, NT], F32)
        Wqkcv = sb("Wqkcv", [FC, 2, 4 * D], F32)
        Wo = sb("Wo", [FC, 2, D], F32)
        Wi = sb("Wi", [FC, 2, FF], F32)
        Wo2 = sb("Wo2", [P, NM, D], F32)
        bcol = sb("bcol", [FC, 3, 2], F32)
        bicol = sb("bicol", [P, NM], F32)
        MT1 = REM[0:H * NT].rearrange("p c t -> p (c t)").bitcast(BF16)[:, 0:3 * S].rearrange(
            "p (k t) -> p k t", k=3)
        brow = sb("brow", [P, 7, D], F32)
        W1T = sb("W1T", [FC, 2, P], F32)
        W2T = sb("W2T", [P, D], F32)
        WoT = sb("WoT", [FC, 2, D], F32)
        WqkvT = sb("WqkvT", [FC, 2, 3 * D], F32)
        WoutT = sb("WoutT", [FC, 2, D], F32)
        Wg = sb("Wg", [FC, 2, E_], F32)
        EMB = sb("EMB", [FC, 6 * NREL], F32)
        fcol = sb("fcol", [P, 1], F32)
        f2col = sb("f2col", [FC, 2], F32)
        qkcol = sb("qkcol", [FC, 2, 2], F32)
        frow = sb("frow", [P, 5, D], F32)
        LGT = sb("LGT", [P, NT, E_], F32)
        RB = sb("RB", [P, NT, H, 2], F32)
        BS = sb("BS", [P, NT, H, NT], F32)
        MX6 = sb("MX6", [P, NT, H, NT], F32)
        VVP = sb("VVP", [P, 3, NT, H * NT], BF16)
        M1 = sb("M1", [P, NT, H], F32)
        idf = sb("idf", [P, P], F32)
        idb = sb("idb", [P, P], BF16)
        negI = sb("negI", [P, P], BF16)
        blk = sb("blk", [FC, FC], F32)

        PS = ctx.enter_context(nc.psum_tensor("PS", [P, 8, BANK], F32))
        flat = lambda b0, n: PS[:, b0, 0:n]

        w_once, w_first, w_rest = sem("w_once"), sem("w_first"), sem("w_rest")
        const_ready, h_in, h_out = sem("const_ready"), sem("h_in"), sem("h_out")
        onehot_in = sem("onehot_in")
        const_in = sem("const_in")
        x_ready = sem("x_ready")
        XPER = 3 * (1 + L)
        NW_FIRST, NW_REST = 3, 5
        onehot_ready = sem("onehot_ready")
        OHF = E[0:RROWS, 0, :]
        OHB = PARTS[0:RROWS, 0:S]
        once = [(idf[:], a["ident"]), (blk[:], a["headblk"]), (W1T[:], a["W1T"]), (W2T[:], a["W2T"]),
                (WoT[:], a["WoT"]), (WqkvT[:], a["WqkvT"]), (WoutT[:], a["WoutT"]), (Wg[:], a["Wg"]),
                (EMB[:], a["relbd"]), (fcol[:], a["fcol"]), (f2col[:], a["f2col"]), (qkcol[:], a["qkcol"]),
                (frow[:], a["frow"].partition_broadcast(P)), (OHF, a["onehot"])]
        NW_ONCE = len(once)
        NSPREAD = 4 * len(KEY_PARTS)
        lay = Counts(nc, ctx, "l_", dict(
            tr_ps=6, tr_dve=3, tr_act=3, v_ps=3, v_dve=3, f_ps=6, f_act=6, sq_act=2, n_ps=2, n_act=4,
            p_dve=3, pd_w=48, **{f"aug{g}": 16 * NSPREAD for g in range(NG)}, sc_ps=144, e_act=144, av_ps=36, osb=6,
            m_ps=157, m_free=157, mt_dve=1, md_w=16, md_r=16, ctx_ready=1, y_ps=3, a1_ready=3,
            ln_var=6, ln_sd=6, f1_ps=12, g_act=12, y2_ps=3, dve_step=LSTEP))
        tail = Counts(nc, ctx, "t_", dict(
            a_ready=9, tr_ps=8, tr_dve=4, tr_act=4, ln_var=15, ln_sd=15, f0_ps=1, relu=1, pr_ps=2, pr_act=2,
            yo_ps=3, v_ps=3, v_dve=3, f_ps=4, f_act=4, p_dve=2, pd_w=32, aug_k=96, aug_q=96,
            rr_ps=6, rr_dve=6, xs=6, xs_w=96, dw_fix=24, sc_ps=72, e_act=72, av_ps=18,
            osb=3, m_ps=144 + 3 + 6, m_free=144 + 3 + 6, mt_dve=3, md_w=16, md_r=48, yo2_ps=3,
            lg_ps=1, out_ready=1, dve_step=TSTEP, **{f"dw_in{r}": 3 * 16 * NT for r in range(8)}))

        def transposes(v, src, pair_ready=None):
            for pair in range(3):
                if pair_ready is not None:
                    pair_ready(pair)
                for c in range(2):
                    for t in range(2 * pair, 2 * pair + 2):
                        last = v.eng.transpose(PS[0:FC, 2 * c + t // 4, (t % 4) * P:(t % 4) * P + P],
                                               src[:, t, c * FC:(c + 1) * FC], idf[:])
                    if pair == 2:
                        v.inc(last, "tr_ps")

        def tr_view(c):
            return PS[0:FC, 2 * c:2 * c + 2, :].rearrange("p a b -> p (a b)")[:, 0:S]

        def take_transposed(v, use, c, act):
            v.wait("tr_ps", 2 * use + c + 1)
            if act:
                v.inc(v.eng.activation(XT[:, c, :], tr_view(c), ACT.Copy), "tr_act")
            else:
                v.inc(v.eng.tensor_copy(XT[:, c, :], tr_view(c)), "tr_dve")

        def token_product(v, bank, weights, ncols, sig):
            for t in range(NT):
                for c in range(2):
                    last = v.eng.matmul(PS[:, bank + t // 2, (t % 2) * 256:(t % 2) * 256 + ncols],
                                        XT[:, c, t * P:(t + 1) * P], weights[:, c, :],
                                        start=(c == 0), stop=(c == 1))
                if t % 2:
                    v.inc(last, sig)

        def feature_product(v, bank, weights, sig):
            for m in range(2):
                for h in range(2):
                    for c in range(2):
                        last = v.eng.matmul(PS[0:FC, bank + 2 * m + h, 0:HALF],
                                            weights[:, c, m * FC:(m + 1) * FC],
                                            XT[:, c, h * HALF:(h + 1) * HALF], start=(c == 0), stop=(c == 1))
                v.inc(last, sig)

        def chunk_view(bank, m):
            return PS[0:FC, bank + 2 * m:bank + 2 * m + 2, 0:HALF]

        def halves(ap):
            return ap.rearrange("p (h t) -> p h t", h=2)

        def token_view(bank, pair):
            return PS[:, bank + pair, :].rearrange("p (t x) -> p t x", t=2)[:, :, 0:D]

        def row_bc(row, n):
            return row.unsqueeze(1).broadcast_to([P, n, D])

        def layer_norm(v, source, src, dst, eps, n, done, gain=None, shift=None):
            dve = v.eng
            for pair in range(4):
                if pair < 3:
                    ts = slice(2 * pair, 2 * pair + 2)
                    if source is not None:
                        v.link(source(pair))
                    for t in range(2 * pair, 2 * pair + 2):
                        ins = dve.bn_stats(ST[:, t, :], src[:, t, :])
                    v.link(ins)
                    dve.tensor_tensor(MV[:, ts, 0], ST[:, ts, 1], ST[:, ts, 4], ALU.add)
                    dve.tensor_tensor(MV[:, ts, 1], ST[:, ts, 1], ST[:, ts, 4], ALU.subtract)
                    v.link(dve.tensor_tensor(SD[:, ts], ST[:, ts, 2], ST[:, ts, 5], ALU.add))
                    dve.tensor_scalar(MV[:, ts, 0], MV[:, ts, 0], 0.5, None, ALU.mult)
                    v.link(dve.tensor_tensor(MV[:, ts, 1], MV[:, ts, 1], MV[:, ts, 1], ALU.mult))
                    v.link(dve.scalar_tensor_tensor(out=SD[:, ts], in0=MV[:, ts, 1], scalar=D / 4.0, in1=SD[:, ts],
                                                    op0=ALU.mult, op1=ALU.add))
                    v.inc(dve.tensor_scalar(SD[:, ts], SD[:, ts], 1.0 / D, eps, ALU.mult, ALU.add), "ln_var")
                if pair:
                    ts = slice(2 * pair - 2, 2 * pair)
                    v.wait("ln_sd", 3 * (n - 1) + pair)
                    v.link(dve.reciprocal(SD[:, ts], SD[:, ts]))
                    for t in range(2 * pair - 2, 2 * pair):
                        if gain is None:
                            ins = dve.tensor_scalar(dst[:, t, :], src[:, t, :], MV[:, t, 0:1], SD[:, t:t + 1],
                                                    ALU.subtract, ALU.mult)
                        else:
                            ins = dve.scalar_tensor_tensor(out=dst[:, t, :], in0=src[:, t, :], scalar=MV[:, t, 0:1],
                                                           in1=gain, op0=ALU.subtract, op1=ALU.mult)
                    if gain is not None:
                        v.link(ins)
                        for t in range(2 * pair - 2, 2 * pair):
                            ins = dve.scalar_tensor_tensor(out=dst[:, t, :], in0=dst[:, t, :], scalar=SD[:, t:t + 1],
                                                           in1=shift, op0=ALU.mult, op1=ALU.add)
                    done(ins)

        def norm_sd(v, n):
            for pair in range(3):
                ts = slice(2 * pair, 2 * pair + 2)
                v.wait("ln_var", 3 * (n - 1) + pair + 1)
                v.inc(v.eng.activation(SD[:, ts], SD[:, ts], ACT.Sqrt), "ln_sd")

        def split(v, f, o, sig):
            v.link(v.eng.tensor_copy(parts[:, o, 0], f))
            v.link(v.eng.tensor_tensor(REM[:], f, parts[:, o, 0], ALU.subtract))
            v.link(v.eng.tensor_copy(parts[:, o, 1], REM[:]))
            v.inc(v.eng.tensor_tensor(parts[:, o, 2], REM[:], parts[:, o, 1], ALU.subtract), sig)

        def pe_scores(v, keys, queries, rows, n, j, unit, cosine, rel):
            g, kt = divmod(n, NT)
            h = g * G + j
            if unit >= 2:
                v.wait("e_act", unit - 1)
            slot = 2 * (unit % 2)
            if rel is not None and kt == 0:
                v.wait("dw_fix", rel + h + 1)
            for c0, nc_ in ((0, BANK), (BANK, S - BANK)):
                last = v.eng.matmul(PS[:, slot + c0 // BANK, 0:nc_], keys[0:rows, h, kt * P:(kt + 1) * P],
                                    queries[0:rows, h, c0:c0 + nc_], start=True, stop=True)
            if cosine:
                last = v.eng.matmul(PS[:, slot + kt // 4, (kt % 4) * P:(kt % 4) * P + P], negI[:], idb[:],
                                    start=False, stop=True, skip_group_check=True)
            if rel is not None:
                last = rel_window(v, window(rel + h), kt, slot)
            v.inc(last, "sc_ps")

        def rel_window(v, DW, kt, slot):
            for qt in (kt - 1, kt, kt + 1):
                if not 0 <= qt < NT:
                    continue
                col = PS[:, slot + qt // 4, (qt % 4) * P:(qt % 4) * P + P]
                if qt == kt:
                    ins = v.eng.matmul(col, DW[:, qt, 32:32 + P], idf[:], start=False, stop=True,
                                       skip_group_check=True)
                elif qt > kt:
                    ins = v.eng.matmul(col[96:128], DW[:, qt, 0:32], idf[:], start=False, stop=True,
                                       skip_group_check=True)
                else:
                    ins = v.eng.matmul(col[0:32], DW[:, qt, 160:192], idf[:], start=False, stop=True,
                                       skip_group_check=True)
            return ins

        def pe_av(v, n, half, block):
            g, kt = divmod(n, NT)
            if half == 0:
                v.wait("e_act", 4 * block + 4)
                if kt == 0 and block >= NT:
                    v.wait("osb", block // NT)
            for j in range(G):
                last = v.eng.matmul(PS[32 * j:32 * j + 32, 4 + half, 0:HALF], VP[:, kt, g * G + j, :],
                                    E[:, (4 * block + j) % 8, half * HALF:(half + 1) * HALF],
                                    start=(kt == 0), stop=(kt == NT - 1))
            if half:
                v.inc(last, "av_ps")

        def pe_norm(v, half, job, group):
            v.wait("osb", group + 1)
            v.wait("m_free", job - 1)
            for t in range(3):
                last = v.eng.transpose(PS[:, 6 + job % 2, t * P:(t + 1) * P],
                                       OS[:, (3 * half + t) * P:(3 * half + t + 1) * P], idf[:])
            v.inc(last, "m_ps")

        def act_exp(v, unit, scale, bias):
            v.wait("sc_ps", unit + 1)
            if unit >= 8:
                v.wait("av_ps", unit // 4 - 1)
            src = PS[:, 2 * (unit % 2):2 * (unit % 2) + 2, :].rearrange("p a b -> p (a b)")[:, 0:S]
            v.inc(v.eng.activation(E[:, unit % 8, :], src, ACT.Exp, bias=bias, scale=scale), "e_act")

        def dve_evac(v, group):
            v.wait("av_ps", NT * (group + 1))
            v.inc(v.eng.tensor_copy(halves(OS), PS[:, 4:6, 0:HALF]), "osb")

        def dve_norm(v, g, half, job, add, twice):
            v.wait("m_ps", job + 1)
            v.wait("m_free", job)
            o = PS[:, 6 + job % 2, 0:3 * P].rearrange("p (t h x) -> p t h x", t=3, h=G)
            v.link(v.eng.reciprocal(RZ[:], o[:, :, :, DH]))
            if twice:
                v.link(v.eng.tensor_scalar(RZ[:], RZ[:], 2.0, None, ALU.mult))
            dst = CTX[:, 3 * half:3 * half + 3, g * G * DH:(g + 1) * G * DH].rearrange("p t (h x) -> p t h x", h=G)
            rz = RZ[:].unsqueeze(3).broadcast_to([P, 3, G, DH])
            ins = v.eng.tensor_tensor(TP[:] if add else dst, o[:, :, :, 0:DH], rz, ALU.mult)
            v.inc(ins, "m_free")
            if add:
                v.wait("m_free", job + 1)
                ins = v.eng.tensor_tensor(dst, dst, TP[:], ALU.add)
                if g == NG - 1 and half == 1:
                    v.inc(ins, "ctx_ready")
                else:
                    v.link(ins)

        def phase(cosine, has_max, unit0, job0, rel=None):
            job = job0
            for kind, i, j in attention_order(has_max):
                if kind == "unit":
                    yield kind, i, j, unit0 + 4 * i + j
                elif kind in ("max", "norm"):
                    yield kind, i, j, job
                    job += 1
                else:
                    yield kind, i, j, 0

        def pe_phase(v, keys, queries, rows, cosine, has_max, unit0, job0, rel=None):
            for kind, i, j, k in phase(cosine, has_max, unit0, job0):
                if kind == "unit" and has_max and i % NT == 0 and j == 0:
                    v.wait(f"aug{i // NT}", 16 * NSPREAD)
                if kind == "unit":
                    pe_scores(v, keys, queries, rows, i, j, k, cosine, rel)
                elif kind == "max":
                    pe_max(v, AQ, AK, i, k, None)
                elif kind == "av":
                    pe_av(v, i, j, unit0 // 4 + i)
                elif kind == "norm":
                    pe_norm(v, j, k, unit0 // (4 * NT) + i)

        def pe_max(v, queries, keys, i, job, rel):
            h, qt, half = i // (2 * NT), i // 2 % NT, i % 2
            if job >= 2:
                v.wait("m_free", job - 1)
            out = PS[:, 6 + job % 2, 0:HALF]
            last = v.eng.matmul(out, queries[0:CORE, h, qt * P:(qt + 1) * P],
                                keys[0:CORE, h, half * HALF:(half + 1) * HALF], start=True, stop=True)
            if rel is not None:
                k0 = max(qt * P - 32, half * HALF)
                k1 = min(qt * P - 32 + WIN, (half + 1) * HALF)
                if k1 > k0:
                    x0 = k0 - (qt * P - 32)
                    last = v.eng.matmul(out[:, k0 - half * HALF:k1 - half * HALF], idf[:],
                                        rel[:, qt, x0:x0 + k1 - k0], start=False, stop=True,
                                        skip_group_check=True)
            v.inc(last, "m_ps")

        def dve_phase(v, has_max, unit0, job0, add, twice, after_evac=None):
            for kind, i, j, k in phase(False, has_max, unit0, job0):
                if kind == "max":
                    h, qt, half = i // (2 * NT), i // 2 % NT, i % 2
                    v.wait("m_ps", k + 1)
                    v.inc(v.eng.tensor_reduce(MX[:, half, h * NT + qt:h * NT + qt + 1], PS[:, 6 + k % 2, 0:HALF],
                                              AX.X, ALU.max), "m_free")
                elif kind == "evac":
                    dve_evac(v, unit0 // (4 * NT) + i)
                    if after_evac:
                        after_evac(i)
                elif kind == "norm":
                    dve_norm(v, i, j, k, add, twice)

        def dve_values(v, bias):
            for pair in range(3):
                v.wait("v_ps", pair + 1)
                o = VP[:, 2 * pair:2 * pair + 2, :, 0:DH]
                i0 = token_view(4, pair).rearrange("p t (h x) -> p t h x", h=H)
                i1 = row_bc(bias, 2).rearrange("p t (h x) -> p t h x", h=H)
                v.inc(v.eng.tensor_tensor(o, i0, i1, ALU.add), "v_dve")

        def product(v, sig, bank, other, dst):
            def source(pair):
                v.wait(sig, pair + 1)
                ts = slice(2 * pair, 2 * pair + 2)
                return v.eng.tensor_tensor(dst[:, ts, :], token_view(bank, pair), other(ts), ALU.add)
            return source

        def fix_window(v, i):
            h = i % H
            w = window(i)
            v.wait(f"dw_in{i % 8}", 16 * NT * (i // 8 + 1))
            dve = v.eng
            dve.tensor_tensor(w[:, 1:NT, 0:32], w[:, 1:NT, 0:32],
                              RB[:, 1:NT, h, 0:1].broadcast_to([P, NT - 1, 32]), ALU.subtract)
            v.inc(dve.tensor_tensor(w[:, 0:NT - 1, 160:192], w[:, 0:NT - 1, 160:192],
                                    RB[:, 0:NT - 1, h, 1:2].broadcast_to([P, NT - 1, 32]), ALU.subtract), "dw_fix")

        with nc.Block() as block:
            @block.tensor
            def _(pe):
                pe.wait_ge(const_ready, 1)
                pe.wait_ge(w_once, 16 * NW_ONCE)
                with pe.Fori(0, B) as b:
                    with pe.Fori(0, L) as l:
                        p = b * L + l
                        v = lay.on(pe, p)
                        transposes(v, X, lambda pair: pe.wait_ge(x_ready, b * XPER + l * 3 + pair + 1))
                        pe.wait_ge(w_first, p * (16 * NW_FIRST) + 16 * NW_FIRST)
                        v.wait("tr_dve", 1)
                        v.wait("tr_act", 1)
                        token_product(v, 4, Wqkcv[:, :, 3 * D:4 * D], D, "v_ps")
                        feature_product(v, 0, Wqkcv[:, :, 2 * D:3 * D], "f_ps")
                        v.wait("v_dve", 3)
                        feature_product(v, 4, Wqkcv[:, :, D:2 * D], "f_ps")
                        v.wait("f_act", 2)
                        feature_product(v, 0, Wqkcv[:, :, 0:D], "f_ps")
                        v.wait("f_act", 4)
                        for m in range(2):
                            v.wait("sq_act", m + 1)
                            for h in range(2):
                                last = pe.matmul(PS[0:FC, 4 + 2 * m + h, 0:HALF], blk[:],
                                                 halves(SQ[:, m, :])[:, h, :], start=True, stop=True)
                            v.inc(last, "n_ps")
                        pe_phase(v, CL, CR, CORE, True, True, 0, 0)
                        v.wait("mt_dve", 0 + 1)
                        v.wait("m_free", 150 - 1)
                        for k in range(3):
                            last = pe.transpose(PS[0:H * NT, 6, 0:192].bitcast(BF16)[:, k * P:(k + 1) * P],
                                                NMP[:, k, :], idb[:])
                        v.inc(last, "m_ps")
                        v.wait("md_r", 16)
                        pe_phase(v, AK, AQ, CORE + MROWS, False, False, 72, 151)
                        v.wait("ctx_ready", 1)
                        transposes(v, CTX)
                        pe.wait_ge(w_rest, p * (16 * NW_REST) + 16 * NW_REST)
                        v.wait("tr_dve", 2)
                        v.wait("tr_act", 2)
                        token_product(v, 4, Wo, D, "y_ps")
                        transposes(v, A1, lambda pair: v.wait("a1_ready", pair + 1))
                        v.wait("tr_dve", 3)
                        v.wait("tr_act", 3)
                        for f in range(2 * NM):
                            m, h = divmod(f, 2)
                            if f >= 4:
                                v.wait("g_act", f - 3)
                            for c in range(2):
                                last = pe.matmul(PS[:, 4 + f % 4, 0:HALF], Wi[:, c, m * P:(m + 1) * P],
                                                 XT[:, c, h * HALF:(h + 1) * HALF], start=(c == 0), stop=(c == 1))
                            v.inc(last, "f1_ps")
                        for t in range(NT):
                            v.wait("g_act", 2 * NM)
                            for m in range(NM):
                                last = pe.matmul(PS[:, 4 + t // 2, (t % 2) * 256:(t % 2) * 256 + D],
                                                 HT[:, m, t * P:(t + 1) * P], Wo2[:, m, :],
                                                 start=(m == 0), stop=(m == NM - 1))
                            if t % 2:
                                v.inc(last, "y2_ps")
                    v = tail.on(pe, b)
                    transposes(v, A1, lambda pair: v.wait("a_ready", pair + 1))
                    v.wait("tr_dve", 1)
                    v.wait("tr_act", 1)
                    for h in range(2):
                        for c in range(2):
                            last = pe.matmul(PS[:, 4 + h, 0:HALF], W1T[:, c, :], XT[:, c, h * HALF:(h + 1) * HALF],
                                             start=(c == 0), stop=(c == 1))
                    v.inc(last, "f0_ps")
                    v.wait("relu", 1)
                    for m in range(2):
                        for h in range(2):
                            last = pe.matmul(PS[0:FC, 2 * m + h, 0:HALF], W2T[:, m * FC:(m + 1) * FC],
                                             E[:, 0, h * HALF:(h + 1) * HALF], start=True, stop=True)
                        v.inc(last, "pr_ps")
                    v.wait("pr_act", 2)
                    for t in range(NT):
                        for c in range(2):
                            last = pe.matmul(PS[:, 4 + t // 2, (t % 2) * 256:(t % 2) * 256 + D],
                                             Fk[:, c, t * P:(t + 1) * P], WoT[:, c, :], start=(c == 0), stop=(c == 1))
                        if t % 2:
                            v.inc(last, "yo_ps")
                    transposes(v, A1, lambda pair: v.wait("a_ready", 3 + pair + 1))
                    v.wait("tr_dve", 2)
                    v.wait("tr_act", 2)
                    token_product(v, 4, WqkvT[:, :, 2 * D:3 * D], D, "v_ps")
                    feature_product(v, 0, WqkvT[:, :, 0:D], "f_ps")
                    v.wait("v_dve", 3)
                    feature_product(v, 4, WqkvT[:, :, D:2 * D], "f_ps")
                    v.wait("f_act", 2)
                    for t in range(NT):
                        if t >= 4:
                            v.wait("rr_dve", t - 3)
                        for c in range(2):
                            last = pe.matmul(PS[:, t % 4, c * 256:c * 256 + 6 * NREL], Fq[:, c, t * P:(t + 1) * P],
                                             EMB[:], start=True, stop=True)
                        v.inc(last, "rr_ps")
                    v.wait("aug_k", 96)
                    v.wait("aug_q", 96)
                    v.wait("f_act", 4)
                    for i in range(2 * H * NT):
                        if i % (2 * NT) == 0:
                            v.wait("dw_fix", i // (2 * NT) + 1)
                        pe_max(v, CR, CL, i, i, window(i // (2 * NT)))
                    for k in range(3):
                        v.wait("mt_dve", k + 1)
                        v.wait("m_free", 144 + k - 1)
                        for t in range(NT):
                            last = pe.transpose(PS[0:H * NT, 6 + k % 2, 0:384].bitcast(BF16)[:, t * P:(t + 1) * P],
                                                VVP[:, k, t, :], idb[:])
                        v.inc(last, "m_ps")
                    v.wait("md_r", 48)
                    v.wait("rr_dve", NT)
                    pe_phase(v, CL, CR, CORE + RROWS, False, False, 0, 147, rel=H)
                    v.wait("m_free", 153)
                    transposes(v, CTX)
                    v.wait("tr_dve", 3)
                    v.wait("tr_act", 3)
                    token_product(v, 4, WoutT, D, "yo2_ps")
                    transposes(v, A1, lambda pair: v.wait("a_ready", 6 + pair + 1))
                    v.wait("tr_dve", 4)
                    v.wait("tr_act", 4)
                    for t in range(NT):
                        for c in range(2):
                            last = pe.matmul(PS[:, 7, t * E_:(t + 1) * E_], XT[:, c, t * P:(t + 1) * P], Wg[:, c, :],
                                             start=(c == 0), stop=(c == 1))
                    v.inc(last, "lg_ps")

            @block.scalar
            def _(act):
                def first(l):
                    act.dma_start(Wqkcv[:], a["Wqkcv"][l]).then_inc(w_first, 16)
                    act.dma_start(bcol[:], a["bcol"][l]).then_inc(w_first, 16)
                    act.dma_start(brow[:, 0], a["brow"][l, 0].partition_broadcast(P)).then_inc(w_first, 16)

                def rest(l):
                    act.dma_start(Wo[:], a["Wo"][l]).then_inc(w_rest, 16)
                    act.dma_start(Wi[:], a["Wi"][l]).then_inc(w_rest, 16)
                    act.dma_start(Wo2[:], a["Wo2"][l]).then_inc(w_rest, 16)
                    act.dma_start(bicol[:], a["bicol"][l]).then_inc(w_rest, 16)
                    act.dma_start(brow[:, 1:7], a["brow"][l, 1:7].partition_broadcast(P)).then_inc(w_rest, 16)

                act.dma_start(HR[:], H0[0]).then_inc(h_in, 16)
                first(0)
                rest(0)
                act.wait_ge(w_once, 16 * NW_ONCE)
                with act.Fori(0, B) as b:
                    tv = tail.on(act, b)
                    norm_sd(tv, 1)
                    with act.Fori(0, L) as l:
                        p = b * L + l
                        v = lay.on(act, p)
                        take_transposed(v, 0, 1, True)
                        act.wait_ge(w_first, p * (16 * NW_FIRST) + 16 * NW_FIRST)
                        for o, f, bank in ((0, Fc, 0), (1, Fk, 4), (2, Fq, 0)):
                            for m in range(2):
                                v.wait("f_ps", 2 * o + m + 1)
                                v.inc(act.activation(halves(f[:, m, :]), chunk_view(bank, m), ACT.Identity,
                                                     bias=bcol[:, o, m:m + 1]), "f_act")
                            if o == 0:
                                v.wait("f_act", 2)
                                for m in range(2):
                                    v.inc(act.activation(SQ[:, m, :], Fc[:, m, :], ACT.Square), "sq_act")
                        for m in range(2):
                            v.wait("n_ps", m + 1)
                            v.inc(act.activation(halves(SQ[:, m, :]), chunk_view(4, m), ACT.Ln), "n_act")
                        v.wait("n_act", 2)
                        for m in range(2):
                            v.inc(act.activation(SQ[:, m, :], SQ[:, m, :], ACT.Exp, scale=-0.5), "n_act")
                        v.wait("v_dve", 3)
                        v.wait("f_act", 6)
                        first(l + 1)
                        for u in range(72):
                            act_exp(v, u, -1.0, 1.0)
                        for u in range(72):
                            act_exp(v, 72 + u, 0.25, 0.0)
                        take_transposed(v, 1, 1, True)
                        norm_sd(v, 1)
                        take_transposed(v, 2, 1, True)
                        act.wait_ge(w_rest, p * (16 * NW_REST) + 16 * NW_REST)
                        for f in range(2 * NM):
                            m, h = divmod(f, 2)
                            v.wait("f1_ps", f + 1)
                            v.inc(act.activation(HT[:, m, h * HALF:(h + 1) * HALF], PS[:, 4 + f % 4, 0:HALF],
                                                 ACT.Gelu, bias=bicol[:, m:m + 1]), "g_act")
                        norm_sd(v, 2)
                        act.wait_ge(x_ready, b * XPER + l * 3 + 6)
                        rest(l + 1)
                    v = tv
                    norm_sd(v, 2)
                    take_transposed(v, 0, 1, True)
                    v.wait("f0_ps", 1)
                    v.inc(act.activation(halves(E[:, 0, :]), PS[:, 4:6, 0:HALF], ACT.Relu, bias=fcol[:]), "relu")
                    for m in range(2):
                        v.wait("pr_ps", m + 1)
                        v.inc(act.activation(halves(Fk[:, m, :]), chunk_view(0, m), ACT.Identity,
                                             bias=f2col[:, m:m + 1]), "pr_act")
                    norm_sd(v, 3)
                    norm_sd(v, 4)
                    take_transposed(v, 1, 1, True)
                    for o, f, bank in ((0, Fq, 0), (1, Fk, 4)):
                        for m in range(2):
                            v.wait("f_ps", 2 * o + m + 1)
                            v.inc(act.activation(halves(f[:, m, :]), chunk_view(bank, m), ACT.Identity,
                                                 bias=qkcol[:, o, m:m + 1]), "f_act")
                    for u in range(72):
                        act_exp(v, u, 0.25, 0.0)
                    take_transposed(v, 2, 1, True)
                    norm_sd(v, 5)
                    v.wait("a_ready", 9)
                    act.dma_start(H1[b], HR[:]).then_inc(h_out, 16)
                    act.dma_start(XF[b], A1[:]).then_inc(h_out, 16)
                    take_transposed(v, 3, 1, True)
                    v.wait("out_ready", 1)
                    act.dma_start(LG[b], LGT[:]).then_inc(h_out, 16)
                    act.wait_ge(h_out, b * 48 + 48)
                    act.dma_start(HR[:], H0[b + 1]).then_inc(h_in, 16)
                act.wait_ge(h_in, 16 * (B + 1))

            @block.vector
            def _(dve):
                dve.wait_ge(w_once, 16 * NW_ONCE)
                dve.tensor_copy(idb[:], idf[:])
                dve.memset(VP[:], 2.0)
                dve.memset(BS[:], 0.0)
                dve.tensor_copy(OHB, OHF).then_inc(onehot_ready, 1)
                dve.tensor_scalar(negI[:], idf[:], -1.0, None, ALU.mult).then_inc(const_ready, 1)
                dve.wait_ge(const_ready, 1)
                dve.wait_ge(onehot_in, 16 * H)
                with dve.Fori(0, B) as b:
                    tv = tail.on(dve, b)
                    dve.wait_ge(h_in, b * 16 + 16)
                    dve.memset(AK[96:96 + MROWS, :, :], 1.0)
                    layer_norm(tv, None, HR, X, 1e-5, 1, lambda ins: ins.then_inc(x_ready, 1))
                    with dve.Fori(0, L) as l:
                        p = b * L + l
                        v = lay.on(dve, p)
                        take_transposed(v, 0, 0, False)
                        dve.wait_ge(w_first, p * (16 * NW_FIRST) + 16 * NW_FIRST)
                        dve_values(v, brow[:, 0])
                        v.wait("f_act", 4)
                        split(v, Fk, 1, "p_dve")
                        v.wait("n_act", 4)
                        v.link(dve.tensor_tensor(Fc, Fc, SQ, ALU.mult))
                        split(v, Fc, 0, "p_dve")
                        v.wait("f_act", 6)
                        split(v, Fq, 2, "p_dve")
                        dve_phase(v, True, 0, 0, False, False)
                        v.wait("m_free", 150)
                        v.link(dve.tensor_tensor(NMX[:], MX[:, 0], MX[:, 1], ALU.max))
                        v.link(dve.tensor_scalar(NMX[:], NMX[:], -1.0, None, ALU.mult))
                        v.link(dve.tensor_copy(NMP[:, 0], NMX[:]))
                        v.link(dve.tensor_tensor(NMR[:], NMX[:], NMP[:, 0], ALU.subtract))
                        v.link(dve.tensor_copy(NMP[:, 1], NMR[:]))
                        v.inc(dve.tensor_tensor(NMP[:, 2], NMR[:], NMP[:, 1], ALU.subtract), "mt_dve")
                        v.wait("m_ps", 151)
                        v.inc(dve.tensor_copy(MT[:], PS[0:H * NT, 6, 0:192].bitcast(BF16).rearrange(
                            "p (k t) -> p k t", k=3)), "m_free")
                        dve.wait_ge(w_rest, p * (16 * NW_REST) + 16 * NW_REST)
                        v.link(dve.tensor_tensor(X[:], X[:], row_bc(brow[:, 1], NT), ALU.add))
                        dve_phase(v, False, 72, 151, True, False)
                        take_transposed(v, 1, 0, False)
                        layer_norm(v, product(v, "y_ps", 4, lambda ts: X[:, ts, :], T2), T2, A1, 1e-12, 1,
                                   lambda ins: v.inc(ins, "a1_ready"), brow[:, 2], brow[:, 3])
                        take_transposed(v, 2, 0, False)
                        v.wait("tr_ps", 6)
                        v.link(dve.tensor_tensor(A1[:], A1[:], row_bc(brow[:, 4], NT), ALU.add))
                        layer_norm(v, product(v, "y2_ps", 4, lambda ts: A1[:, ts, :], T2), T2, X, 1e-12, 2,
                                   lambda ins: ins.then_inc(x_ready, 1), brow[:, 5], brow[:, 6])
                        v.close()
                    v = tv
                    dve.wait_ge(x_ready, b * XPER + XPER)
                    v.link(dve.tensor_tensor(HR[:], HR[:], X[:], ALU.add))
                    layer_norm(v, None, HR, A1, 1e-5, 2, lambda ins: v.inc(ins, "a_ready"))
                    take_transposed(v, 0, 0, False)
                    layer_norm(v, product(v, "yo_ps", 4, lambda ts: row_bc(frow[:, 0], 2), T2), T2, X, 1e-5, 3,
                               v.link, frow[:, 1], frow[:, 2])
                    v.link(dve.tensor_tensor(HR[:], HR[:], X[:], ALU.add))
                    layer_norm(v, None, HR, A1, 1e-5, 4, lambda ins: v.inc(ins, "a_ready"))
                    take_transposed(v, 1, 0, False)
                    dve_values(v, frow[:, 3])
                    v.wait("f_act", 2)
                    split(v, Fq, 0, "p_dve")
                    v.wait("f_act", 4)
                    split(v, Fk, 1, "p_dve")
                    for t in range(NT):
                        v.wait("rr_ps", t + 1)
                        if t:
                            v.wait("xs_w", 16 * t)
                        r = PS[:, t % 4, :].rearrange("p (c x) -> p c x", c=2)[:, :, 0:6 * NREL].rearrange(
                            "p c (h r) -> p c h r", h=6)
                        xs = XS.rearrange("p (c h) x -> p c h x", c=2)
                        rb = RB[:, t].rearrange("p (c h) r -> p c h r", c=2)
                        v.link(dve.tensor_copy(rb, r[:, :, :, 0:NREL:NREL - 1]))
                        v.inc(dve.tensor_copy(xs[:, :, :, FILL:FILL + NREL], r), "rr_dve")
                        dve.tensor_copy(XS[:, :, 0:FILL], RB[:, t, :, 0:1].broadcast_to([P, H, FILL]))
                        v.inc(dve.tensor_copy(XS[:, :, FILL + NREL:XL], RB[:, t, :, 1:2].broadcast_to([P, H, FILL])),
                              "xs")
                    for t in range(NT):
                        if t:
                            ins = dve.tensor_copy(BS[:, t, :, 0:t], RB[:, t, :, 0:1].broadcast_to([P, H, t]))
                        if t < NT - 1:
                            ins = dve.tensor_copy(BS[:, t, :, t + 1:NT],
                                                  RB[:, t, :, 1:2].broadcast_to([P, H, NT - 1 - t]))
                    v.link(ins)
                    for i in range(8):
                        fix_window(v, i)
                    for i in range(2 * H * NT):
                        h, qt, half = i // (2 * NT), i // 2 % NT, i % 2
                        v.wait("m_ps", i + 1)
                        v.inc(dve.tensor_reduce(MX6[:, qt, h, 3 * half:3 * half + 3],
                                                PS[:, 6 + i % 2, 0:HALF].rearrange("p (t s) -> p t s", t=3),
                                                AX.X, ALU.max), "m_free")
                        if i % (2 * NT) == 2 * NT - 1 and h >= 3:
                            fix_window(v, h + 5)
                    v.wait("m_free", 144)
                    v.link(dve.tensor_tensor(MX6[:], MX6[:], BS[:], ALU.add))
                    v.link(dve.tensor_reduce(M1[:], MX6[:], AX.X, ALU.max))
                    v.link(dve.tensor_tensor(MX6[:], BS[:], M1[:].unsqueeze(3).broadcast_to([P, NT, H, NT]),
                                             ALU.subtract))
                    mx6 = MX6[:].rearrange("p t h k -> p t (h k)")
                    for k in range(3):
                        ins = dve.tensor_copy(VVP[:, k], mx6)
                        v.inc(ins, "mt_dve")
                        if k < 2:
                            v.wait("mt_dve", k + 1)
                            v.link(dve.tensor_tensor(mx6, mx6, VVP[:, k], ALU.subtract))
                    for k in range(3):
                        v.wait("m_ps", 144 + k + 1)
                        v.inc(dve.tensor_copy(MT1[:, k, :], PS[0:H * NT, 6 + k % 2, 0:384].bitcast(BF16)), "m_free")
                    for i in range(17, 20):
                        fix_window(v, i)

                    def more(g):
                        if g == 0:
                            for i in range(20, 24):
                                fix_window(v, i)

                    v.link(dve.tensor_tensor(HR[:], HR[:], row_bc(frow[:, 4], NT), ALU.add))
                    dve_phase(v, False, 0, 147, False, True, more)
                    take_transposed(v, 2, 0, False)
                    layer_norm(v, product(v, "yo2_ps", 4, lambda ts: HR[:, ts, :], HR), HR, A1, 1e-5, 5,
                               lambda ins: v.inc(ins, "a_ready"))
                    take_transposed(v, 3, 0, False)
                    v.wait("lg_ps", 1)
                    v.inc(dve.tensor_copy(LGT[:], PS[:, 7, 0:NT * E_].rearrange("p (t e) -> p t e", t=NT)),
                          "out_ready")
                    v.close()

            @block.sync
            def _(sp):
                for dst, src in once:
                    sp.dma_start(dst, src).then_inc(w_once, 16)
                sp.wait_ge(onehot_ready, 1)
                for h in range(H):
                    sp.dma_start(CL[CORE:CORE + RROWS, h, :], OHB).then_inc(onehot_in, 16)
                sp.wait_ge(onehot_in, 16 * H)

                def spread(v, dst, o, part_of, sig, h0=0, h1=H):
                    for s_, k in enumerate(part_of):
                        v.inc(sp.dma_start(dst[s_ * DH:(s_ + 1) * DH, h0:h1, :],
                                           PD[o, k].rearrange("(h d) t -> d h t", h=H)[:, h0:h1, :]), sig, 16)

                def to_dram(v, o, n):
                    for k in range(1):
                        v.inc(sp.dma_start(PD[o].rearrange("k (c f) t -> f k c t", c=2), parts[:, o]), "pd_w", 16)
                    v.wait("pd_w", 16 * n)

                with sp.Fori(0, B) as b:
                    with sp.Fori(0, L) as l:
                        v = lay.on(sp, b * L + l)
                        v.wait("p_dve", 1)
                        to_dram(v, 1, 1)
                        spread(v, AK, 1, KEY_PARTS, "aug0", 0, G)
                        v.wait("p_dve", 2)
                        to_dram(v, 0, 2)
                        spread(v, CL, 0, KEY_PARTS, "aug0", 0, G)
                        spread(v, CR, 0, QRY_PARTS, "aug0", 0, G)
                        v.wait("p_dve", 3)
                        to_dram(v, 2, 3)
                        spread(v, AQ, 2, QRY_PARTS, "aug0", 0, G)
                        for g in range(1, NG):
                            for dst, o, part_of in ((CL, 0, KEY_PARTS), (CR, 0, QRY_PARTS), (AK, 1, KEY_PARTS),
                                                    (AQ, 2, QRY_PARTS)):
                                spread(v, dst, o, part_of, f"aug{g}", g * G, (g + 1) * G)
                        v.wait("m_free", 151)
                        v.inc(sp.dma_start(MD.rearrange("k r t -> r k t"), MT[:]), "md_w", 16)
                        v.wait("md_w", 16)
                        v.inc(sp.dma_start(AQ[CORE:CORE + MROWS, :, :].rearrange("k h s -> k (h s)"),
                                           MD.rearrange("k r t -> k (r t)")), "md_r", 16)
                    v = tail.on(sp, b)
                    v.wait("p_dve", 1)
                    to_dram(v, 0, 1)
                    spread(v, CR, 0, QRY_PARTS, "aug_q")
                    v.wait("p_dve", 2)
                    to_dram(v, 1, 2)
                    spread(v, CL, 1, KEY_PARTS, "aug_k")
                    for t in range(NT):
                        v.wait("xs", t + 1)
                        v.inc(sp.dma_start(XD[t * P:(t + 1) * P, :, :], XS), "xs_w", 16)
                    v.wait("xs_w", 16 * NT)
                    for i in range(24):
                        if 8 <= i < 20:
                            v.wait("m_ps", 2 * NT * (i - 8 + 1))
                        if i == 20:
                            v.wait("m_free", 144 + 3)
                            v.inc(sp.dma_start(RD.rearrange("k r t -> r k t"), MT1), "md_w", 16)
                            v.wait("md_w", 16)
                            for k in range(3):
                                v.inc(sp.dma_start(CR[CORE + k * NT:CORE + (k + 1) * NT, :, :],
                                                   RD[k].rearrange("(h t) s -> t h s", h=H)), "md_r", 16)
                            v.wait("sc_ps", 4 * NT)
                        h = i % H
                        w = window(i)
                        for qt in range(NT):
                            src = bass.AP(XD.tensor, qt * P * H * XL + h * XL + P - 1,
                                          [[H * XL - 1, P], [1, WIN]])
                            v.inc(sp.dma_start(w[:, qt, :], src), f"dw_in{i % 8}", 16)


def experts(nc, a, H1, XF, LG, XG, YD, out):
    with ExitStack() as ctx:
        sb = lambda n, s, d: ctx.enter_context(nc.sbuf_tensor(n, s, d))
        sem = lambda n: ctx.enter_context(nc.semaphore(n))
        T = B * NT
        lg = sb("lg", [P, T, E_], F32)
        xf = sb("xf", [P, T, D], F32)
        h1 = sb("h1", [P, T, D], F32)
        gy = sb("gy", [P, T, TOPK, D], F32)
        v8 = sb("v8", [P, T, 8], F32)
        i8 = sb("i8", [P, T, 8], U32)
        idx = sb("idx", [P, T, TOPK], F32)
        iota = sb("iota", [P, E_], F32)
        oh = sb("oh", [P, T, TOPK, E_], F32)
        ohb = sb("ohb", [P, T, TOPK, E_], BF16)
        trif = sb("trif", [P, P], F32)
        trib = sb("trib", [P, P], BF16)
        oneb = sb("oneb", [P, P], BF16)
        idm = sb("idm", [P, P], F32)
        tot = sb("tot", [P, T, TOPK * E_], F32)
        pre = [sb(f"pre{i}", [P, T, TOPK * E_], F32) for i in range(2)]
        pos = sb("pos", [P, T, TOPK], F32)
        keep = sb("keep", [P, T, TOPK], F32)
        slot = sb("slot", [P, T, TOPK], F32)
        koff = sb("koff", [P, TOPK], F32)
        sidf = sb("sidf", [P, T, TOPK], F32)
        sid = sb("sid", [P, T, TOPK], I32)
        gidf = sb("gidf", [P, T, TOPK], F32)
        gid = sb("gid", [P, T, TOPK], I32)
        dv = sb("dv", [P, T], F32)
        ew = sb("ew", [P, T], F32)
        den = sb("den", [P, T], F32)
        w = sb("w", [P, T, TOPK], F32)
        w1 = sb("w1", [FC, 2, 2, 2 * HID], F32)
        w2 = sb("w2", [P, 2, 4, D], F32)
        xg = sb("xg", [CP, 2, CC, D], F32)
        xgT = sb("xgT", [FC, 2, 2, CAP], F32)
        sg = sb("sg", [P, 2, CAP], F32)
        at = sb("at", [P, 2, 4, CAP], F32)
        ye = sb("ye", [CP, 2, CC, D], F32)
        PS = ctx.enter_context(nc.psum_tensor("PSX", [P, 8, BANK], F32))

        const_in, lg_in, xf_in, h1_in = sem("x_const_in"), sem("lg_in"), sem("xf_in"), sem("h1_in")
        oh_ready, pos_ps, dv_ready, ew_ready = sem("oh_ready"), sem("pos_ps"), sem("dv_ready"), sem("ew_ready")
        sid_ready, gid_ready, step = sem("sid_ready"), sem("gid_ready"), sem("x_step")
        scattered, gathered, done, stored = sem("scattered"), sem("gathered"), sem("x_done"), sem("x_stored")

        def passes(eng, body):
            body(ex.on(eng, 0), 0)
            with eng.Fori(1, E_ // 2) as i:
                body(ex.on(eng, i), i)

        U = 2 * TOPK
        ex = Counts(nc, ctx, "e_", dict(w_in0=32, w_in1=32, xg_in0=8 * U, xg_in1=8 * U, y_out0=8 * U, y_out1=8 * U, xt_ps=2 * U, xt_dve=U, xt_act=U, ug_ps=4 * U,
                                        silu=4 * U, at=4 * U, y_ps=2 * U, ye=2 * U))

        with nc.Block() as block:
            @block.sync
            def _(sp):
                sp.dma_start(lg[:].rearrange("p (b t) e -> p b (t e)", b=B),
                             LG.rearrange("b p t e -> p b (t e)")).then_inc(lg_in, 16)
                sp.dma_start(xf[:].rearrange("p (b t) d -> p b (t d)", b=B), XF.rearrange("b p t d -> p b (t d)")).then_inc(xf_in, 16)
                for dst, src in ((iota[:], a["iota"].partition_broadcast(P)), (koff[:], a["koff"].partition_broadcast(P)),
                                 (trif[:], a["tri"]), (idm[:], a["ident"])):
                    sp.dma_start(dst, src).then_inc(const_in, 16)
                sp.dma_start(h1[:].rearrange("p (b t) d -> p b (t d)", b=B), H1.rearrange("b p t d -> p b (t d)")).then_inc(h1_in, 16)
                sp.wait_ge(scattered, 16 * T * TOPK)

                def loads(v, i):
                    for u in range(U):
                        j, k = divmod(u, TOPK)
                        if k == 0:
                            v.wait("y_ps", 4 * j - 4)
                            sp.wait_ge(const_in, 64)
                            v.inc(sp.dma_start(w1[:, j], a["W1"][2 * i + j]), f"w_in{j}", 16)
                            v.inc(sp.dma_start(w2[:, j], a["W2"][2 * i + j]), f"w_in{j}", 16)
                        v.wait("xt_ps", 2 * u - 2)
                        sp.wait_ge(const_in, 64)
                        v.inc(sp.dma_start(xg[:, u % 2], XG[bass.ds((2 * i + (k * E_ + j)) * CAP, CAP), :]
                                           .rearrange("(p c) d -> p c d", c=CC)), f"xg_in{u % 2}", 16)

                passes(sp, loads)
                sp.wait_ge(done, 1)
                sp.dma_start(out.rearrange("b (t p) d -> p (b t) d", p=P), h1[:]).then_inc(stored, 16)
                sp.wait_ge(stored, 16)

            @block.gpsimd
            def _(pool):
                pool.wait_ge(xf_in, 16)
                pool.wait_ge(sid_ready, 1)
                for t in range(T):
                    for k in range(TOPK):
                        pool.indirect_dma_start(
                            out=XG, out_offset=bass.IndirectOffsetOnAxis(ap=sid[:, t, k:k + 1], axis=0),
                            in_=xf[:, t, :], in_offset=None, bounds_check=SLOTS - 1, oob_is_err=False
                        ).then_inc(scattered, 16)

                for r in range(2):
                    pool.wait_ge(ex.sem[f"y_out{r}"], (E_ // 2) * 8 * U)
                pool.wait_ge(gid_ready, 1)
                for t in range(T):
                    for k in range(TOPK):
                        pool.indirect_dma_start(
                            out=gy[:, t, k, :], out_offset=None, in_=YD,
                            in_offset=bass.IndirectOffsetOnAxis(ap=gid[:, t, k:k + 1], axis=0)
                        ).then_inc(gathered, 16)

            @block.scalar
            def _(act):
                act.wait_ge(dv_ready, 1)
                act.activation(ew[:], dv[:], ACT.Exp).then_inc(ew_ready, 1)

                def store(v, i, u):
                    j, k = divmod(u, TOPK)
                    v.wait("ye", 2 * u + 2)
                    v.inc(act.dma_start(YD[bass.ds((2 * i + (k * E_ + j)) * CAP, CAP), :]
                                        .rearrange("(p c) d -> p c d", c=CC), ye[:, u % 2]), f"y_out{u % 2}", 16)

                def silus(v, i):
                    for u in range(U):
                        v.wait("xt_ps", 2 * u + 2)
                        v.inc(act.activation(xgT[:, u % 2, 1, :], PS[0:FC, 1, 0:CAP], ACT.Copy), "xt_act")
                        for jj in range(4):
                            q = 4 * u + jj
                            v.wait("ug_ps", q + 1)
                            v.wait("at", q - 1)
                            v.inc(act.activation(sg[:, q % 2], PS[:, 3 + 2 * (q % 2), 0:CAP], ACT.Silu), "silu")
                            if u and jj == 1:
                                store(v, i, u - 1)
                    store(v, i, U - 1)

                passes(act, silus)

            @block.tensor
            def _(pe):
                pe.wait_ge(oh_ready, 1)
                ohm = ohb[:].rearrange("p t k e -> p (t k e)")
                pe.matmul(PS[:, 0, 0:T * TOPK * E_], trib[:], ohm, start=True, stop=True)
                pe.matmul(PS[:, 1, 0:T * TOPK * E_], oneb[:], ohm, start=True, stop=True).then_inc(pos_ps, 1)
                pe.wait_ge(sid_ready, 1)
                pe.wait_ge(const_in, 16 * 4)

                def blocks(v, i):
                    for u in range(U):
                        j, k = divmod(u, TOPK)
                        v.wait(f"xg_in{u % 2}", 16 * (u // 2 + 1))
                        v.wait("xt_dve", u)
                        v.wait("xt_act", u)
                        for c in range(2):
                            for cc in range(CC):
                                last = pe.transpose(PS[0:FC, c, cc * CP:(cc + 1) * CP],
                                                    xg[:, u % 2, cc, c * FC:(c + 1) * FC], idm[0:CP, 0:CP])
                            v.inc(last, "xt_ps")
                        v.wait(f"w_in{j}", 32)
                        v.wait("xt_dve", u + 1)
                        v.wait("xt_act", u + 1)
                        for jj in range(4):
                            q = 4 * u + jj
                            v.wait("at", q - 1)
                            for half in range(2):
                                for c in range(2):
                                    last = pe.matmul(PS[:, 2 + 2 * (q % 2) + half, 0:CAP],
                                                     w1[:, j, c, half * HID + jj * P:half * HID + (jj + 1) * P],
                                                     xgT[:, u % 2, c, :], start=(c == 0), stop=(c == 1))
                            v.inc(last, "ug_ps")
                        v.wait("at", 4 * u + 4)
                        v.wait("ye", 2 * u)
                        for cc in range(CC):
                            for jj in range(4):
                                last = pe.matmul(PS[0:CP, 6 + cc // 2, (cc % 2) * 256:(cc % 2) * 256 + D],
                                                 at[:, u % 2, jj, cc * CP:(cc + 1) * CP], w2[:, j, jj, :],
                                                 start=(jj == 0), stop=(jj == 3))
                            if cc % 2:
                                v.inc(last, "y_ps")

                passes(pe, blocks)

            @block.vector
            def _(dve):
                links = [0]

                def link(ins):
                    links[0] += 1
                    ins.then_inc(step, 1)
                    dve.wait_ge(step, links[0])

                dve.memset(oneb[:], 1.0)
                dve.wait_ge(lg_in, 16)
                dve.wait_ge(const_in, 16 * 4)
                link(dve.tensor_copy(trib[:], trif[:]))
                for t in range(T):
                    ins = dve.max(v8[:, t, :], lg[:, t, :])
                link(ins)
                for t in range(T):
                    ins = dve.max_index(i8[:, t, :], v8[:, t, :], lg[:, t, :])
                link(ins)
                dve.tensor_tensor(dv[:], v8[:, :, 1], v8[:, :, 0], ALU.subtract).then_inc(dv_ready, 1)
                link(dve.tensor_copy(idx[:], i8[:, :, 0:TOPK]))
                for k in range(TOPK):
                    ins = dve.tensor_tensor(oh[:, :, k, :], idx[:, :, k:k + 1].broadcast_to([P, T, E_]),
                                            iota[:].unsqueeze(1).broadcast_to([P, T, E_]), ALU.is_equal)
                link(ins)
                dve.tensor_copy(ohb[:], oh[:]).then_inc(oh_ready, 1)
                dve.wait_ge(pos_ps, 1)
                three = lambda bank: PS[:, bank, 0:T * TOPK * E_].rearrange("p (t x) -> p t x", t=T)
                link(dve.tensor_copy(tot[:], three(1)))
                link(dve.tensor_copy(pre[0][:], tot[:]))
                src, s_ = 0, 1
                while s_ < T:
                    link(dve.tensor_tensor(pre[1 - src][:, s_:T], pre[src][:, s_:T], pre[src][:, 0:T - s_], ALU.add))
                    link(dve.tensor_copy(pre[1 - src][:, 0:s_], pre[src][:, 0:s_]))
                    src, s_ = 1 - src, 2 * s_
                link(dve.tensor_tensor(pre[src][:], pre[src][:], tot[:], ALU.subtract))
                link(dve.tensor_tensor(pre[src][:], pre[src][:], three(0), ALU.add))
                ohv = oh[:].rearrange("p t k e -> p t (k e)")
                link(dve.tensor_tensor(pre[src][:], pre[src][:], ohv, ALU.mult))
                link(dve.tensor_reduce(pos[:], pre[src][:].rearrange("p t (k e) -> p t k e", k=TOPK), AX.X, ALU.add))
                link(dve.tensor_scalar(keep[:], pos[:], float(CAP), None, ALU.is_le))
                link(dve.scalar_tensor_tensor(out=slot[:], in0=idx[:], scalar=float(CAP), in1=pos[:],
                                              op0=ALU.mult, op1=ALU.add))
                link(dve.tensor_tensor(slot[:], slot[:], koff[:].unsqueeze(1).broadcast_to([P, T, TOPK]), ALU.add))
                link(dve.tensor_scalar(sidf[:], keep[:], float(-2 * SLOTS), float(2 * SLOTS), ALU.mult, ALU.add))
                link(dve.tensor_tensor(sidf[:], sidf[:], slot[:], ALU.add))
                dve.tensor_copy(sid[:], sidf[:]).then_inc(sid_ready, 1)
                link(dve.tensor_tensor(gidf[:], slot[:], keep[:], ALU.mult))
                dve.tensor_copy(gid[:], gidf[:]).then_inc(gid_ready, 1)
                dve.wait_ge(ew_ready, 1)
                link(dve.tensor_scalar(den[:], ew[:], 1.0, None, ALU.add))
                link(dve.reciprocal(den[:], den[:]))
                link(dve.tensor_copy(w[:, :, 0], den[:]))
                link(dve.tensor_tensor(w[:, :, 1], den[:], ew[:], ALU.mult))
                link(dve.tensor_tensor(w[:], w[:], keep[:], ALU.mult))

                def products(v, i):
                    for u in range(U):
                        v.wait("xt_ps", 2 * u + 1)
                        v.inc(dve.tensor_copy(xgT[:, u % 2, 0, :], PS[0:FC, 0, 0:CAP]), "xt_dve")
                        for jj in range(4):
                            q = 4 * u + jj
                            v.wait("silu", q + 1)
                            v.wait("y_ps", 2 * u - 2)
                            v.inc(dve.tensor_tensor(at[:, u % 2, jj, :], PS[:, 2 + 2 * (q % 2), 0:CAP], sg[:, q % 2],
                                                    ALU.mult), "at")
                        for c in range(2):
                            v.wait("y_ps", 2 * u + c + 1)
                            v.wait(f"y_out{u % 2}", 16 * (u // 2))
                            o = PS[0:CP, 6 + c, :].rearrange("p (t x) -> p t x", t=2)[:, :, 0:D]
                            v.inc(dve.tensor_copy(ye[:, u % 2, 2 * c:2 * c + 2, :], o), "ye")

                passes(dve, products)
                dve.wait_ge(h1_in, 16)
                dve.wait_ge(gathered, 16 * T * TOPK)
                for k in range(TOPK):
                    for t in range(T):
                        ins = dve.scalar_tensor_tensor(out=h1[:, t, :], in0=gy[:, t, k, :], scalar=w[:, t, k:k + 1],
                                                       in1=h1[:, t, :], op0=ALU.mult, op1=ALU.add)
                    if k < TOPK - 1:
                        link(ins)
                ins.then_inc(done, 1)


def program(nc, a, out, scratch):
    embed(nc, a, scratch["H0"], scratch["XG"])
    layers(nc, a, scratch["H0"], scratch["H1"], scratch["XF"], scratch["LG"], scratch["PD"], scratch["MD"],
           scratch["RD"], scratch["XD"])
    experts(nc, a, scratch["H1"], scratch["XF"], scratch["LG"], scratch["XG"], scratch["YD"], out)


def chunks(w):
    return w.reshape(2, FC, -1).transpose(1, 0, 2)


def kernel(**x):
    import numpy as np
    import concourse.bacc as bacc
    from concourse.bass_utils import run_bass_kernel_spmd as run

    x = {k: np.asarray(v) for k, v in x.items()}
    again = list(range(L)) + [0]
    col = lambda v, n: v.reshape(-1, n).T
    la = {k[8:]: v for k, v in x.items() if k.startswith("L0_attn_")}
    a = {
        "ids": x["x_txt"].reshape(B * 4, P).T,
        "curve": x["L0_tok_curve"].reshape(2, P, 2).transpose(1, 0, 2),
        "tok_w": x["L0_tok_proj_w"].T,
        "tok_b": x["L0_tok_proj_b"],
        "txt_w": x["L0_txt_weights"],
        "colmask": (np.arange(D)[None, :] < np.array([192, 96, 144, 192])[:, None]).astype(np.float32),
        "emb": x["L0_txt_emb_weight"],
        "img": x["x"].reshape(-1, 1),
        "ident": np.eye(P, dtype=np.float32),
        "headblk": np.kron(np.eye(H // 2), np.ones((DH, DH))).astype(np.float32),
        "onehot": np.tile(np.kron(np.eye(NT), np.ones((1, P))), (3, 1)).astype(np.float32),
        "Wqkcv": np.stack([np.concatenate([chunks(la[k][l]) for k in ("Wq", "Wk", "Wc", "Wv")], axis=2)
                           for l in again]),
        "bcol": np.stack([np.stack([col(la[k][l], FC) for k in ("bc", "bk", "bq")], axis=1) for l in again]),
        "Wo": np.stack([chunks(la["Wo"][l]) for l in again]),
        "Wi": np.stack([chunks(la["Wi"][l]) for l in again]),
        "Wo2": np.stack([la["Wo2"][l].reshape(NM, P, D).transpose(1, 0, 2) for l in again]),
        "bicol": np.stack([col(la["bi"][l], P) for l in again]),
        "brow": np.stack([np.stack([la[k][l] for k in ("bv", "bo", "g1", "b1", "bo2", "g2", "b2")])
                          for l in again]),
        "W1T": chunks(x["L0_ffn_W1"].T),
        "W2T": x["L0_ffn_W2"].T,
        "WoT": chunks(x["L0_ffn_Wo"].T),
        "WqkvT": chunks(x["L1_attn_qkv_w"].T),
        "WoutT": chunks(x["L1_attn_out_w"].T),
        "Wg": chunks(x["L1_ffn_Wg"]),
        "relbd": block_diagonal(np, x["L1_attn_rel_pos_emb"].T),
        "fcol": x["L0_ffn_b1"].reshape(P, 1),
        "f2col": col(x["L0_ffn_b2"], FC),
        "qkcol": np.stack([col(x["L1_attn_qkv_b"][i * D:(i + 1) * D], FC) for i in range(2)], axis=1),
        "frow": np.stack([x["L0_ffn_bo"], x["L0_ffn_gamma"], x["L0_ffn_beta"], x["L1_attn_qkv_b"][2 * D:],
                          x["L1_attn_out_b"]]),
        "iota": np.arange(E_, dtype=np.float32),
        "koff": np.array([k * E_ * CAP - 1 for k in range(TOPK)], np.float32),
        "tri": np.triu(np.ones((P, P), np.float32)),
        "W1": np.stack([chunks(w) for w in x["L1_ffn_W1"]]),
        "W2": x["L1_ffn_W2"].reshape(E_, 4, P, D).transpose(0, 2, 1, 3),
    }
    a = {k: np.ascontiguousarray(v) for k, v in a.items()}
    nc = bacc.Bacc("TRN2", target_bir_lowering=False, num_devices=1)
    aps = {k: nc.dram_tensor("in_" + k, v.shape, mybir.dt.from_np(v.dtype), kind="ExternalInput").ap()
           for k, v in a.items()}
    out = nc.dram_tensor("out_0", (B, S, D), F32, kind="ExternalOutput").ap()
    scratch = {k: nc.dram_tensor("scratch_" + k, shape, dt).ap() for k, shape, dt in (
        ("H0", (B + 1, P, NT, D), F32), ("H1", (B, P, NT, D), F32), ("XF", (B, P, NT, D), F32),
        ("LG", (B, P, NT, E_), F32), ("XG", (SLOTS, D), F32), ("YD", (SLOTS, D), F32),
        ("PD", (3, 3, D, S), BF16), ("MD", (3, H * NT, P), BF16), ("RD", (3, H * NT, S), BF16),
        ("XD", (S, H, XL), F32))}
    program(nc, aps, out, scratch)
    r = run(nc, [{"in_" + k: v for k, v in a.items()}], core_ids=[0])
    return r.results[0]["out_0"]


def block_diagonal(np, w):
    out = np.zeros((FC, (H // 2) * NREL), w.dtype)
    for h in range(H // 2):
        out[h * DH:(h + 1) * DH, h * NREL:(h + 1) * NREL] = w
    return out
```

```python
import concourse.bass as bass
from concourse import mybir
from concourse.alu_op_type import AluOpType as ALU
from contextlib import ExitStack

F32 = mybir.dt.float32
BF16 = mybir.dt.bfloat16
I32 = mybir.dt.int32
U32 = mybir.dt.uint32
ACT = mybir.ActivationFunctionType
AX = mybir.AxisListType

P = 128
B, NPATCH, NTXT = 4, 256, 512
S = NPATCH + NTXT
NT = S // P
D, H, DH = 192, 12, 16
L = 4
FC = D // 2
HALF = S // 2
FF = 768
NM = FF // P
BANK = 512
G = 4
NG = H // G
PLANE = 224 * 224
VOCAB = 50257
MAXREL = 16
NREL = 2 * MAXREL + 1
WIN = 192
XL = WIN + P - 1
FILL = (XL - NREL) // 2
E_, TOPK, HID = 8, 2, 512
N = B * S
CAP = int(1.2 * N / E_)
CP, CC = 115, 4
NBLK = TOPK * E_
SLOTS = NBLK * CAP

KEY_PARTS = (0, 0, 0, 1, 1, 2)
QRY_PARTS = (0, 1, 2, 0, 1, 0)
NRUN = 6
CORE = len(KEY_PARTS) * DH
MROWS = 3
RROWS = 3 * NT


LSTEP, TSTEP = 96, 136


class Counts:

    def __init__(self, nc, ctx, prefix, per):
        self.per, self.prefix = per, prefix
        self.sem = {k: ctx.enter_context(nc.semaphore(prefix + k)) for k in per}

    def on(self, eng, passes):
        return View(self, eng, passes)


class View:

    def __init__(self, counts, eng, passes):
        self.c, self.eng, self.passes, self.links = counts, eng, passes, {}

    def wait(self, name, k):
        if isinstance(self.passes, int) and self.passes * self.c.per[name] + k <= 0:
            return
        self.eng.wait_ge(self.c.sem[name], self.passes * self.c.per[name] + k)

    def inc(self, ins, name, by=1):
        ins.then_inc(self.c.sem[name], by)

    def link(self, ins, name="dve_step"):
        self.links[name] = self.links.get(name, 0) + 1
        ins.then_inc(self.c.sem[name], 1)
        self.wait(name, self.links[name])

    def close(self, name="dve_step"):
        assert self.links.get(name, 0) == self.c.per[name], (self.c.prefix, self.links.get(name, 0))


def attention_order(runs, lead, rate, bias_jobs):
    ring = iter(range(10 ** 6))
    total = 2 * H * NT
    per_group = 2 * G * NT
    job = 0
    due = None
    blocks = [(kind, g, kt) for kind, g in runs for kt in range(NT)]

    def maxima(n):
        nonlocal job, due
        while job < min(n, total):
            yield ("max", job, next(ring))
            job += 1
            if job % per_group == 0:
                due = job // per_group - 1
                yield ("negmax", due)
            elif due is not None and job % per_group == 8:
                yield from bias()

    def bias():
        nonlocal due
        if due is not None:
            for k in range(bias_jobs):
                yield ("bias", due, k, next(ring))
            due = None

    yield from maxima(lead)
    quota = float(lead)
    ended = None
    for n in range(len(blocks) + 1):
        for j in range(G):
            if j == 1 and (job == total or not rate(n)):
                yield from bias()
            if n < len(blocks):
                yield ("unit", n) + blocks[n] + (j,)
                quota += rate(n) / G
                yield from maxima(int(quota + 1e-6))
            if n and j % 2:
                yield ("av", n - 1) + blocks[n - 1] + (j // 2,)
        if ended is not None:
            for half in range(2):
                yield ("norm", ended) + runs[ended] + (half, next(ring))
            ended = None
        if n and (n - 1) % NT == NT - 1:
            ended = (n - 1) // NT
            yield ("evac", ended)
    for half in range(2):
        yield ("norm", ended) + runs[ended] + (half, next(ring))


COS, DOT = 0, 1
LAYER_ORDER = list(attention_order([(COS, 0), (COS, 1), (DOT, 0), (COS, 2), (DOT, 1), (DOT, 2)], 0,
                                   lambda n: 0 if n < 1 else 6, 1))
TAIL_ORDER = list(attention_order([(DOT, 0), (DOT, 1), (DOT, 2)], 64, lambda n: 6.4 if n < NT - 1 else 0 if n <= NT else 12, 3))


def embed(nc, a, H0, XG):
    with ExitStack() as ctx:
        sb = lambda n, s, d: ctx.enter_context(nc.sbuf_tensor(n, s, d))
        sem = lambda n: ctx.enter_context(nc.semaphore(n))
        ids = sb("ids", [P, B * 4], I32)
        cur = sb("cur", [P, 2, 2], I32)
        curf = sb("curf", [P, 2, 2], F32)
        pixf = sb("pixf", [P, 2], F32)
        pix = sb("pix", [P, 2], I32)
        pw = sb("pw", [P, 4, D], F32)
        wt = sb("wt", [P, 4], F32)
        mask = sb("mask", [P, 4, D], F32)
        cs = sb("cs", [P, D], F32)
        gim = sb("gim", [P, 2, 3 * B], F32)
        hs = sb("hs", [P, B, NT, D], F32)
        zero = sb("zero", [CP, 8 * D], F32)
        loaded, pix_ready = sem("emb_loaded"), sem("pix_ready")
        img_in, txt_in, step = sem("img_in"), sem("txt_in"), sem("emb_step")
        h_ready, stored, zeroed, zset = sem("h_ready"), sem("h_stored"), sem("xg_zeroed"), sem("zero_set")
        nload = 6

        with nc.Block() as block:
            @block.sync
            def _(sp):
                sp.dma_start(ids[:], a["ids"]).then_inc(loaded, 16)
                sp.dma_start(cur[:], a["curve"]).then_inc(loaded, 16)
                sp.dma_start(pw[:, 0:3], a["tok_w"].partition_broadcast(P)).then_inc(loaded, 16)
                sp.dma_start(pw[:, 3], a["tok_b"].partition_broadcast(P)).then_inc(loaded, 16)
                sp.dma_start(wt[:], a["txt_w"].partition_broadcast(P)).then_inc(loaded, 16)
                sp.dma_start(mask[:], a["colmask"].partition_broadcast(P)).then_inc(loaded, 16)
                sp.wait_ge(zset, 1)
                for i in range(8):
                    sp.dma_start(XG[i * SLOTS // 8:(i + 1) * SLOTS // 8, :].rearrange("(p c) d -> p (c d)", p=CP),
                                 zero[:]).then_inc(zeroed, 16)
                sp.wait_ge(h_ready, 1)
                sp.dma_start(H0[0:B].rearrange("b p t d -> p b t d"), hs[:]).then_inc(stored, 16)
                sp.dma_start(H0[B], hs[:, 0]).then_inc(stored, 16)
                sp.wait_ge(stored, 32)
                sp.wait_ge(zeroed, 8 * 16)

            @block.gpsimd
            def _(pool):
                pool.wait_ge(loaded, 16 * nload)
                for b in range(B):
                    for t in range(4):
                        pool.indirect_dma_start(
                            out=hs[:, b, 2 + t, :], out_offset=None, in_=a["emb"],
                            in_offset=bass.IndirectOffsetOnAxis(ap=ids[:, b * 4 + t:b * 4 + t + 1], axis=0)
                        ).then_inc(txt_in, 16)
                pool.wait_ge(pix_ready, 1)
                for t in range(2):
                    for c in range(3 * B):
                        pool.indirect_dma_start(
                            out=gim[:, t, c:c + 1], out_offset=None, in_=a["img"],
                            in_offset=bass.IndirectOffsetOnAxis(ap=pix[:, t:t + 1], axis=0),
                            element_offset=c * PLANE).then_inc(img_in, 16)

            @block.vector
            def _(dve):
                links = [0]

                def link(ins):
                    links[0] += 1
                    ins.then_inc(step, 1)
                    dve.wait_ge(step, links[0])

                dve.memset(zero[:], 0.0).then_inc(zset, 1)
                dve.wait_ge(loaded, 16 * nload)
                link(dve.tensor_copy(curf[:], cur[:]))
                link(dve.scalar_tensor_tensor(out=pixf[:], in0=curf[:, :, 1], scalar=224.0, in1=curf[:, :, 0],
                                              op0=ALU.mult, op1=ALU.add))
                dve.tensor_copy(pix[:], pixf[:]).then_inc(pix_ready, 1)
                link(dve.tensor_scalar(cs[:], mask[:, 0], wt[:, 0:1], None, ALU.mult))
                for i in range(1, 4):
                    link(dve.scalar_tensor_tensor(out=cs[:], in0=mask[:, i], scalar=wt[:, i:i + 1], in1=cs[:],
                                                  op0=ALU.mult, op1=ALU.add))
                dve.wait_ge(txt_in, 16 * 16)
                link(dve.tensor_tensor(hs[:, :, 2:NT, :], hs[:, :, 2:NT, :],
                                       cs[:].unsqueeze(1).unsqueeze(1).broadcast_to([P, B, 4, D]), ALU.mult))
                dve.wait_ge(img_in, 16 * 2 * 3 * B)
                last = None
                for c in range(3):
                    for b in range(B):
                        for t in range(2):
                            prev = pw[:, 3] if c == 0 else hs[:, b, t]
                            last = dve.scalar_tensor_tensor(out=hs[:, b, t], in0=pw[:, c],
                                                            scalar=gim[:, t, 3 * b + c:3 * b + c + 1], in1=prev,
                                                            op0=ALU.mult, op1=ALU.add)
                    if c < 2:
                        link(last)
                last.then_inc(h_ready, 1)


def layers(nc, a, H0, H1, XF, LG, PD, MD, RD, XD):
    with ExitStack() as ctx:
        sb = lambda n, s, d: ctx.enter_context(nc.sbuf_tensor(n, s, d))
        sem = lambda n: ctx.enter_context(nc.semaphore(n))

        X = sb("X", [P, NT, D], F32)
        HR = sb("HR", [P, NT, D], F32)
        A1 = sb("A1", [P, NT, D], F32)
        XT = sb("XT", [FC, 2, S], F32)
        PARTS = sb("PARTS", [P, 3 * 3 * 2 * S], BF16)
        parts = PARTS[0:FC, :].rearrange("p (o k c t) -> p o k c t", o=3, k=3, c=2)
        pf = PARTS[:].bitcast(F32)
        OS = pf[:, 0:S]
        T2, CTX = (pf[:, S + i * NT * D:S + (i + 1) * NT * D].rearrange("p (t d) -> p t d", t=NT)
                   for i in range(2))
        AQ = sb("AQ", [P, H, S], BF16)
        AK = sb("AK", [P, H, S], BF16)
        CL = sb("CL", [P, H, S], BF16)
        CR = sb("CR", [P, H, S], BF16)
        XS = AQ[:].rearrange("p h s -> p (h s)").bitcast(F32)[:, 0:H * XL].rearrange("p (h x) -> p h x", h=H)
        DWH = [w[:].rearrange("p h s -> p (h s)").bitcast(F32).rearrange("p (r t x) -> p r t x", r=4, t=NT)
               for w in (AQ, AK)]
        window = lambda h: DWH[(h % 8) // 4][:, h % 4]
        HT = AQ[:].rearrange("p h s -> p (h s)").bitcast(F32).rearrange("p (m s) -> p m s", m=NM)
        VP = sb("VP", [P, NT, H, 2 * DH], F32)
        E = sb("E", [P, 8, S], F32)
        exp_tile = lambda unit: E[:, (unit + 6) % 8, :]
        Fc, Fk, Fq, SQ = E[0:FC, 0:2, :], E[0:FC, 2:5:2, :], E[0:FC, 3:6:2, :], E[0:FC, 6:8, :]
        REM = sb("REM", [FC, 2, S], F32)
        MX = sb("MX", [P, 2, H * NT], F32)
        NMX = sb("NMX", [P, G * NT], F32)
        NMR = sb("NMR", [P, G * NT], F32)
        NMP = sb("NMP", [P, 3, G * NT], BF16)
        MT = sb("MT", [G * NT, 3, P], BF16)
        RZ = sb("RZ", [P, 3, G], F32)
        TP = sb("TP", [P, 3, G, DH], F32)
        ST = sb("ST", [P, NT, 6], F32)
        MV = sb("MV", [P, NT, 2], F32)
        SD = sb("SD", [P, NT], F32)
        Wqkcv = sb("Wqkcv", [FC, 2, 4 * D], F32)
        Wo = sb("Wo", [FC, 2, D], F32)
        Wi = sb("Wi", [FC, 2, FF], F32)
        Wo2 = sb("Wo2", [P, NM, D], F32)
        bcol = sb("bcol", [FC, 3, 2], F32)
        bicol = sb("bicol", [P, NM], F32)
        MT1 = REM[0:G * NT].rearrange("p c t -> p (c t)").bitcast(BF16)[:, 0:3 * S].rearrange(
            "p (k t) -> p k t", k=3)
        brow = sb("brow", [P, 7, D], F32)
        W1T = sb("W1T", [FC, 2, P], F32)
        W2T = sb("W2T", [P, D], F32)
        WoT = sb("WoT", [FC, 2, D], F32)
        WqkvT = sb("WqkvT", [FC, 2, 3 * D], F32)
        WoutT = sb("WoutT", [FC, 2, D], F32)
        Wg = sb("Wg", [FC, 2, E_], F32)
        EMB = sb("EMB", [FC, 6 * NREL], F32)
        fcol = sb("fcol", [P, 1], F32)
        f2col = sb("f2col", [FC, 2], F32)
        qkcol = sb("qkcol", [FC, 2, 2], F32)
        frow = sb("frow", [P, 5, D], F32)
        LGT = sb("LGT", [P, NT, E_], F32)
        RB = sb("RB", [P, NT, H, 2], F32)
        BS = sb("BS", [P, NT, H, NT], F32)
        MX6 = sb("MX6", [P, NT, H, NT], F32)
        VVP = sb("VVP", [P, 3, NT, G * NT], BF16)
        BM = sb("BM", [P, NT, G, NT], F32)
        M1 = sb("M1", [P, NT, G], F32)
        idf = sb("idf", [P, P], F32)
        idb = sb("idb", [P, P], BF16)
        negI = sb("negI", [P, P], BF16)
        blk = sb("blk", [FC, FC], F32)

        PS = ctx.enter_context(nc.psum_tensor("PS", [P, 8, BANK], F32))
        flat = lambda b0, n: PS[:, b0, 0:n]

        w_once, w_first, w_rest = sem("w_once"), sem("w_first"), sem("w_rest")
        const_ready, h_in, h_out = sem("const_ready"), sem("h_in"), sem("h_out")
        onehot_in = sem("onehot_in")
        const_in = sem("const_in")
        x_ready = sem("x_ready")
        XPER = 3 * (1 + L)
        NW_FIRST, NW_REST = 3, 5
        onehot_ready = sem("onehot_ready")
        OHF = E[0:RROWS, 0, :]
        OHB = PARTS[0:RROWS, 0:S]
        once = [(idf[:], a["ident"]), (blk[:], a["headblk"]), (W1T[:], a["W1T"]), (W2T[:], a["W2T"]),
                (WoT[:], a["WoT"]), (WqkvT[:], a["WqkvT"]), (WoutT[:], a["WoutT"]), (Wg[:], a["Wg"]),
                (EMB[:], a["relbd"]), (fcol[:], a["fcol"]), (f2col[:], a["f2col"]), (qkcol[:], a["qkcol"]),
                (frow[:], a["frow"].partition_broadcast(P)), (OHF, a["onehot"])]
        NW_ONCE = len(once)
        lay = Counts(nc, ctx, "l_", dict(
            tr_ps=6, tr_dve=3, tr_act=3, v_ps=3, v_dve=3, f_ps=6, f_act=6, sq_act=2, n_ps=2, n_act=4,
            p_dve=6, sc_ps=144, e_act=144, av_ps=36, osb=6, m_ps=144 + 12 + NG, m_free=144 + 12 + NG,
            mt_dve=NG, ctx_ready=1, y_ps=3, a1_ready=3, **{f"pd_w{i}": 16 for i in range(6)},
            **{f"c_in{g}": 2 * 16 * NRUN for g in range(NG)}, **{f"qk_in{g}": 2 * 16 * NRUN for g in range(NG)},
            **{f"md_w{g}": 16 for g in range(NG)}, **{f"md_r{g}": 16 for g in range(NG)},
            ln_var=6, ln_sd=6, f1_ps=12, g_act=12, y2_ps=3, dve_step=LSTEP))
        tail = Counts(nc, ctx, "t_", dict(
            a_ready=9, tr_ps=8, tr_dve=4, tr_act=4, ln_var=15, ln_sd=15, f0_ps=1, relu=1, pr_ps=2, pr_act=2,
            yo_ps=3, v_ps=3, v_dve=3, f_ps=4, f_act=4, p_dve=4, **{f"pd_w{i}": 16 for i in range(4)},
            **{f"qk_in{g}": 2 * 16 * NRUN for g in range(NG)}, rr_ps=6, rr_dve=6, xs=6, xs_w=96, dw_fix=H,
            sc_ps=72, e_act=72, av_ps=18, osb=3, m_ps=144 + 3 * NG + 6, m_free=144 + 3 * NG + 6, mt_dve=3 * NG,
            yo2_ps=3, lg_ps=1, out_ready=1, dve_step=TSTEP,
            **{f"dw_in{r}": 16 * (2 if r < 4 else 1) for r in range(8)},
            **{f"md_w{g}": 16 for g in range(NG)}, **{f"md_r{g}": 48 for g in range(NG)}))

        def transposes(v, src, pair_ready=None):
            for pair in range(3):
                if pair_ready is not None:
                    pair_ready(pair)
                for c in range(2):
                    for t in range(2 * pair, 2 * pair + 2):
                        last = v.eng.transpose(PS[0:FC, 2 * c + t // 4, (t % 4) * P:(t % 4) * P + P],
                                               src[:, t, c * FC:(c + 1) * FC], idf[:])
                    if pair == 2:
                        v.inc(last, "tr_ps")

        def tr_view(c):
            return PS[0:FC, 2 * c:2 * c + 2, :].rearrange("p a b -> p (a b)")[:, 0:S]

        def take_transposed(v, use, c, act):
            v.wait("tr_ps", 2 * use + c + 1)
            if act:
                v.inc(v.eng.activation(XT[:, c, :], tr_view(c), ACT.Copy), "tr_act")
            else:
                v.inc(v.eng.tensor_copy(XT[:, c, :], tr_view(c)), "tr_dve")

        def token_product(v, bank, weights, ncols, sig):
            for t in range(NT):
                for c in range(2):
                    last = v.eng.matmul(PS[:, bank + t // 2, (t % 2) * 256:(t % 2) * 256 + ncols],
                                        XT[:, c, t * P:(t + 1) * P], weights[:, c, :],
                                        start=(c == 0), stop=(c == 1))
                if t % 2:
                    v.inc(last, sig)

        def feature_product(v, bank, weights, sig, m):
            for h in range(2):
                for c in range(2):
                    last = v.eng.matmul(PS[0:FC, bank + 2 * m + h, 0:HALF],
                                        weights[:, c, m * FC:(m + 1) * FC],
                                        XT[:, c, h * HALF:(h + 1) * HALF], start=(c == 0), stop=(c == 1))
            v.inc(last, sig)

        def chunk_view(bank, m):
            return PS[0:FC, bank + 2 * m:bank + 2 * m + 2, 0:HALF]

        def halves(ap):
            return ap.rearrange("p (h t) -> p h t", h=2)

        def token_view(bank, pair):
            return PS[:, bank + pair, :].rearrange("p (t x) -> p t x", t=2)[:, :, 0:D]

        def row_bc(row, n):
            return row.unsqueeze(1).broadcast_to([P, n, D])

        def layer_norm(v, source, src, dst, eps, n, done, gain=None, shift=None):
            dve = v.eng
            for pair in range(4):
                if pair < 3:
                    ts = slice(2 * pair, 2 * pair + 2)
                    if source is not None:
                        v.link(source(pair))
                    for t in range(2 * pair, 2 * pair + 2):
                        ins = dve.bn_stats(ST[:, t, :], src[:, t, :])
                    v.link(ins)
                    dve.tensor_tensor(MV[:, ts, 0], ST[:, ts, 1], ST[:, ts, 4], ALU.add)
                    dve.tensor_tensor(MV[:, ts, 1], ST[:, ts, 1], ST[:, ts, 4], ALU.subtract)
                    v.link(dve.tensor_tensor(SD[:, ts], ST[:, ts, 2], ST[:, ts, 5], ALU.add))
                    dve.tensor_scalar(MV[:, ts, 0], MV[:, ts, 0], 0.5, None, ALU.mult)
                    v.link(dve.tensor_tensor(MV[:, ts, 1], MV[:, ts, 1], MV[:, ts, 1], ALU.mult))
                    v.link(dve.scalar_tensor_tensor(out=SD[:, ts], in0=MV[:, ts, 1], scalar=D / 4.0, in1=SD[:, ts],
                                                    op0=ALU.mult, op1=ALU.add))
                    v.inc(dve.tensor_scalar(SD[:, ts], SD[:, ts], 1.0 / D, eps, ALU.mult, ALU.add), "ln_var")
                if pair:
                    ts = slice(2 * pair - 2, 2 * pair)
                    v.wait("ln_sd", 3 * (n - 1) + pair)
                    v.link(dve.reciprocal(SD[:, ts], SD[:, ts]))
                    for t in range(2 * pair - 2, 2 * pair):
                        if gain is None:
                            ins = dve.tensor_scalar(dst[:, t, :], src[:, t, :], MV[:, t, 0:1], SD[:, t:t + 1],
                                                    ALU.subtract, ALU.mult)
                        else:
                            ins = dve.scalar_tensor_tensor(out=dst[:, t, :], in0=src[:, t, :], scalar=MV[:, t, 0:1],
                                                           in1=gain, op0=ALU.subtract, op1=ALU.mult)
                    if gain is not None:
                        v.link(ins)
                        for t in range(2 * pair - 2, 2 * pair):
                            ins = dve.scalar_tensor_tensor(out=dst[:, t, :], in0=dst[:, t, :], scalar=SD[:, t:t + 1],
                                                           in1=shift, op0=ALU.mult, op1=ALU.add)
                    done(ins)

        def norm_sd(v, n):
            for pair in range(3):
                ts = slice(2 * pair, 2 * pair + 2)
                v.wait("ln_var", 3 * (n - 1) + pair + 1)
                v.inc(v.eng.activation(SD[:, ts], SD[:, ts], ACT.Sqrt), "ln_sd")

        def split(v, f, o, m, sig):
            f = f[:, m, :]
            rem = REM[:, m, :]
            v.link(v.eng.tensor_copy(parts[:, o, 0, m], f))
            v.link(v.eng.tensor_tensor(rem, f, parts[:, o, 0, m], ALU.subtract))
            v.link(v.eng.tensor_copy(parts[:, o, 1, m], rem))
            v.inc(v.eng.tensor_tensor(parts[:, o, 2, m], rem, parts[:, o, 1, m], ALU.subtract), sig)

        def pe_scores(v, keys, queries, rows, unit, h, kt, cosine, rel):
            if unit >= 2:
                v.wait("e_act", unit - 1)
            slot = 2 * (unit % 2)
            for c0, nc_ in ((0, BANK), (BANK, S - BANK)):
                last = v.eng.matmul(PS[:, slot + c0 // BANK, 0:nc_], keys[0:rows, h, kt * P:(kt + 1) * P],
                                    queries[0:rows, h, c0:c0 + nc_], start=True, stop=True)
            if cosine:
                last = v.eng.matmul(PS[:, slot + kt // 4, (kt % 4) * P:(kt % 4) * P + P], negI[:], idb[:],
                                    start=False, stop=True, skip_group_check=True)
            if rel:
                last = rel_window(v, window(h), kt, slot)
            v.inc(last, "sc_ps")

        def rel_window(v, DW, kt, slot):
            for qt in (kt - 1, kt, kt + 1):
                if not 0 <= qt < NT:
                    continue
                col = PS[:, slot + qt // 4, (qt % 4) * P:(qt % 4) * P + P]
                if qt == kt:
                    ins = v.eng.matmul(col, DW[:, qt, 32:32 + P], idf[:], start=False, stop=True,
                                       skip_group_check=True)
                elif qt > kt:
                    ins = v.eng.matmul(col[96:128], DW[:, qt, 0:32], idf[:], start=False, stop=True,
                                       skip_group_check=True)
                else:
                    ins = v.eng.matmul(col[0:32], DW[:, qt, 160:192], idf[:], start=False, stop=True,
                                       skip_group_check=True)
            return ins

        def pe_av(v, n, g, kt, half):
            if half == 0:
                v.wait("e_act", 4 * n + 4)
                if kt == 0 and n >= NT:
                    v.wait("osb", n // NT)
            for j in range(G):
                last = v.eng.matmul(PS[32 * j:32 * j + 32, 4 + half, 0:HALF], VP[:, kt, g * G + j, :],
                                    exp_tile(4 * n + j)[:, half * HALF:(half + 1) * HALF],
                                    start=(kt == 0), stop=(kt == NT - 1))
            if half:
                v.inc(last, "av_ps")

        def pe_norm(v, run, half, ring):
            v.wait("osb", run + 1)
            v.wait("m_free", ring - 1)
            for t in range(3):
                last = v.eng.transpose(PS[:, 6 + ring % 2, t * P:(t + 1) * P],
                                       OS[:, (3 * half + t) * P:(3 * half + t + 1) * P], idf[:])
            v.inc(last, "m_ps")

        def act_exp(v, unit, scale, bias):
            v.wait("sc_ps", unit + 1)
            if unit >= 8:
                v.wait("av_ps", unit // 4 - 1)
            src = PS[:, 2 * (unit % 2):2 * (unit % 2) + 2, :].rearrange("p a b -> p (a b)")[:, 0:S]
            v.inc(v.eng.activation(exp_tile(unit), src, ACT.Exp, bias=bias, scale=scale), "e_act")

        def dve_evac(v, group):
            v.wait("av_ps", NT * (group + 1))
            v.inc(v.eng.tensor_copy(halves(OS), PS[:, 4:6, 0:HALF]), "osb")

        def dve_norm(v, g, half, ring, add, twice, last=False):
            v.wait("m_ps", ring + 1)
            v.wait("m_free", ring)
            o = PS[:, 6 + ring % 2, 0:3 * P].rearrange("p (t h x) -> p t h x", t=3, h=G)
            v.link(v.eng.reciprocal(RZ[:], o[:, :, :, DH]))
            if twice:
                v.link(v.eng.tensor_scalar(RZ[:], RZ[:], 2.0, None, ALU.mult))
            dst = CTX[:, 3 * half:3 * half + 3, g * G * DH:(g + 1) * G * DH].rearrange("p t (h x) -> p t h x", h=G)
            rz = RZ[:].unsqueeze(3).broadcast_to([P, 3, G, DH])
            ins = v.eng.tensor_tensor(TP[:] if add else dst, o[:, :, :, 0:DH], rz, ALU.mult)
            v.inc(ins, "m_free")
            if add:
                v.wait("m_free", ring + 1)
                ins = v.eng.tensor_tensor(dst, dst, TP[:], ALU.add)
                if last:
                    v.inc(ins, "ctx_ready")
                else:
                    v.link(ins)

        def pe_max(v, queries, keys, i, ring, rel):
            h, qt, half = i // (2 * NT), i // 2 % NT, i % 2
            if ring >= 2:
                v.wait("m_free", ring - 1)
            out = PS[:, 6 + ring % 2, 0:HALF]
            last = v.eng.matmul(out, queries[0:CORE, h, qt * P:(qt + 1) * P],
                                keys[0:CORE, h, half * HALF:(half + 1) * HALF], start=True, stop=True)
            if rel is not None:
                k0 = max(qt * P - 32, half * HALF)
                k1 = min(qt * P - 32 + WIN, (half + 1) * HALF)
                if k1 > k0:
                    x0 = k0 - (qt * P - 32)
                    last = v.eng.matmul(out[:, k0 - half * HALF:k1 - half * HALF], idf[:],
                                        rel[:, qt, x0:x0 + k1 - k0], start=False, stop=True,
                                        skip_group_check=True)
            v.inc(last, "m_ps")

        def dve_values(v, bank, bias):
            for pair in range(3):
                v.wait("v_ps", pair + 1)
                o = VP[:, 2 * pair:2 * pair + 2, :, 0:DH]
                i0 = token_view(bank, pair).rearrange("p t (h x) -> p t h x", h=H)
                i1 = row_bc(bias, 2).rearrange("p t (h x) -> p t h x", h=H)
                v.inc(v.eng.tensor_tensor(o, i0, i1, ALU.add), "v_dve")

        def product(v, sig, bank, other, dst):
            def source(pair):
                v.wait(sig, pair + 1)
                ts = slice(2 * pair, 2 * pair + 2)
                return v.eng.tensor_tensor(dst[:, ts, :], token_view(bank, pair), other(ts), ALU.add)
            return source

        def fix_window(v, h):
            w = window(h)
            v.wait(f"dw_in{h % 8}", 16 * (h // 8 + 1))
            dve = v.eng
            dve.tensor_tensor(w[:, 1:NT, 0:32], w[:, 1:NT, 0:32],
                              RB[:, 1:NT, h, 0:1].broadcast_to([P, NT - 1, 32]), ALU.subtract)
            v.inc(dve.tensor_tensor(w[:, 0:NT - 1, 160:192], w[:, 0:NT - 1, 160:192],
                                    RB[:, 0:NT - 1, h, 1:2].broadcast_to([P, NT - 1, 32]), ALU.subtract), "dw_fix")

        def pe_attention(v, order, relative):
            operands = {COS: (CL, CR, CORE), DOT: (CL, CR, CORE + RROWS) if relative else (AK, AQ, CORE + MROWS)}
            for event, *x in order:
                if event == "unit":
                    n, kind, g, kt, j = x
                    if kt == 0 and j == 0:
                        if kind == COS:
                            v.wait(f"c_in{g}", 2 * 16 * NRUN)
                        else:
                            v.wait(f"md_r{g}", 48 if relative else 16)
                    keys, queries, rows = operands[kind]
                    pe_scores(v, keys, queries, rows, 4 * n + j, g * G + j, kt, kind == COS, relative)
                elif event == "max":
                    i, ring = x
                    if i % (2 * G * NT) == 0:
                        v.wait(f"qk_in{i // (2 * G * NT)}", 2 * 16 * NRUN)
                    if relative:
                        h = i // (2 * NT)
                        if i % (2 * NT) == 0:
                            v.wait("dw_fix", h + 1)
                        pe_max(v, CR, CL, i, ring, window(h))
                    else:
                        pe_max(v, AQ, AK, i, ring, None)
                elif event == "bias":
                    g, k, ring = x
                    v.wait("m_free", ring - 1)
                    if relative:
                        v.wait("mt_dve", 3 * g + k + 1)
                        for t in range(NT):
                            last = v.eng.transpose(
                                PS[0:G * NT, 6 + ring % 2, 0:384].bitcast(BF16)[:, t * P:(t + 1) * P],
                                VVP[:, k, t, :], idb[:])
                    else:
                        v.wait("mt_dve", g + 1)
                        for k in range(3):
                            last = v.eng.transpose(
                                PS[0:G * NT, 6 + ring % 2, 0:192].bitcast(BF16)[:, k * P:(k + 1) * P],
                                NMP[:, k, :], idb[:])
                    v.inc(last, "m_ps")
                elif event == "av":
                    n, kind, g, kt, half = x
                    pe_av(v, n, g, kt, half)
                elif event == "norm":
                    run, kind, g, half, ring = x
                    pe_norm(v, run, half, ring)

        def act_attention(v, order, relative):
            for event, *x in order:
                if event == "unit":
                    n, kind, g, kt, j = x
                    unit = 4 * n + j
                    if unit < 8:
                        v.wait("p_dve", 4 if relative else (1, 2, 2, 2, 3, 4, 5, 6)[unit])
                    scale, bias = (-1.0, 1.0) if kind == COS else (0.25, 0.0)
                    act_exp(v, unit, scale, bias)

        def negate_maxima(v, g):
            dve = v.eng
            cols = slice(g * G * NT, (g + 1) * G * NT)
            v.link(dve.tensor_tensor(NMX[:], MX[:, 0, cols], MX[:, 1, cols], ALU.max))
            v.link(dve.tensor_scalar(NMX[:], NMX[:], -1.0, None, ALU.mult))
            v.link(dve.tensor_copy(NMP[:, 0], NMX[:]))
            v.link(dve.tensor_tensor(NMR[:], NMX[:], NMP[:, 0], ALU.subtract))
            v.link(dve.tensor_copy(NMP[:, 1], NMR[:]))
            v.inc(dve.tensor_tensor(NMP[:, 2], NMR[:], NMP[:, 1], ALU.subtract), "mt_dve")

        def relative_minus_maxima(v, g):
            dve = v.eng
            hs = slice(g * G, (g + 1) * G)
            v.link(dve.tensor_tensor(MX6[:, :, hs], MX6[:, :, hs], BS[:, :, hs], ALU.add))
            v.link(dve.tensor_reduce(M1[:], MX6[:, :, hs], AX.X, ALU.max))
            v.link(dve.tensor_tensor(BM[:], BS[:, :, hs], M1[:].unsqueeze(3).broadcast_to([P, NT, G, NT]),
                                     ALU.subtract))
            bm = BM[:].rearrange("p t h k -> p t (h k)")
            for k in range(3):
                v.inc(dve.tensor_copy(VVP[:, k], bm), "mt_dve")
                if k < 2:
                    v.wait("mt_dve", 3 * g + k + 1)
                    v.link(dve.tensor_tensor(bm, bm, VVP[:, k], ALU.subtract))

        def dve_attention(v, order, relative):
            runs = max(x[0] for event, *x in order if event == "evac") + 1
            for event, *x in order:
                if event == "max":
                    i, ring = x
                    h, qt, half = i // (2 * NT), i // 2 % NT, i % 2
                    v.wait("m_ps", ring + 1)
                    src = PS[:, 6 + ring % 2, 0:HALF]
                    if relative:
                        v.inc(v.eng.tensor_reduce(MX6[:, qt, h, 3 * half:3 * half + 3],
                                                  src.rearrange("p (t s) -> p t s", t=3), AX.X, ALU.max), "m_free")
                    else:
                        v.inc(v.eng.tensor_reduce(MX[:, half, h * NT + qt:h * NT + qt + 1], src, AX.X, ALU.max),
                              "m_free")
                    last_max = ring
                elif event == "negmax":
                    g, = x
                    v.wait("m_free", last_max + 1)
                    if g:
                        v.wait("m_ps", bias_ring + 1)
                    (relative_minus_maxima if relative else negate_maxima)(v, g)
                elif event == "bias":
                    g, k, ring = x
                    v.wait("m_ps", ring + 1)
                    if g:
                        v.wait(f"md_w{g - 1}", 16)
                    if relative:
                        ins = v.eng.tensor_copy(MT1[:, k, :], PS[0:G * NT, 6 + ring % 2, 0:384].bitcast(BF16))
                    else:
                        ins = v.eng.tensor_copy(MT[:], PS[0:G * NT, 6 + ring % 2, 0:192].bitcast(BF16).rearrange(
                            "p (k t) -> p k t", k=3))
                    v.inc(ins, "m_free")
                    bias_ring = ring
                elif event == "evac":
                    if x[0] == 0:
                        for n in range(4 if relative else 6):
                            v.wait(f"pd_w{n}", 16)
                    dve_evac(v, x[0])
                    if relative and x[0] == 0:
                        for h in range(8, H):
                            fix_window(v, h)
                elif event == "norm":
                    run, kind, g, half, ring = x
                    dve_norm(v, g, half, ring, kind == DOT and not relative, relative,
                             run == runs - 1 and half == 1)

        def ring_of(order, event, g):
            return max(x[-1] for e, *x in order if e == event and x[0] == g) + 1

        with nc.Block() as block:
            @block.tensor
            def _(pe):
                pe.wait_ge(const_ready, 1)
                pe.wait_ge(w_once, 16 * NW_ONCE)
                with pe.Fori(0, B) as b:
                    with pe.Fori(0, L) as l:
                        p = b * L + l
                        v = lay.on(pe, p)
                        transposes(v, X, lambda pair: pe.wait_ge(x_ready, b * XPER + l * 3 + pair + 1))
                        pe.wait_ge(w_first, p * (16 * NW_FIRST) + 16 * NW_FIRST)
                        v.wait("tr_dve", 1)
                        v.wait("tr_act", 1)
                        feature_product(v, 0, Wqkcv[:, :, 2 * D:3 * D], "f_ps", 0)
                        feature_product(v, 0, Wqkcv[:, :, 2 * D:3 * D], "f_ps", 1)
                        for m in range(2):
                            v.wait("sq_act", m + 1)
                            v.wait("f_act", m + 1)
                            for h in range(2):
                                last = pe.matmul(PS[0:FC, 2 * m + h, 0:HALF], blk[:],
                                                 halves(SQ[:, m, :])[:, h, :], start=True, stop=True)
                            v.inc(last, "n_ps")
                            feature_product(v, 4, Wqkcv[:, :, D:2 * D], "f_ps", m)
                        for m in range(2):
                            v.wait("f_act", 2 + m + 1)
                            feature_product(v, 4, Wqkcv[:, :, 0:D], "f_ps", m)
                        v.wait("n_act", 2)
                        token_product(v, 0, Wqkcv[:, :, 3 * D:4 * D], D, "v_ps")
                        v.wait("f_act", 6)
                        v.wait("v_dve", 3)
                        pe_attention(v, LAYER_ORDER, False)
                        v.wait("ctx_ready", 1)
                        transposes(v, CTX)
                        pe.wait_ge(w_rest, p * (16 * NW_REST) + 16 * NW_REST)
                        v.wait("tr_dve", 2)
                        v.wait("tr_act", 2)
                        token_product(v, 4, Wo, D, "y_ps")
                        transposes(v, A1, lambda pair: v.wait("a1_ready", pair + 1))
                        v.wait("tr_dve", 3)
                        v.wait("tr_act", 3)
                        for f in range(2 * NM):
                            m, h = divmod(f, 2)
                            if f >= 4:
                                v.wait("g_act", f - 3)
                            for c in range(2):
                                last = pe.matmul(PS[:, 4 + f % 4, 0:HALF], Wi[:, c, m * P:(m + 1) * P],
                                                 XT[:, c, h * HALF:(h + 1) * HALF], start=(c == 0), stop=(c == 1))
                            v.inc(last, "f1_ps")
                        for t in range(NT):
                            v.wait("g_act", 2 * NM)
                            for m in range(NM):
                                last = pe.matmul(PS[:, 4 + t // 2, (t % 2) * 256:(t % 2) * 256 + D],
                                                 HT[:, m, t * P:(t + 1) * P], Wo2[:, m, :],
                                                 start=(m == 0), stop=(m == NM - 1))
                            if t % 2:
                                v.inc(last, "y2_ps")
                    v = tail.on(pe, b)
                    transposes(v, A1, lambda pair: v.wait("a_ready", pair + 1))
                    v.wait("tr_dve", 1)
                    v.wait("tr_act", 1)
                    for h in range(2):
                        for c in range(2):
                            last = pe.matmul(PS[:, 4 + h, 0:HALF], W1T[:, c, :], XT[:, c, h * HALF:(h + 1) * HALF],
                                             start=(c == 0), stop=(c == 1))
                    v.inc(last, "f0_ps")
                    v.wait("relu", 1)
                    for m in range(2):
                        for h in range(2):
                            last = pe.matmul(PS[0:FC, 2 * m + h, 0:HALF], W2T[:, m * FC:(m + 1) * FC],
                                             E[:, 0, h * HALF:(h + 1) * HALF], start=True, stop=True)
                        v.inc(last, "pr_ps")
                    v.wait("pr_act", 2)
                    for t in range(NT):
                        for c in range(2):
                            last = pe.matmul(PS[:, 4 + t // 2, (t % 2) * 256:(t % 2) * 256 + D],
                                             Fk[:, c, t * P:(t + 1) * P], WoT[:, c, :], start=(c == 0), stop=(c == 1))
                        if t % 2:
                            v.inc(last, "yo_ps")
                    transposes(v, A1, lambda pair: v.wait("a_ready", 3 + pair + 1))
                    v.wait("tr_dve", 2)
                    v.wait("tr_act", 2)
                    token_product(v, 4, WqkvT[:, :, 2 * D:3 * D], D, "v_ps")
                    for m in range(2):
                        feature_product(v, 0, WqkvT[:, :, 0:D], "f_ps", m)
                    v.wait("v_dve", 3)
                    for m in range(2):
                        feature_product(v, 4, WqkvT[:, :, D:2 * D], "f_ps", m)
                    v.wait("f_act", 2)
                    for t in range(NT):
                        if t >= 4:
                            v.wait("rr_dve", t - 3)
                        for c in range(2):
                            last = pe.matmul(PS[:, t % 4, c * 256:c * 256 + 6 * NREL], Fq[:, c, t * P:(t + 1) * P],
                                             EMB[:], start=True, stop=True)
                        v.inc(last, "rr_ps")
                    v.wait("f_act", 4)
                    v.wait("rr_dve", NT)
                    pe_attention(v, TAIL_ORDER, True)
                    v.wait("m_free", ring_of(TAIL_ORDER, "norm", NG - 1))
                    transposes(v, CTX)
                    v.wait("tr_dve", 3)
                    v.wait("tr_act", 3)
                    token_product(v, 4, WoutT, D, "yo2_ps")
                    transposes(v, A1, lambda pair: v.wait("a_ready", 6 + pair + 1))
                    v.wait("tr_dve", 4)
                    v.wait("tr_act", 4)
                    for t in range(NT):
                        for c in range(2):
                            last = pe.matmul(PS[:, 7, t * E_:(t + 1) * E_], XT[:, c, t * P:(t + 1) * P], Wg[:, c, :],
                                             start=(c == 0), stop=(c == 1))
                    v.inc(last, "lg_ps")

            @block.scalar
            def _(act):
                def first(l):
                    act.dma_start(Wqkcv[:], a["Wqkcv"][l]).then_inc(w_first, 16)
                    act.dma_start(bcol[:], a["bcol"][l]).then_inc(w_first, 16)
                    act.dma_start(brow[:, 0], a["brow"][l, 0].partition_broadcast(P)).then_inc(w_first, 16)

                def rest(l):
                    act.dma_start(Wo[:], a["Wo"][l]).then_inc(w_rest, 16)
                    act.dma_start(Wi[:], a["Wi"][l]).then_inc(w_rest, 16)
                    act.dma_start(Wo2[:], a["Wo2"][l]).then_inc(w_rest, 16)
                    act.dma_start(bicol[:], a["bicol"][l]).then_inc(w_rest, 16)
                    act.dma_start(brow[:, 1:7], a["brow"][l, 1:7].partition_broadcast(P)).then_inc(w_rest, 16)

                act.dma_start(HR[:], H0[0]).then_inc(h_in, 16)
                first(0)
                rest(0)
                act.wait_ge(w_once, 16 * NW_ONCE)
                with act.Fori(0, B) as b:
                    tv = tail.on(act, b)
                    norm_sd(tv, 1)
                    with act.Fori(0, L) as l:
                        p = b * L + l
                        v = lay.on(act, p)
                        take_transposed(v, 0, 1, True)
                        act.wait_ge(w_first, p * (16 * NW_FIRST) + 16 * NW_FIRST)
                        for o, f in ((0, Fc), (1, Fk), (2, Fq)):
                            if o == 1:
                                for m in range(2):
                                    v.wait("n_ps", m + 1)
                                    v.inc(act.activation(halves(SQ[:, m, :]), chunk_view(0, m), ACT.Ln), "n_act")
                                for m in range(2):
                                    v.wait("n_act", 2)
                                    v.inc(act.activation(SQ[:, m, :], SQ[:, m, :], ACT.Exp, scale=-0.5), "n_act")
                            for m in range(2):
                                v.wait("f_ps", 2 * o + m + 1)
                                if o == 0:
                                    v.inc(act.activation(halves(SQ[:, m, :]), chunk_view(0, m), ACT.Square,
                                                         bias=bcol[:, o, m:m + 1]), "sq_act")
                                v.inc(act.activation(halves(f[:, m, :]), chunk_view(4 if o else 0, m),
                                                     ACT.Identity, bias=bcol[:, o, m:m + 1]), "f_act")
                        v.wait("v_dve", 3)
                        v.wait("f_act", 6)
                        first(l + 1)
                        act_attention(v, LAYER_ORDER, False)
                        take_transposed(v, 1, 1, True)
                        norm_sd(v, 1)
                        take_transposed(v, 2, 1, True)
                        act.wait_ge(w_rest, p * (16 * NW_REST) + 16 * NW_REST)
                        for f in range(2 * NM):
                            m, h = divmod(f, 2)
                            v.wait("f1_ps", f + 1)
                            v.inc(act.activation(HT[:, m, h * HALF:(h + 1) * HALF], PS[:, 4 + f % 4, 0:HALF],
                                                 ACT.Gelu, bias=bicol[:, m:m + 1]), "g_act")
                        norm_sd(v, 2)
                        act.wait_ge(x_ready, b * XPER + l * 3 + 6)
                        rest(l + 1)
                    v = tv
                    norm_sd(v, 2)
                    take_transposed(v, 0, 1, True)
                    v.wait("f0_ps", 1)
                    v.inc(act.activation(halves(E[:, 0, :]), PS[:, 4:6, 0:HALF], ACT.Relu, bias=fcol[:]), "relu")
                    for m in range(2):
                        v.wait("pr_ps", m + 1)
                        v.inc(act.activation(halves(Fk[:, m, :]), chunk_view(0, m), ACT.Identity,
                                             bias=f2col[:, m:m + 1]), "pr_act")
                    norm_sd(v, 3)
                    norm_sd(v, 4)
                    take_transposed(v, 1, 1, True)
                    for o, f, bank in ((0, Fq, 0), (1, Fk, 4)):
                        for m in range(2):
                            v.wait("f_ps", 2 * o + m + 1)
                            v.inc(act.activation(halves(f[:, m, :]), chunk_view(bank, m), ACT.Identity,
                                                 bias=qkcol[:, o, m:m + 1]), "f_act")
                    act_attention(v, TAIL_ORDER, True)
                    take_transposed(v, 2, 1, True)
                    norm_sd(v, 5)
                    v.wait("a_ready", 9)
                    act.dma_start(H1[b], HR[:]).then_inc(h_out, 16)
                    act.dma_start(XF[b], A1[:]).then_inc(h_out, 16)
                    take_transposed(v, 3, 1, True)
                    v.wait("out_ready", 1)
                    act.dma_start(LG[b], LGT[:]).then_inc(h_out, 16)
                    act.wait_ge(h_out, b * 48 + 48)
                    act.dma_start(HR[:], H0[b + 1]).then_inc(h_in, 16)
                act.wait_ge(h_in, 16 * (B + 1))

            @block.vector
            def _(dve):
                dve.wait_ge(w_once, 16 * NW_ONCE)
                dve.tensor_copy(idb[:], idf[:])
                dve.memset(VP[:], 2.0)
                dve.memset(BS[:], 0.0)
                dve.tensor_copy(OHB, OHF).then_inc(onehot_ready, 1)
                dve.tensor_scalar(negI[:], idf[:], -1.0, None, ALU.mult).then_inc(const_ready, 1)
                dve.wait_ge(const_ready, 1)
                dve.wait_ge(onehot_in, 16 * H)
                with dve.Fori(0, B) as b:
                    tv = tail.on(dve, b)
                    dve.wait_ge(h_in, b * 16 + 16)
                    dve.memset(AK[96:96 + MROWS, :, :], 1.0)
                    layer_norm(tv, None, HR, X, 1e-5, 1, lambda ins: ins.then_inc(x_ready, 1))
                    with dve.Fori(0, L) as l:
                        p = b * L + l
                        v = lay.on(dve, p)
                        take_transposed(v, 0, 0, False)
                        dve.wait_ge(w_first, p * (16 * NW_FIRST) + 16 * NW_FIRST)
                        for o, f, m in ((0, Fc, 0), (0, Fc, 1), (1, Fk, 0), (2, Fq, 0), (1, Fk, 1), (2, Fq, 1)):
                            if o == 0:
                                v.wait("n_act", 2 + m + 1)
                                v.link(dve.tensor_tensor(Fc[:, m, :], Fc[:, m, :], SQ[:, m, :], ALU.mult))
                            else:
                                v.wait("f_act", 2 * o + m + 1)
                            split(v, f, o, m, "p_dve")
                            if (o, m) == (2, 0):
                                dve_values(v, 0, brow[:, 0])
                        v.wait("p_dve", 6)
                        dve.wait_ge(w_rest, p * (16 * NW_REST) + 16 * NW_REST)
                        v.link(dve.tensor_tensor(X[:], X[:], row_bc(brow[:, 1], NT), ALU.add))
                        dve_attention(v, LAYER_ORDER, False)
                        take_transposed(v, 1, 0, False)
                        layer_norm(v, product(v, "y_ps", 4, lambda ts: X[:, ts, :], T2), T2, A1, 1e-12, 1,
                                   lambda ins: v.inc(ins, "a1_ready"), brow[:, 2], brow[:, 3])
                        take_transposed(v, 2, 0, False)
                        v.wait("tr_ps", 6)
                        v.link(dve.tensor_tensor(A1[:], A1[:], row_bc(brow[:, 4], NT), ALU.add))
                        layer_norm(v, product(v, "y2_ps", 4, lambda ts: A1[:, ts, :], T2), T2, X, 1e-12, 2,
                                   lambda ins: ins.then_inc(x_ready, 1), brow[:, 5], brow[:, 6])
                        v.close()
                    v = tv
                    dve.wait_ge(x_ready, b * XPER + XPER)
                    v.link(dve.tensor_tensor(HR[:], HR[:], X[:], ALU.add))
                    layer_norm(v, None, HR, A1, 1e-5, 2, lambda ins: v.inc(ins, "a_ready"))
                    take_transposed(v, 0, 0, False)
                    layer_norm(v, product(v, "yo_ps", 4, lambda ts: row_bc(frow[:, 0], 2), T2), T2, X, 1e-5, 3,
                               v.link, frow[:, 1], frow[:, 2])
                    v.link(dve.tensor_tensor(HR[:], HR[:], X[:], ALU.add))
                    layer_norm(v, None, HR, A1, 1e-5, 4, lambda ins: v.inc(ins, "a_ready"))
                    take_transposed(v, 1, 0, False)
                    dve_values(v, 4, frow[:, 3])
                    for o, f in ((0, Fq), (1, Fk)):
                        for m in range(2):
                            v.wait("f_act", 2 * o + m + 1)
                            split(v, f, o, m, "p_dve")
                    for t in range(NT):
                        v.wait("rr_ps", t + 1)
                        if t:
                            v.wait("xs_w", 16 * t)
                        r = PS[:, t % 4, :].rearrange("p (c x) -> p c x", c=2)[:, :, 0:6 * NREL].rearrange(
                            "p c (h r) -> p c h r", h=6)
                        xs = XS.rearrange("p (c h) x -> p c h x", c=2)
                        rb = RB[:, t].rearrange("p (c h) r -> p c h r", c=2)
                        v.link(dve.tensor_copy(rb, r[:, :, :, 0:NREL:NREL - 1]))
                        v.inc(dve.tensor_copy(xs[:, :, :, FILL:FILL + NREL], r), "rr_dve")
                        dve.tensor_copy(XS[:, :, 0:FILL], RB[:, t, :, 0:1].broadcast_to([P, H, FILL]))
                        v.inc(dve.tensor_copy(XS[:, :, FILL + NREL:XL], RB[:, t, :, 1:2].broadcast_to([P, H, FILL])),
                              "xs")
                    for t in range(NT):
                        if t:
                            ins = dve.tensor_copy(BS[:, t, :, 0:t], RB[:, t, :, 0:1].broadcast_to([P, H, t]))
                        if t < NT - 1:
                            ins = dve.tensor_copy(BS[:, t, :, t + 1:NT],
                                                  RB[:, t, :, 1:2].broadcast_to([P, H, NT - 1 - t]))
                    v.link(ins)
                    for h in range(8):
                        fix_window(v, h)
                    v.link(dve.tensor_tensor(HR[:], HR[:], row_bc(frow[:, 4], NT), ALU.add))
                    dve_attention(v, TAIL_ORDER, True)
                    take_transposed(v, 2, 0, False)
                    layer_norm(v, product(v, "yo2_ps", 4, lambda ts: HR[:, ts, :], HR), HR, A1, 1e-5, 5,
                               lambda ins: v.inc(ins, "a_ready"))
                    take_transposed(v, 3, 0, False)
                    v.wait("lg_ps", 1)
                    v.inc(dve.tensor_copy(LGT[:], PS[:, 7, 0:NT * E_].rearrange("p (t e) -> p t e", t=NT)),
                          "out_ready")
                    v.close()

            @block.sync
            def _(sp):
                for dst, src in once:
                    sp.dma_start(dst, src).then_inc(w_once, 16)
                sp.wait_ge(onehot_ready, 1)
                for h in range(H):
                    sp.dma_start(CL[CORE:CORE + RROWS, h, :], OHB).then_inc(onehot_in, 16)
                sp.wait_ge(onehot_in, 16 * H)

                def spread(v, dst, o, part_of, sig, g):
                    hs = slice(g * G, (g + 1) * G)
                    for s_, k in enumerate(part_of):
                        v.inc(sp.dma_start(dst[s_ * DH:(s_ + 1) * DH, hs, :],
                                           PD[o, k].rearrange("(h d) t -> d h t", h=H)[:, hs, :]), sig, 16)

                def to_dram(v, o, m, n):
                    v.wait("p_dve", n + 1)
                    v.inc(sp.dma_start(PD[o].rearrange("k (c f) t -> f k c t", c=2)[:, :, m], parts[:, o, :, m]),
                          f"pd_w{n}", 16)

                with sp.Fori(0, B) as b:
                    with sp.Fori(0, L) as l:
                        v = lay.on(sp, b * L + l)

                        def cosine_operands(g):
                            spread(v, CL, 0, KEY_PARTS, f"c_in{g}", g)
                            spread(v, CR, 0, QRY_PARTS, f"c_in{g}", g)

                        def dot_operands(g):
                            spread(v, AK, 1, KEY_PARTS, f"qk_in{g}", g)
                            spread(v, AQ, 2, QRY_PARTS, f"qk_in{g}", g)

                        to_dram(v, 0, 0, 0)
                        to_dram(v, 0, 1, 1)
                        v.wait("pd_w0", 16)
                        cosine_operands(0)
                        to_dram(v, 1, 0, 2)
                        to_dram(v, 2, 0, 3)
                        v.wait("pd_w2", 16)
                        v.wait("pd_w3", 16)
                        dot_operands(0)
                        to_dram(v, 1, 1, 4)
                        to_dram(v, 2, 1, 5)
                        v.wait("pd_w1", 16)
                        cosine_operands(1)
                        v.wait("pd_w4", 16)
                        v.wait("pd_w5", 16)
                        dot_operands(1)
                        cosine_operands(2)
                        dot_operands(2)
                        for g in range(NG):
                            v.wait("m_free", ring_of(LAYER_ORDER, "bias", g))
                            v.inc(sp.dma_start(MD[:, g * G * NT:(g + 1) * G * NT].rearrange("k r t -> r k t"),
                                               MT[:]), f"md_w{g}", 16)
                            v.wait(f"md_w{g}", 16)
                            v.inc(sp.dma_start(
                                AQ[CORE:CORE + MROWS, g * G:(g + 1) * G, :].rearrange("k h s -> k (h s)"),
                                MD[:, g * G * NT:(g + 1) * G * NT].rearrange("k r t -> k (r t)")), f"md_r{g}", 16)
                    v = tail.on(sp, b)
                    for o in range(2):
                        for m in range(2):
                            to_dram(v, o, m, 2 * o + m)
                    for n in range(4):
                        v.wait(f"pd_w{n}", 16)
                    for g in range(NG):
                        spread(v, CR, 0, QRY_PARTS, f"qk_in{g}", g)
                        spread(v, CL, 1, KEY_PARTS, f"qk_in{g}", g)
                    for t in range(NT):
                        v.wait("xs", t + 1)
                        v.inc(sp.dma_start(XD[t * P:(t + 1) * P, :, :], XS), "xs_w", 16)
                    v.wait("xs_w", 16 * NT)
                    def windows(h):
                        w = window(h)
                        src = bass.AP(XD.tensor, h * XL + P - 1, [[H * XL - 1, P], [P * H * XL, NT], [1, WIN]])
                        v.inc(sp.dma_start(w, src), f"dw_in{h % 8}", 16)

                    for h in range(8):
                        windows(h)
                    for g in range(NG):
                        v.wait("m_free", ring_of(TAIL_ORDER, "bias", g))
                        v.inc(sp.dma_start(RD[:, g * G * NT:(g + 1) * G * NT].rearrange("k r t -> r k t"), MT1),
                              f"md_w{g}", 16)
                        v.wait(f"md_w{g}", 16)
                        for k in range(3):
                            v.inc(sp.dma_start(
                                CR[CORE + k * NT:CORE + (k + 1) * NT, g * G:(g + 1) * G, :],
                                RD[k, g * G * NT:(g + 1) * G * NT].rearrange("(h t) s -> t h s", h=G)), f"md_r{g}", 16)
                        if g == 0:
                            v.wait("sc_ps", 4 * NT)
                            for h in range(8, H):
                                windows(h)


def experts(nc, a, H1, XF, LG, XG, YD, out):
    with ExitStack() as ctx:
        sb = lambda n, s, d: ctx.enter_context(nc.sbuf_tensor(n, s, d))
        sem = lambda n: ctx.enter_context(nc.semaphore(n))
        T = B * NT
        lg = sb("lg", [P, T, E_], F32)
        xf = sb("xf", [P, T, D], F32)
        h1 = sb("h1", [P, T, D], F32)
        gy = sb("gy", [P, T, TOPK, D], F32)
        v8 = sb("v8", [P, T, 8], F32)
        i8 = sb("i8", [P, T, 8], U32)
        idx = sb("idx", [P, T, TOPK], F32)
        iota = sb("iota", [P, E_], F32)
        oh = sb("oh", [P, T, TOPK, E_], F32)
        ohb = sb("ohb", [P, T, TOPK, E_], BF16)
        trif = sb("trif", [P, P], F32)
        trib = sb("trib", [P, P], BF16)
        oneb = sb("oneb", [P, P], BF16)
        idm = sb("idm", [P, P], F32)
        tot = sb("tot", [P, T, TOPK * E_], F32)
        pre = [sb(f"pre{i}", [P, T, TOPK * E_], F32) for i in range(2)]
        pos = sb("pos", [P, T, TOPK], F32)
        keep = sb("keep", [P, T, TOPK], F32)
        slot = sb("slot", [P, T, TOPK], F32)
        koff = sb("koff", [P, TOPK], F32)
        sidf = sb("sidf", [P, T, TOPK], F32)
        sid = sb("sid", [P, T, TOPK], I32)
        gidf = sb("gidf", [P, T, TOPK], F32)
        gid = sb("gid", [P, T, TOPK], I32)
        dv = sb("dv", [P, T], F32)
        ew = sb("ew", [P, T], F32)
        den = sb("den", [P, T], F32)
        w = sb("w", [P, T, TOPK], F32)
        w1 = sb("w1", [FC, 2, 2, 2 * HID], F32)
        w2 = sb("w2", [P, 2, 4, D], F32)
        xg = sb("xg", [CP, 2, CC, D], F32)
        xgT = sb("xgT", [FC, 2, 2, CAP], F32)
        sg = sb("sg", [P, 2, CAP], F32)
        at = sb("at", [P, 2, 4, CAP], F32)
        ye = sb("ye", [CP, 2, CC, D], F32)
        PS = ctx.enter_context(nc.psum_tensor("PSX", [P, 8, BANK], F32))

        const_in, lg_in, xf_in, h1_in = sem("x_const_in"), sem("lg_in"), sem("xf_in"), sem("h1_in")
        oh_ready, pos_ps, dv_ready, ew_ready = sem("oh_ready"), sem("pos_ps"), sem("dv_ready"), sem("ew_ready")
        sid_ready, gid_ready, step = sem("sid_ready"), sem("gid_ready"), sem("x_step")
        scattered, gathered, done, stored = sem("scattered"), sem("gathered"), sem("x_done"), sem("x_stored")

        def passes(eng, body):
            body(ex.on(eng, 0), 0)
            with eng.Fori(1, E_ // 2) as i:
                body(ex.on(eng, i), i)

        U = 2 * TOPK
        ex = Counts(nc, ctx, "e_", dict(w_in0=32, w_in1=32, xg_in0=8 * U, xg_in1=8 * U, y_out0=8 * U, y_out1=8 * U, xt_ps=2 * U, xt_dve=U, xt_act=U, ug_ps=4 * U,
                                        silu=4 * U, at=4 * U, y_ps=2 * U, ye=2 * U))

        with nc.Block() as block:
            @block.sync
            def _(sp):
                sp.dma_start(lg[:].rearrange("p (b t) e -> p b (t e)", b=B),
                             LG.rearrange("b p t e -> p b (t e)")).then_inc(lg_in, 16)
                sp.dma_start(xf[:].rearrange("p (b t) d -> p b (t d)", b=B), XF.rearrange("b p t d -> p b (t d)")).then_inc(xf_in, 16)
                for dst, src in ((iota[:], a["iota"].partition_broadcast(P)), (koff[:], a["koff"].partition_broadcast(P)),
                                 (trif[:], a["tri"]), (idm[:], a["ident"])):
                    sp.dma_start(dst, src).then_inc(const_in, 16)
                sp.dma_start(h1[:].rearrange("p (b t) d -> p b (t d)", b=B), H1.rearrange("b p t d -> p b (t d)")).then_inc(h1_in, 16)
                sp.wait_ge(scattered, 16 * T * TOPK)

                def loads(v, i):
                    for u in range(U):
                        j, k = divmod(u, TOPK)
                        if k == 0:
                            v.wait("y_ps", 4 * j - 4)
                            sp.wait_ge(const_in, 64)
                            v.inc(sp.dma_start(w1[:, j], a["W1"][2 * i + j]), f"w_in{j}", 16)
                            v.inc(sp.dma_start(w2[:, j], a["W2"][2 * i + j]), f"w_in{j}", 16)
                        v.wait("xt_ps", 2 * u - 2)
                        sp.wait_ge(const_in, 64)
                        v.inc(sp.dma_start(xg[:, u % 2], XG[bass.ds((2 * i + (k * E_ + j)) * CAP, CAP), :]
                                           .rearrange("(p c) d -> p c d", c=CC)), f"xg_in{u % 2}", 16)

                passes(sp, loads)
                sp.wait_ge(done, 1)
                sp.dma_start(out.rearrange("b (t p) d -> p (b t) d", p=P), h1[:]).then_inc(stored, 16)
                sp.wait_ge(stored, 16)

            @block.gpsimd
            def _(pool):
                pool.wait_ge(xf_in, 16)
                pool.wait_ge(sid_ready, 1)
                for t in range(T):
                    for k in range(TOPK):
                        pool.indirect_dma_start(
                            out=XG, out_offset=bass.IndirectOffsetOnAxis(ap=sid[:, t, k:k + 1], axis=0),
                            in_=xf[:, t, :], in_offset=None, bounds_check=SLOTS - 1, oob_is_err=False
                        ).then_inc(scattered, 16)

                for r in range(2):
                    pool.wait_ge(ex.sem[f"y_out{r}"], (E_ // 2) * 8 * U)
                pool.wait_ge(gid_ready, 1)
                for t in range(T):
                    for k in range(TOPK):
                        pool.indirect_dma_start(
                            out=gy[:, t, k, :], out_offset=None, in_=YD,
                            in_offset=bass.IndirectOffsetOnAxis(ap=gid[:, t, k:k + 1], axis=0)
                        ).then_inc(gathered, 16)

            @block.scalar
            def _(act):
                act.wait_ge(dv_ready, 1)
                act.activation(ew[:], dv[:], ACT.Exp).then_inc(ew_ready, 1)

                def store(v, i, u):
                    j, k = divmod(u, TOPK)
                    v.wait("ye", 2 * u + 2)
                    v.inc(act.dma_start(YD[bass.ds((2 * i + (k * E_ + j)) * CAP, CAP), :]
                                        .rearrange("(p c) d -> p c d", c=CC), ye[:, u % 2]), f"y_out{u % 2}", 16)

                def silus(v, i):
                    for u in range(U):
                        v.wait("xt_ps", 2 * u + 2)
                        v.inc(act.activation(xgT[:, u % 2, 1, :], PS[0:FC, 1, 0:CAP], ACT.Copy), "xt_act")
                        for jj in range(4):
                            q = 4 * u + jj
                            v.wait("ug_ps", q + 1)
                            v.wait("at", q - 1)
                            v.inc(act.activation(sg[:, q % 2], PS[:, 3 + 2 * (q % 2), 0:CAP], ACT.Silu), "silu")
                            if u and jj == 1:
                                store(v, i, u - 1)
                    store(v, i, U - 1)

                passes(act, silus)

            @block.tensor
            def _(pe):
                pe.wait_ge(oh_ready, 1)
                ohm = ohb[:].rearrange("p t k e -> p (t k e)")
                pe.matmul(PS[:, 0, 0:T * TOPK * E_], trib[:], ohm, start=True, stop=True)
                pe.matmul(PS[:, 1, 0:T * TOPK * E_], oneb[:], ohm, start=True, stop=True).then_inc(pos_ps, 1)
                pe.wait_ge(sid_ready, 1)
                pe.wait_ge(const_in, 16 * 4)

                def blocks(v, i):
                    for u in range(U):
                        j, k = divmod(u, TOPK)
                        v.wait(f"xg_in{u % 2}", 16 * (u // 2 + 1))
                        v.wait("xt_dve", u)
                        v.wait("xt_act", u)
                        for c in range(2):
                            for cc in range(CC):
                                last = pe.transpose(PS[0:FC, c, cc * CP:(cc + 1) * CP],
                                                    xg[:, u % 2, cc, c * FC:(c + 1) * FC], idm[0:CP, 0:CP])
                            v.inc(last, "xt_ps")
                        v.wait(f"w_in{j}", 32)
                        v.wait("xt_dve", u + 1)
                        v.wait("xt_act", u + 1)
                        for jj in range(4):
                            q = 4 * u + jj
                            v.wait("at", q - 1)
                            for half in range(2):
                                for c in range(2):
                                    last = pe.matmul(PS[:, 2 + 2 * (q % 2) + half, 0:CAP],
                                                     w1[:, j, c, half * HID + jj * P:half * HID + (jj + 1) * P],
                                                     xgT[:, u % 2, c, :], start=(c == 0), stop=(c == 1))
                            v.inc(last, "ug_ps")
                        v.wait("at", 4 * u + 4)
                        v.wait("ye", 2 * u)
                        for cc in range(CC):
                            for jj in range(4):
                                last = pe.matmul(PS[0:CP, 6 + cc // 2, (cc % 2) * 256:(cc % 2) * 256 + D],
                                                 at[:, u % 2, jj, cc * CP:(cc + 1) * CP], w2[:, j, jj, :],
                                                 start=(jj == 0), stop=(jj == 3))
                            if cc % 2:
                                v.inc(last, "y_ps")

                passes(pe, blocks)

            @block.vector
            def _(dve):
                links = [0]

                def link(ins):
                    links[0] += 1
                    ins.then_inc(step, 1)
                    dve.wait_ge(step, links[0])

                dve.memset(oneb[:], 1.0)
                dve.wait_ge(lg_in, 16)
                dve.wait_ge(const_in, 16 * 4)
                link(dve.tensor_copy(trib[:], trif[:]))
                for t in range(T):
                    ins = dve.max(v8[:, t, :], lg[:, t, :])
                link(ins)
                for t in range(T):
                    ins = dve.max_index(i8[:, t, :], v8[:, t, :], lg[:, t, :])
                link(ins)
                dve.tensor_tensor(dv[:], v8[:, :, 1], v8[:, :, 0], ALU.subtract).then_inc(dv_ready, 1)
                link(dve.tensor_copy(idx[:], i8[:, :, 0:TOPK]))
                for k in range(TOPK):
                    ins = dve.tensor_tensor(oh[:, :, k, :], idx[:, :, k:k + 1].broadcast_to([P, T, E_]),
                                            iota[:].unsqueeze(1).broadcast_to([P, T, E_]), ALU.is_equal)
                link(ins)
                dve.tensor_copy(ohb[:], oh[:]).then_inc(oh_ready, 1)
                dve.wait_ge(pos_ps, 1)
                three = lambda bank: PS[:, bank, 0:T * TOPK * E_].rearrange("p (t x) -> p t x", t=T)
                link(dve.tensor_copy(tot[:], three(1)))
                link(dve.tensor_copy(pre[0][:], tot[:]))
                src, s_ = 0, 1
                while s_ < T:
                    link(dve.tensor_tensor(pre[1 - src][:, s_:T], pre[src][:, s_:T], pre[src][:, 0:T - s_], ALU.add))
                    link(dve.tensor_copy(pre[1 - src][:, 0:s_], pre[src][:, 0:s_]))
                    src, s_ = 1 - src, 2 * s_
                link(dve.tensor_tensor(pre[src][:], pre[src][:], tot[:], ALU.subtract))
                link(dve.tensor_tensor(pre[src][:], pre[src][:], three(0), ALU.add))
                ohv = oh[:].rearrange("p t k e -> p t (k e)")
                link(dve.tensor_tensor(pre[src][:], pre[src][:], ohv, ALU.mult))
                link(dve.tensor_reduce(pos[:], pre[src][:].rearrange("p t (k e) -> p t k e", k=TOPK), AX.X, ALU.add))
                link(dve.tensor_scalar(keep[:], pos[:], float(CAP), None, ALU.is_le))
                link(dve.scalar_tensor_tensor(out=slot[:], in0=idx[:], scalar=float(CAP), in1=pos[:],
                                              op0=ALU.mult, op1=ALU.add))
                link(dve.tensor_tensor(slot[:], slot[:], koff[:].unsqueeze(1).broadcast_to([P, T, TOPK]), ALU.add))
                link(dve.tensor_scalar(sidf[:], keep[:], float(-2 * SLOTS), float(2 * SLOTS), ALU.mult, ALU.add))
                link(dve.tensor_tensor(sidf[:], sidf[:], slot[:], ALU.add))
                dve.tensor_copy(sid[:], sidf[:]).then_inc(sid_ready, 1)
                link(dve.tensor_tensor(gidf[:], slot[:], keep[:], ALU.mult))
                dve.tensor_copy(gid[:], gidf[:]).then_inc(gid_ready, 1)
                dve.wait_ge(ew_ready, 1)
                link(dve.tensor_scalar(den[:], ew[:], 1.0, None, ALU.add))
                link(dve.reciprocal(den[:], den[:]))
                link(dve.tensor_copy(w[:, :, 0], den[:]))
                link(dve.tensor_tensor(w[:, :, 1], den[:], ew[:], ALU.mult))
                link(dve.tensor_tensor(w[:], w[:], keep[:], ALU.mult))

                def products(v, i):
                    for u in range(U):
                        v.wait("xt_ps", 2 * u + 1)
                        v.inc(dve.tensor_copy(xgT[:, u % 2, 0, :], PS[0:FC, 0, 0:CAP]), "xt_dve")
                        for jj in range(4):
                            q = 4 * u + jj
                            v.wait("silu", q + 1)
                            v.wait("y_ps", 2 * u - 2)
                            v.inc(dve.tensor_tensor(at[:, u % 2, jj, :], PS[:, 2 + 2 * (q % 2), 0:CAP], sg[:, q % 2],
                                                    ALU.mult), "at")
                        for c in range(2):
                            v.wait("y_ps", 2 * u + c + 1)
                            v.wait(f"y_out{u % 2}", 16 * (u // 2))
                            o = PS[0:CP, 6 + c, :].rearrange("p (t x) -> p t x", t=2)[:, :, 0:D]
                            v.inc(dve.tensor_copy(ye[:, u % 2, 2 * c:2 * c + 2, :], o), "ye")

                passes(dve, products)
                dve.wait_ge(h1_in, 16)
                dve.wait_ge(gathered, 16 * T * TOPK)
                for k in range(TOPK):
                    for t in range(T):
                        ins = dve.scalar_tensor_tensor(out=h1[:, t, :], in0=gy[:, t, k, :], scalar=w[:, t, k:k + 1],
                                                       in1=h1[:, t, :], op0=ALU.mult, op1=ALU.add)
                    if k < TOPK - 1:
                        link(ins)
                ins.then_inc(done, 1)


def program(nc, a, out, scratch):
    embed(nc, a, scratch["H0"], scratch["XG"])
    layers(nc, a, scratch["H0"], scratch["H1"], scratch["XF"], scratch["LG"], scratch["PD"], scratch["MD"],
           scratch["RD"], scratch["XD"])
    experts(nc, a, scratch["H1"], scratch["XF"], scratch["LG"], scratch["XG"], scratch["YD"], out)


def chunks(w):
    return w.reshape(2, FC, -1).transpose(1, 0, 2)


def kernel(**x):
    import numpy as np
    import concourse.bacc as bacc
    from concourse.bass_utils import run_bass_kernel_spmd as run

    x = {k: np.asarray(v) for k, v in x.items()}
    again = list(range(L)) + [0]
    col = lambda v, n: v.reshape(-1, n).T
    la = {k[8:]: v for k, v in x.items() if k.startswith("L0_attn_")}
    a = {
        "ids": x["x_txt"].reshape(B * 4, P).T,
        "curve": x["L0_tok_curve"].reshape(2, P, 2).transpose(1, 0, 2),
        "tok_w": x["L0_tok_proj_w"].T,
        "tok_b": x["L0_tok_proj_b"],
        "txt_w": x["L0_txt_weights"],
        "colmask": (np.arange(D)[None, :] < np.array([192, 96, 144, 192])[:, None]).astype(np.float32),
        "emb": x["L0_txt_emb_weight"],
        "img": x["x"].reshape(-1, 1),
        "ident": np.eye(P, dtype=np.float32),
        "headblk": np.kron(np.eye(H // 2), np.ones((DH, DH))).astype(np.float32),
        "onehot": np.tile(np.kron(np.eye(NT), np.ones((1, P))), (3, 1)).astype(np.float32),
        "Wqkcv": np.stack([np.concatenate([chunks(la[k][l]) for k in ("Wq", "Wk", "Wc", "Wv")], axis=2)
                           for l in again]),
        "bcol": np.stack([np.stack([col(la[k][l], FC) for k in ("bc", "bk", "bq")], axis=1) for l in again]),
        "Wo": np.stack([chunks(la["Wo"][l]) for l in again]),
        "Wi": np.stack([chunks(la["Wi"][l]) for l in again]),
        "Wo2": np.stack([la["Wo2"][l].reshape(NM, P, D).transpose(1, 0, 2) for l in again]),
        "bicol": np.stack([col(la["bi"][l], P) for l in again]),
        "brow": np.stack([np.stack([la[k][l] for k in ("bv", "bo", "g1", "b1", "bo2", "g2", "b2")])
                          for l in again]),
        "W1T": chunks(x["L0_ffn_W1"].T),
        "W2T": x["L0_ffn_W2"].T,
        "WoT": chunks(x["L0_ffn_Wo"].T),
        "WqkvT": chunks(x["L1_attn_qkv_w"].T),
        "WoutT": chunks(x["L1_attn_out_w"].T),
        "Wg": chunks(x["L1_ffn_Wg"]),
        "relbd": block_diagonal(np, x["L1_attn_rel_pos_emb"].T),
        "fcol": x["L0_ffn_b1"].reshape(P, 1),
        "f2col": col(x["L0_ffn_b2"], FC),
        "qkcol": np.stack([col(x["L1_attn_qkv_b"][i * D:(i + 1) * D], FC) for i in range(2)], axis=1),
        "frow": np.stack([x["L0_ffn_bo"], x["L0_ffn_gamma"], x["L0_ffn_beta"], x["L1_attn_qkv_b"][2 * D:],
                          x["L1_attn_out_b"]]),
        "iota": np.arange(E_, dtype=np.float32),
        "koff": np.array([k * E_ * CAP - 1 for k in range(TOPK)], np.float32),
        "tri": np.triu(np.ones((P, P), np.float32)),
        "W1": np.stack([chunks(w) for w in x["L1_ffn_W1"]]),
        "W2": x["L1_ffn_W2"].reshape(E_, 4, P, D).transpose(0, 2, 1, 3),
    }
    a = {k: np.ascontiguousarray(v) for k, v in a.items()}
    nc = bacc.Bacc("TRN2", target_bir_lowering=False, num_devices=1)
    aps = {k: nc.dram_tensor("in_" + k, v.shape, mybir.dt.from_np(v.dtype), kind="ExternalInput").ap()
           for k, v in a.items()}
    out = nc.dram_tensor("out_0", (B, S, D), F32, kind="ExternalOutput").ap()
    scratch = {k: nc.dram_tensor("scratch_" + k, shape, dt).ap() for k, shape, dt in (
        ("H0", (B + 1, P, NT, D), F32), ("H1", (B, P, NT, D), F32), ("XF", (B, P, NT, D), F32),
        ("LG", (B, P, NT, E_), F32), ("XG", (SLOTS, D), F32), ("YD", (SLOTS, D), F32),
        ("PD", (3, 3, D, S), BF16), ("MD", (3, H * NT, P), BF16), ("RD", (3, H * NT, S), BF16),
        ("XD", (S, H, XL), F32))}
    program(nc, aps, out, scratch)
    r = run(nc, [{"in_" + k: v for k, v in a.items()}], core_ids=[0])
    return r.results[0]["out_0"]


def block_diagonal(np, w):
    out = np.zeros((FC, (H // 2) * NREL), w.dtype)
    for h in range(H // 2):
        out[h * DH:(h + 1) * DH, h * NREL:(h + 1) * NREL] = w
    return out
```

```python
import concourse.bass as bass
from concourse import mybir
from concourse.alu_op_type import AluOpType as ALU
from contextlib import ExitStack

F32 = mybir.dt.float32
BF16 = mybir.dt.bfloat16
I32 = mybir.dt.int32
U32 = mybir.dt.uint32
ACT = mybir.ActivationFunctionType
AX = mybir.AxisListType

P = 128
B, NPATCH, NTXT = 4, 256, 512
S = NPATCH + NTXT
NT = S // P
D, H, DH = 192, 12, 16
L = 4
FC = D // 2
HALF = S // 2
FF = 768
NM = FF // P
BANK = 512
G = 4
NG = H // G
PLANE = 224 * 224
VOCAB = 50257
MAXREL = 16
NREL = 2 * MAXREL + 1
WIN = 192
XL = WIN + P - 1
FILL = (XL - NREL) // 2
E_, TOPK, HID = 8, 2, 512
N = B * S
CAP = int(1.2 * N / E_)
CP, CC = 115, 4
NBLK = TOPK * E_
SLOTS = NBLK * CAP

KEY_PARTS = (0, 0, 0, 1, 1, 2)
QRY_PARTS = (0, 1, 2, 0, 1, 0)
NRUN = len(KEY_PARTS)
CORE = len(KEY_PARTS) * DH
MROWS = 3
RROWS = 3 * NT


LSTEP, TSTEP = 78, 85


class Counts:

    def __init__(self, nc, ctx, prefix, per):
        self.per, self.prefix = per, prefix
        self.sem = {k: ctx.enter_context(nc.semaphore(prefix + k)) for k in per}

    def on(self, eng, passes):
        return View(self, eng, passes)


class View:

    def __init__(self, counts, eng, passes):
        self.c, self.eng, self.passes, self.links = counts, eng, passes, {}

    def wait(self, name, k):
        if isinstance(self.passes, int) and self.passes * self.c.per[name] + k <= 0:
            return
        self.eng.wait_ge(self.c.sem[name], self.passes * self.c.per[name] + k)

    def inc(self, ins, name, by=1):
        ins.then_inc(self.c.sem[name], by)

    def step(self, ins, name="dve_step"):
        self.links[name] = self.links.get(name, 0) + 1
        ins.then_inc(self.c.sem[name], 1)
        return self.links[name]

    def link(self, ins, name="dve_step"):
        self.wait(name, self.step(ins, name))

    def close(self, name="dve_step"):
        assert self.links.get(name, 0) == self.c.per[name], (self.c.prefix, self.links.get(name, 0))


def attention_order(runs, lead, rate, bias_jobs):
    ring = iter(range(10 ** 6))
    total = 2 * H * NT
    per_group = 2 * G * NT
    job = 0
    due = None
    blocks = [(kind, g, kt) for kind, g in runs for kt in range(NT)]

    def maxima(n):
        nonlocal job, due
        while job < min(n, total):
            yield ("max", job, next(ring))
            job += 1
            if job % per_group == 0:
                due = job // per_group - 1
                yield ("negmax", due)
            elif due is not None and job % per_group == 4:
                yield from bias()

    def bias():
        nonlocal due
        if due is not None:
            for k in range(bias_jobs):
                yield ("bias", due, k, next(ring))
            due = None

    yield from maxima(lead)
    quota = float(lead)
    ended = None
    for n in range(len(blocks) + 1):
        for j in range(G):
            if j == 1 and (job == total or not rate(n)):
                yield from bias()
            if n < len(blocks):
                yield ("unit", n) + blocks[n] + (j,)
                quota += rate(n) / 6
                yield from maxima(int(quota + 1e-6))
            if n and j % 2:
                yield ("av", n - 1) + blocks[n - 1] + (j // 2,)
            if j % 2:
                quota += rate(n) / 6
                yield from maxima(int(quota + 1e-6))
        if ended is not None:
            for half in range(2):
                yield ("norm", ended) + runs[ended] + (half, next(ring))
            ended = None
        if n and (n - 1) % NT == NT - 1:
            ended = (n - 1) // NT
            yield ("evac", ended)
    for half in range(2):
        yield ("norm", ended) + runs[ended] + (half, next(ring))


COS, DOT = 0, 1
LAYER_ORDER = list(attention_order([(COS, 0), (COS, 1), (DOT, 0), (COS, 2), (DOT, 1), (DOT, 2)], 0,
                                   lambda n: 0 if n < 2 else 6.5 if n < 10 else 5.3, 1))
TAIL_ORDER = list(attention_order([(DOT, 0), (DOT, 1), (DOT, 2)], 64, lambda n: 8, 3))


def embed(nc, a, H0, XG):
    with ExitStack() as ctx:
        sb = lambda n, s, d: ctx.enter_context(nc.sbuf_tensor(n, s, d))
        sem = lambda n: ctx.enter_context(nc.semaphore(n))
        ids = sb("ids", [P, B * 4], I32)
        cur = sb("cur", [P, 2, 2], I32)
        curf = sb("curf", [P, 2, 2], F32)
        pixf = sb("pixf", [P, 2], F32)
        pix = sb("pix", [P, 2], I32)
        pw = sb("pw", [P, 4, D], F32)
        wt = sb("wt", [P, 4], F32)
        mask = sb("mask", [P, 4, D], F32)
        cs = sb("cs", [P, D], F32)
        gim = sb("gim", [P, 2, 3 * B], F32)
        hs = sb("hs", [P, B, NT, D], F32)
        zero = sb("zero", [CP, 8 * D], F32)
        loaded, pix_ready = sem("emb_loaded"), sem("pix_ready")
        img_in, txt_in, step = sem("img_in"), sem("txt_in"), sem("emb_step")
        h_ready, stored, zeroed, zset = sem("h_ready"), sem("h_stored"), sem("xg_zeroed"), sem("zero_set")
        patches_ready = sem("patches_ready")
        nload = 6

        with nc.Block() as block:
            @block.sync
            def _(sp):
                sp.dma_start(ids[:], a["ids"]).then_inc(loaded, 16)
                sp.dma_start(cur[:], a["curve"]).then_inc(loaded, 16)
                sp.dma_start(pw[:, 0:3], a["tok_w"].partition_broadcast(P)).then_inc(loaded, 16)
                sp.dma_start(pw[:, 3], a["tok_b"].partition_broadcast(P)).then_inc(loaded, 16)
                sp.dma_start(wt[:], a["txt_w"].partition_broadcast(P)).then_inc(loaded, 16)
                sp.dma_start(mask[:], a["colmask"].partition_broadcast(P)).then_inc(loaded, 16)
                sp.wait_ge(zset, 1)
                for i in range(8):
                    sp.dma_start(XG[i * SLOTS // 8:(i + 1) * SLOTS // 8, :].rearrange("(p c) d -> p (c d)", p=CP),
                                 zero[:]).then_inc(zeroed, 16)
                sp.wait_ge(h_ready, 1)
                sp.wait_ge(patches_ready, 1)
                sp.dma_start(H0[0:B].rearrange("b p t d -> p b t d"), hs[:]).then_inc(stored, 16)
                sp.dma_start(H0[B], hs[:, 0]).then_inc(stored, 16)
                sp.wait_ge(stored, 32)
                sp.wait_ge(zeroed, 8 * 16)

            @block.gpsimd
            def _(pool):
                pool.wait_ge(loaded, 16 * nload)
                pool.wait_ge(pix_ready, 1)
                for t in range(2):
                    for c in range(3 * B):
                        pool.indirect_dma_start(
                            out=gim[:, t, c:c + 1], out_offset=None, in_=a["img"],
                            in_offset=bass.IndirectOffsetOnAxis(ap=pix[:, t:t + 1], axis=0),
                            element_offset=c * PLANE).then_inc(img_in, 16)
                for b in range(B):
                    for t in range(4):
                        pool.indirect_dma_start(
                            out=hs[:, b, 2 + t, :], out_offset=None, in_=a["emb"],
                            in_offset=bass.IndirectOffsetOnAxis(ap=ids[:, b * 4 + t:b * 4 + t + 1], axis=0)
                        ).then_inc(txt_in, 16)

            @block.vector
            def _(dve):
                links = [0]

                def link(ins):
                    links[0] += 1
                    ins.then_inc(step, 1)
                    dve.wait_ge(step, links[0])

                dve.memset(zero[:], 0.0).then_inc(zset, 1)
                dve.wait_ge(loaded, 16 * nload)
                link(dve.tensor_copy(curf[:], cur[:]))
                link(dve.scalar_tensor_tensor(out=pixf[:], in0=curf[:, :, 1], scalar=224.0, in1=curf[:, :, 0],
                                              op0=ALU.mult, op1=ALU.add))
                dve.tensor_copy(pix[:], pixf[:]).then_inc(pix_ready, 1)
                link(dve.tensor_scalar(cs[:], mask[:, 0], wt[:, 0:1], None, ALU.mult))
                for i in range(1, 4):
                    link(dve.scalar_tensor_tensor(out=cs[:], in0=mask[:, i], scalar=wt[:, i:i + 1], in1=cs[:],
                                                  op0=ALU.mult, op1=ALU.add))
                dve.wait_ge(img_in, 16 * 2 * 3 * B)
                last = None
                for c in range(3):
                    for b in range(B):
                        for t in range(2):
                            prev = pw[:, 3] if c == 0 else hs[:, b, t]
                            last = dve.scalar_tensor_tensor(out=hs[:, b, t], in0=pw[:, c],
                                                            scalar=gim[:, t, 3 * b + c:3 * b + c + 1], in1=prev,
                                                            op0=ALU.mult, op1=ALU.add)
                    if c < 2:
                        link(last)
                last.then_inc(patches_ready, 1)
                dve.wait_ge(txt_in, 16 * 16)
                dve.tensor_tensor(hs[:, :, 2:NT, :], hs[:, :, 2:NT, :],
                                  cs[:].unsqueeze(1).unsqueeze(1).broadcast_to([P, B, 4, D]),
                                  ALU.mult).then_inc(h_ready, 1)


def layers(nc, a, H0, H1, XF, LG, PD, MD, RD, XD, ONES):
    with ExitStack() as ctx:
        sb = lambda n, s, d: ctx.enter_context(nc.sbuf_tensor(n, s, d))
        sem = lambda n: ctx.enter_context(nc.semaphore(n))

        X = sb("X", [P, NT, D], F32)
        HR = sb("HR", [P, NT, D], F32)
        A1 = sb("A1", [P, NT, D], F32)
        XT = sb("XT", [FC, 2, S], F32)
        PARTS = sb("PARTS", [P, 3 * 3 * 2 * S], BF16)
        parts = PARTS[0:FC, :].rearrange("p (o k c t) -> p o k c t", o=3, k=3, c=2)
        pf = PARTS[:].bitcast(F32)
        OS = pf[:, 0:S]
        T2, CTX = (pf[:, S + i * NT * D:S + (i + 1) * NT * D].rearrange("p (t d) -> p t d", t=NT)
                   for i in range(2))
        AQ = sb("AQ", [P, H, S], BF16)
        AK = sb("AK", [P, H, S], BF16)
        CL = sb("CL", [P, H, S], BF16)
        CR = sb("CR", [P, H, S], BF16)
        DWH = [w[:].rearrange("p h s -> p (h s)").bitcast(F32).rearrange("p (r t x) -> p r t x", r=4, t=NT)
               for w in (AQ, AK)]
        PWN = pf[:, 2 * 3 * S:3 * 3 * S].rearrange("p (r t x) -> p r t x", r=2, t=NT)
        WINDOWS = [DWH[r // 4][:, r % 4] for r in range(8)] + [PWN[:, 0], PWN[:, 1], A1[:], X[:]]
        window = lambda h: WINDOWS[h]
        HT = AQ[:].rearrange("p h s -> p (h s)").bitcast(F32).rearrange("p (m s) -> p m s", m=NM)
        VP = sb("VP", [P, NT, H, 2 * DH], F32)
        E = sb("E", [P, 8, S], F32)
        exp_tile = lambda unit: E[:, (unit + 6) % 8, :]
        FKP = sb("FKP", [P, 2, S], F32)
        Fk = FKP[0:FC]
        MX6 = FKP[:, 0, 0:NT * H * NT].rearrange("p (t h k) -> p t h k", t=NT, h=H)
        BM = FKP[:, 1, 0:NT * G * NT].rearrange("p (t h k) -> p t h k", t=NT, h=G)
        VVP = FKP[:, 1, NT * G * NT:NT * G * NT + 3 * NT * G * NT // 2].bitcast(BF16).rearrange(
            "p (k t x) -> p k t x", k=3, t=NT)
        Fc, Fq, SQ = E[0:FC, 0:2, :], E[0:FC, 4:6, :], E[0:FC, 6:8, :]
        NXS = 3
        XS = [w[:, 0:G * XL].rearrange("p (h x) -> p h x", h=G) for w in (
            pf[:, 2 * 3 * S:3 * 3 * S], E[:, 0:2, :].rearrange("p e t -> p (e t)"),
            E[:, 6:8, :].rearrange("p e t -> p (e t)"))]
        HN = E[:, 0:2, :].rearrange("p e t -> p (e t)")[:, 0:NT * D].rearrange("p (t d) -> p t d", t=NT)
        REM = sb("REM", [FC, 2, S], F32)
        MX = sb("MX", [P, 2, H * NT], F32)
        NMX = sb("NMX", [P, G * NT], F32)
        NMR = sb("NMR", [P, G * NT], F32)
        NMP = sb("NMP", [P, 3, G * NT], BF16)
        MT = sb("MT", [G * NT, 3, P], BF16)
        RZ = sb("RZ", [P, 3, G], F32)
        TP = sb("TP", [P, 3, G, DH], F32)
        ST = sb("ST", [P, NT, 6], F32)
        MV = sb("MV", [P, NT, 2], F32)
        SD = sb("SD", [P, NT], F32)
        EPS = sb("EPS", [P, 2], F32)
        Wqkcv = sb("Wqkcv", [FC, 2, 4 * D], F32)
        Wo = sb("Wo", [FC, 2, D], F32)
        Wi = sb("Wi", [FC, 2, FF], F32)
        Wo2 = sb("Wo2", [P, NM, D], F32)
        bcol = sb("bcol", [FC, 3, 2], F32)
        bicol = sb("bicol", [P, NM], F32)
        MT1 = REM[0:G * NT].rearrange("p c t -> p (c t)").bitcast(BF16)[:, 0:3 * S].rearrange(
            "p (k t) -> p k t", k=3)
        brow = sb("brow", [P, 7, D], F32)
        W1T = sb("W1T", [FC, 2, P], F32)
        W2T = sb("W2T", [P, D], F32)
        WoT = sb("WoT", [FC, 2, D], F32)
        WqkvT = sb("WqkvT", [FC, 2, 3 * D], F32)
        WoutT = sb("WoutT", [FC, 2, D], F32)
        Wg = sb("Wg", [FC, 2, E_], F32)
        EMB = sb("EMB", [FC, 6 * NREL], F32)
        fcol = sb("fcol", [P, 1], F32)
        f2col = sb("f2col", [FC, 2], F32)
        qkcol = sb("qkcol", [FC, 2, 2], F32)
        frow = sb("frow", [P, 5, D], F32)
        LGT = sb("LGT", [P, NT, E_], F32)
        RB = sb("RB", [P, NT, H, 2], F32)
        BS = sb("BS", [P, NT, H, NT], F32)
        M1 = sb("M1", [P, NT, G], F32)
        idf = sb("idf", [P, P], F32)
        idb = sb("idb", [P, P], BF16)
        negI = sb("negI", [P, P], BF16)
        blk = sb("blk", [FC, FC], F32)

        PS = ctx.enter_context(nc.psum_tensor("PS", [P, 8, BANK], F32))
        flat = lambda b0, n: PS[:, b0, 0:n]

        w_once, w_first, w_rest = sem("w_once"), sem("w_first"), sem("w_rest")
        const_ready, h_in, h_out = sem("const_ready"), sem("h_in"), sem("h_out")
        onehot_in, ones_in, hr_ready = sem("onehot_in"), sem("ones_in"), sem("hr_ready")
        x_ready = sem("x_ready")
        XPER = 3 * (1 + L)
        NW_FIRST, NW_REST = 3, 5
        onehot_ready = sem("onehot_ready")
        OHF = E[0:RROWS, 2, :]
        OHB = AQ[0:RROWS, 0, :]
        once = [(idf[:], a["ident"]), (blk[:], a["headblk"]), (W1T[:], a["W1T"]), (W2T[:], a["W2T"]),
                (WoT[:], a["WoT"]), (WqkvT[:], a["WqkvT"]), (WoutT[:], a["WoutT"]), (Wg[:], a["Wg"]),
                (EMB[:], a["relbd"]), (fcol[:], a["fcol"]), (f2col[:], a["f2col"]), (qkcol[:], a["qkcol"]),
                (frow[:], a["frow"].partition_broadcast(P)), (OHF, a["onehot"])]
        NW_ONCE = len(once)
        lay = Counts(nc, ctx, "l_", dict(
            tr_ps=6, tr_dve=3, tr_act=3, v_ps=3, v_dve=3, f_ps=6, f_act=6, sq_act=2, n_ps=2, n_act=4,
            p_dve=6, sc_ps=144, e_act=144, av_ps=36, osb=6, m_ps=144 + 12 + NG, m_free=144 + 12 + NG,
            mt_dve=NG, ctx_ready=1, y_ps=3, a1_ready=3, **{f"pd_w{i}": 16 for i in range(6)},
            **{f"c_in{g}": 2 * 16 * NRUN for g in range(NG)}, **{f"qk_in{g}": 2 * 16 * NRUN for g in range(NG)},
            **{f"md_w{g}": 16 for g in range(NG)}, **{f"md_r{g}": 16 for g in range(NG)},
            ln_var=6, ln_sd=6, f1_ps=12, g_act=12, y2_ps=3, dve_step=LSTEP))
        tail = Counts(nc, ctx, "t_", dict(
            a_ready=9, tr_ps=8, tr_dve=4, tr_act=4, ln_var=15, ln_sd=15, f0_ps=1, relu=1, pr_ps=2, pr_act=2,
            yo_ps=3, v_ps=3, v_dve=3, f_ps=4, f_act=4, p_dve=4, **{f"pd_w{i}": 16 for i in range(4)},
            **{f"qk_in{g}": 2 * 16 * NRUN for g in range(NG)}, rr_ps=6, rr_dve=6, xs_act=3 * NG * NT,
            **{f"xs_w{i}": 16 * NG * NT // NXS for i in range(NXS)}, dw_fix=H,
            sc_ps=72, e_act=72, av_ps=18, osb=3, m_ps=144 + 3 * NG + 6, m_free=144 + 3 * NG + 6, mt_dve=3 * NG,
            yo2_ps=3, lg_ps=1, out_ready=1, dve_step=TSTEP,
            **{f"dw_in{h}": 16 for h in range(H)},
            **{f"md_w{g}": 16 for g in range(NG)}, **{f"md_r{g}": 48 for g in range(NG)}))

        def transposes(v, src, pair_ready=None):
            for pair in range(3):
                if pair_ready is not None:
                    pair_ready(pair)
                for c in range(2):
                    for t in range(2 * pair, 2 * pair + 2):
                        last = v.eng.transpose(PS[0:FC, 2 * c + t // 4, (t % 4) * P:(t % 4) * P + P],
                                               src[:, t, c * FC:(c + 1) * FC], idf[:])
                    if pair == 2:
                        v.inc(last, "tr_ps")

        def tr_view(c):
            return PS[0:FC, 2 * c:2 * c + 2, :].rearrange("p a b -> p (a b)")[:, 0:S]

        def take_transposed(v, use, c, act):
            v.wait("tr_ps", 2 * use + c + 1)
            if act:
                v.inc(v.eng.activation(XT[:, c, :], tr_view(c), ACT.Copy), "tr_act")
            else:
                v.inc(v.eng.tensor_copy(XT[:, c, :], tr_view(c)), "tr_dve")

        def token_product(v, bank, weights, ncols, sig):
            for t in range(NT):
                for c in range(2):
                    last = v.eng.matmul(PS[:, bank + t // 2, (t % 2) * 256:(t % 2) * 256 + ncols],
                                        XT[:, c, t * P:(t + 1) * P], weights[:, c, :],
                                        start=(c == 0), stop=(c == 1))
                if t % 2:
                    v.inc(last, sig)

        def feature_product(v, bank, weights, sig, m):
            for h in range(2):
                for c in range(2):
                    last = v.eng.matmul(PS[0:FC, bank + 2 * m + h, 0:HALF],
                                        weights[:, c, m * FC:(m + 1) * FC],
                                        XT[:, c, h * HALF:(h + 1) * HALF], start=(c == 0), stop=(c == 1))
            v.inc(last, sig)

        def chunk_view(bank, m):
            return PS[0:FC, bank + 2 * m:bank + 2 * m + 2, 0:HALF]

        def halves(ap):
            return ap.rearrange("p (h t) -> p h t", h=2)

        def token_view(bank, pair):
            return PS[:, bank + pair, :].rearrange("p (t x) -> p t x", t=2)[:, :, 0:D]

        def row_bc(row, n):
            return row.unsqueeze(1).broadcast_to([P, n, D])

        def layer_norm(v, source, src, dst, n, done, gain=None, shift=None):
            dve = v.eng
            tiles = lambda pair: range(2 * pair, 2 * pair + 2)

            def statistics(pair):
                if source is not None:
                    v.link(source(pair))
                for t in tiles(pair):
                    ins = dve.bn_stats(ST[:, t, :], src[:, t, :])
                return v.step(ins)

            def aggregate(pair):
                for t in tiles(pair):
                    ins = dve.bn_aggr(MV[:, t, :], ST[:, t, :])
                v.inc(ins, "ln_var")

            def inverse(pair):
                v.wait("ln_sd", 3 * (n - 1) + pair + 1)
                ts = slice(2 * pair, 2 * pair + 2)
                return v.step(dve.reciprocal(SD[:, ts], SD[:, ts]))

            def apply(pair):
                for t in tiles(pair):
                    if gain is None:
                        ins = dve.tensor_scalar(dst[:, t, :], src[:, t, :], MV[:, t, 0:1], SD[:, t:t + 1],
                                                ALU.subtract, ALU.mult)
                    else:
                        ins = dve.scalar_tensor_tensor(out=dst[:, t, :], in0=src[:, t, :], scalar=MV[:, t, 0:1],
                                                       in1=gain, op0=ALU.subtract, op1=ALU.mult)
                if gain is not None:
                    v.link(ins)
                    for t in tiles(pair):
                        ins = dve.scalar_tensor_tensor(out=dst[:, t, :], in0=dst[:, t, :], scalar=SD[:, t:t + 1],
                                                       in1=shift, op0=ALU.mult, op1=ALU.add)
                done(ins)

            stats = statistics(0)
            v.wait("dve_step", stats)
            dve.memset(SD[:, 0:2], 0.0)
            aggregate(0)
            stats = statistics(1)
            for pair in range(3):
                if pair < 2:
                    v.wait("dve_step", stats)
                inverted = inverse(pair)
                if pair < 2:
                    aggregate(pair + 1)
                v.wait("dve_step", inverted)
                if pair == 0:
                    stats = statistics(2)
                apply(pair)

        def norm_sd(v, n, eps):
            for pair in range(3):
                ts = slice(2 * pair, 2 * pair + 2)
                v.wait("ln_var", 3 * (n - 1) + pair + 1)
                v.inc(v.eng.activation(SD[:, ts], MV[:, ts, 1], ACT.Sqrt, bias=EPS[:, eps:eps + 1]), "ln_sd")

        def split(v, f, o, m, sig):
            f = f[:, m, :]
            rem = REM[:, m, :]
            v.link(v.eng.tensor_copy(parts[:, o, 0, m], f))
            v.link(v.eng.tensor_tensor(rem, f, parts[:, o, 0, m], ALU.subtract))
            v.link(v.eng.tensor_copy(parts[:, o, 1, m], rem))
            v.inc(v.eng.tensor_tensor(parts[:, o, 2, m], rem, parts[:, o, 1, m], ALU.subtract), sig)

        def pe_scores(v, keys, queries, rows, unit, h, kt, cosine, rel):
            if unit >= 2:
                v.wait("e_act", unit - 1)
            slot = 2 * (unit % 2)
            for c0, nc_ in ((0, BANK), (BANK, S - BANK)):
                last = v.eng.matmul(PS[:, slot + c0 // BANK, 0:nc_], keys[0:rows, h, kt * P:(kt + 1) * P],
                                    queries[0:rows, h, c0:c0 + nc_], start=True, stop=True)
            if cosine:
                last = v.eng.matmul(PS[:, slot + kt // 4, (kt % 4) * P:(kt % 4) * P + P], negI[:], idb[:],
                                    start=False, stop=True, skip_group_check=True)
            if rel:
                last = rel_window(v, window(h), kt, slot)
            v.inc(last, "sc_ps")

        def rel_window(v, DW, kt, slot):
            for qt in (kt - 1, kt, kt + 1):
                if not 0 <= qt < NT:
                    continue
                col = PS[:, slot + qt // 4, (qt % 4) * P:(qt % 4) * P + P]
                if qt == kt:
                    ins = v.eng.matmul(col, DW[:, qt, 32:32 + P], idf[:], start=False, stop=True,
                                       skip_group_check=True)
                elif qt > kt:
                    ins = v.eng.matmul(col[96:128], DW[:, qt, 0:32], idf[:], start=False, stop=True,
                                       skip_group_check=True)
                else:
                    ins = v.eng.matmul(col[0:32], DW[:, qt, 160:192], idf[:], start=False, stop=True,
                                       skip_group_check=True)
            return ins

        def pe_av(v, n, g, kt, half):
            if half == 0:
                v.wait("e_act", 4 * n + 4)
                if kt == 0 and n >= NT:
                    v.wait("osb", n // NT)
            for j in range(G):
                last = v.eng.matmul(PS[32 * j:32 * j + 32, 4 + half, 0:HALF], VP[:, kt, g * G + j, :],
                                    exp_tile(4 * n + j)[:, half * HALF:(half + 1) * HALF],
                                    start=(kt == 0), stop=(kt == NT - 1))
            if half:
                v.inc(last, "av_ps")

        def pe_norm(v, run, half, ring):
            v.wait("osb", run + 1)
            v.wait("m_free", ring - 1)
            for t in range(3):
                last = v.eng.transpose(PS[:, 6 + ring % 2, t * P:(t + 1) * P],
                                       OS[:, (3 * half + t) * P:(3 * half + t + 1) * P], idf[:])
            v.inc(last, "m_ps")

        def act_exp(v, unit, scale, bias):
            v.wait("sc_ps", unit + 1)
            if unit >= 8:
                v.wait("av_ps", unit // 4 - 1)
            src = PS[:, 2 * (unit % 2):2 * (unit % 2) + 2, :].rearrange("p a b -> p (a b)")[:, 0:S]
            v.inc(v.eng.activation(exp_tile(unit), src, ACT.Exp, bias=bias, scale=scale), "e_act")

        def dve_evac(v, group):
            v.wait("av_ps", NT * (group + 1))
            v.inc(v.eng.tensor_copy(halves(OS), PS[:, 4:6, 0:HALF]), "osb")

        def dve_norm(v, g, half, ring, add, twice, last=False):
            v.wait("m_ps", ring + 1)
            v.wait("m_free", ring)
            o = PS[:, 6 + ring % 2, 0:3 * P].rearrange("p (t h x) -> p t h x", t=3, h=G)
            v.link(v.eng.reciprocal(RZ[:], o[:, :, :, DH]))
            if twice:
                v.link(v.eng.tensor_scalar(RZ[:], RZ[:], 2.0, None, ALU.mult))
            dst = CTX[:, 3 * half:3 * half + 3, g * G * DH:(g + 1) * G * DH].rearrange("p t (h x) -> p t h x", h=G)
            rz = RZ[:].unsqueeze(3).broadcast_to([P, 3, G, DH])
            ins = v.eng.tensor_tensor(TP[:] if add else dst, o[:, :, :, 0:DH], rz, ALU.mult)
            v.inc(ins, "m_free")
            if add:
                v.wait("m_free", ring + 1)
                ins = v.eng.tensor_tensor(dst, dst, TP[:], ALU.add)
                if last:
                    v.inc(ins, "ctx_ready")
                else:
                    v.link(ins)

        def pe_max(v, queries, keys, i, ring, rel):
            h, qt, half = i // (2 * NT), i // 2 % NT, i % 2
            if ring >= 2:
                v.wait("m_free", ring - 1)
            out = PS[:, 6 + ring % 2, 0:HALF]
            last = v.eng.matmul(out, queries[0:CORE, h, qt * P:(qt + 1) * P],
                                keys[0:CORE, h, half * HALF:(half + 1) * HALF], start=True, stop=True)
            if rel is not None:
                k0 = max(qt * P - 32, half * HALF)
                k1 = min(qt * P - 32 + WIN, (half + 1) * HALF)
                if k1 > k0:
                    x0 = k0 - (qt * P - 32)
                    last = v.eng.matmul(out[:, k0 - half * HALF:k1 - half * HALF], idf[:],
                                        rel[:, qt, x0:x0 + k1 - k0], start=False, stop=True,
                                        skip_group_check=True)
            v.inc(last, "m_ps")

        def dve_values(v, bank, bias):
            for pair in range(3):
                v.wait("v_ps", pair + 1)
                o = VP[:, 2 * pair:2 * pair + 2, :, 0:DH]
                i0 = token_view(bank, pair).rearrange("p t (h x) -> p t h x", h=H)
                i1 = row_bc(bias, 2).rearrange("p t (h x) -> p t h x", h=H)
                v.inc(v.eng.tensor_tensor(o, i0, i1, ALU.add), "v_dve")

        def product(v, sig, bank, other, dst):
            def source(pair):
                v.wait(sig, pair + 1)
                ts = slice(2 * pair, 2 * pair + 2)
                return v.eng.tensor_tensor(dst[:, ts, :], token_view(bank, pair), other(ts), ALU.add)
            return source

        def fix_window(v, h):
            w = window(h)
            v.wait(f"dw_in{h}", 16)
            dve = v.eng
            dve.tensor_tensor(w[:, 1:NT, 0:32], w[:, 1:NT, 0:32],
                              RB[:, 1:NT, h, 0:1].broadcast_to([P, NT - 1, 32]), ALU.subtract)
            v.inc(dve.tensor_tensor(w[:, 0:NT - 1, 160:192], w[:, 0:NT - 1, 160:192],
                                    RB[:, 0:NT - 1, h, 1:2].broadcast_to([P, NT - 1, 32]), ALU.subtract), "dw_fix")

        def pe_attention(v, order, relative):
            operands = {COS: (CL, CR, CORE), DOT: (CL, CR, CORE + RROWS) if relative else (AK, AQ, CORE + MROWS)}
            for event, *x in order:
                if event == "unit":
                    n, kind, g, kt, j = x
                    if kt == 0 and j == 0:
                        if relative and n == 0:
                            v.wait("xs_act", 3 * NG * NT)
                        if kind == COS:
                            v.wait(f"c_in{g}", 2 * 16 * NRUN)
                        else:
                            v.wait(f"md_r{g}", 48 if relative else 16)
                    keys, queries, rows = operands[kind]
                    pe_scores(v, keys, queries, rows, 4 * n + j, g * G + j, kt, kind == COS, relative)
                elif event == "max":
                    i, ring = x
                    if i % (2 * G * NT) == 0:
                        v.wait(f"qk_in{i // (2 * G * NT)}", 2 * 16 * NRUN)
                    if relative:
                        h = i // (2 * NT)
                        if i % (2 * NT) == 0:
                            v.wait("dw_fix", h + 1)
                        pe_max(v, CR, CL, i, ring, window(h))
                    else:
                        pe_max(v, AQ, AK, i, ring, None)
                elif event == "bias":
                    g, k, ring = x
                    v.wait("m_free", ring - 1)
                    if relative:
                        v.wait("mt_dve", 3 * g + k + 1)
                        for t in range(NT):
                            last = v.eng.transpose(
                                PS[0:G * NT, 6 + ring % 2, 0:384].bitcast(BF16)[:, t * P:(t + 1) * P],
                                VVP[:, k, t, :], idb[:])
                    else:
                        v.wait("mt_dve", g + 1)
                        for k in range(3):
                            last = v.eng.transpose(
                                PS[0:G * NT, 6 + ring % 2, 0:192].bitcast(BF16)[:, k * P:(k + 1) * P],
                                NMP[:, k, :], idb[:])
                    v.inc(last, "m_ps")
                elif event == "av":
                    n, kind, g, kt, half = x
                    pe_av(v, n, g, kt, half)
                elif event == "norm":
                    run, kind, g, half, ring = x
                    pe_norm(v, run, half, ring)

        def act_attention(v, order, relative):
            for event, *x in order:
                if event == "unit":
                    n, kind, g, kt, j = x
                    unit = 4 * n + j
                    if unit in (6, 7) and relative:
                        v.wait("p_dve", 4)
                    elif unit < 8 and not relative:
                        v.wait("p_dve", (1, 2, 2, 2, 2, 2, 4, 5)[unit])
                    scale, bias = (-1.0, 1.0) if kind == COS else (0.25, 0.0)
                    act_exp(v, unit, scale, bias)

        def negate_maxima(v, g):
            dve = v.eng
            cols = slice(g * G * NT, (g + 1) * G * NT)
            v.link(dve.tensor_tensor(NMX[:], MX[:, 0, cols], MX[:, 1, cols], ALU.max))
            v.link(dve.tensor_scalar(NMX[:], NMX[:], -1.0, None, ALU.mult))
            v.link(dve.tensor_copy(NMP[:, 0], NMX[:]))
            v.link(dve.tensor_tensor(NMR[:], NMX[:], NMP[:, 0], ALU.subtract))
            v.link(dve.tensor_copy(NMP[:, 1], NMR[:]))
            v.inc(dve.tensor_tensor(NMP[:, 2], NMR[:], NMP[:, 1], ALU.subtract), "mt_dve")

        def relative_minus_maxima(v, g):
            dve = v.eng
            hs = slice(g * G, (g + 1) * G)
            v.link(dve.tensor_tensor(MX6[:, :, hs], MX6[:, :, hs], BS[:, :, hs], ALU.add))
            v.link(dve.tensor_reduce(M1[:], MX6[:, :, hs], AX.X, ALU.max))
            v.link(dve.tensor_tensor(BM, BS[:, :, hs], M1[:].unsqueeze(3).broadcast_to([P, NT, G, NT]),
                                     ALU.subtract))
            bm = BM.rearrange("p t h k -> p t (h k)")
            for k in range(3):
                v.inc(dve.tensor_copy(VVP[:, k], bm), "mt_dve")
                if k < 2:
                    v.wait("mt_dve", 3 * g + k + 1)
                    v.link(dve.tensor_tensor(bm, bm, VVP[:, k], ALU.subtract))

        def dve_attention(v, order, relative):
            runs = max(x[0] for event, *x in order if event == "evac") + 1
            for event, *x in order:
                if event == "max":
                    i, ring = x
                    h, qt, half = i // (2 * NT), i // 2 % NT, i % 2
                    v.wait("m_ps", ring + 1)
                    src = PS[:, 6 + ring % 2, 0:HALF]
                    if relative:
                        v.inc(v.eng.tensor_reduce(MX6[:, qt, h, 3 * half:3 * half + 3],
                                                  src.rearrange("p (t s) -> p t s", t=3), AX.X, ALU.max), "m_free")
                    else:
                        v.inc(v.eng.tensor_reduce(MX[:, half, h * NT + qt:h * NT + qt + 1], src, AX.X, ALU.max),
                              "m_free")
                    last_max = ring
                    if relative and i % (2 * NT) == 2 * NT - 5 and h < H - 1:
                        fix_window(v, h + 1)
                elif event == "negmax":
                    g, = x
                    v.wait("m_free", last_max + 1)
                    if g:
                        v.wait("m_ps", bias_ring + 1)
                    (relative_minus_maxima if relative else negate_maxima)(v, g)
                elif event == "bias":
                    g, k, ring = x
                    v.wait("m_ps", ring + 1)
                    if g:
                        v.wait(f"md_w{g - 1}", 16)
                    if relative:
                        ins = v.eng.tensor_copy(MT1[:, k, :], PS[0:G * NT, 6 + ring % 2, 0:384].bitcast(BF16))
                    else:
                        ins = v.eng.tensor_copy(MT[:], PS[0:G * NT, 6 + ring % 2, 0:192].bitcast(BF16).rearrange(
                            "p (k t) -> p k t", k=3))
                    v.inc(ins, "m_free")
                    bias_ring = ring
                elif event == "evac":
                    if x[0] == 0:
                        for n in range(4 if relative else 6):
                            v.wait(f"pd_w{n}", 16)
                    dve_evac(v, x[0])
                elif event == "norm":
                    run, kind, g, half, ring = x
                    dve_norm(v, g, half, ring, kind == DOT and not relative, relative,
                             run == runs - 1 and half == 1)

        def ring_of(order, event, g):
            return max(x[-1] for e, *x in order if e == event and x[0] == g) + 1

        with nc.Block() as block:
            @block.tensor
            def _(pe):
                pe.wait_ge(const_ready, 1)
                pe.wait_ge(w_once, 16 * NW_ONCE)
                with pe.Fori(0, B) as b:
                    with pe.Fori(0, L) as l:
                        p = b * L + l
                        v = lay.on(pe, p)
                        transposes(v, X, lambda pair: pe.wait_ge(x_ready, b * XPER + l * 3 + pair + 1))
                        pe.wait_ge(w_first, p * (16 * NW_FIRST) + 16 * NW_FIRST)
                        v.wait("tr_dve", 1)
                        v.wait("tr_act", 1)
                        feature_product(v, 0, Wqkcv[:, :, 2 * D:3 * D], "f_ps", 0)
                        feature_product(v, 0, Wqkcv[:, :, 2 * D:3 * D], "f_ps", 1)
                        for m in range(2):
                            v.wait("sq_act", m + 1)
                            v.wait("f_act", m + 1)
                            for h in range(2):
                                last = pe.matmul(PS[0:FC, 2 * m + h, 0:HALF], blk[:],
                                                 halves(SQ[:, m, :])[:, h, :], start=True, stop=True)
                            v.inc(last, "n_ps")
                            feature_product(v, 4, Wqkcv[:, :, D:2 * D], "f_ps", m)
                        for m in range(2):
                            v.wait("f_act", 2 + m + 1)
                            feature_product(v, 4, Wqkcv[:, :, 0:D], "f_ps", m)
                        v.wait("n_act", 2)
                        token_product(v, 0, Wqkcv[:, :, 3 * D:4 * D], D, "v_ps")
                        v.wait("f_act", 6)
                        v.wait("v_dve", 3)
                        pe.wait_ge(ones_in, b * 16 + 16)
                        pe_attention(v, LAYER_ORDER, False)
                        v.wait("ctx_ready", 1)
                        transposes(v, CTX)
                        pe.wait_ge(w_rest, p * (16 * NW_REST) + 16 * NW_REST)
                        v.wait("tr_dve", 2)
                        v.wait("tr_act", 2)
                        token_product(v, 4, Wo, D, "y_ps")
                        transposes(v, A1, lambda pair: v.wait("a1_ready", pair + 1))
                        v.wait("tr_dve", 3)
                        v.wait("tr_act", 3)
                        for f in range(2 * NM):
                            m, h = divmod(f, 2)
                            if f >= 4:
                                v.wait("g_act", f - 3)
                            for c in range(2):
                                last = pe.matmul(PS[:, 4 + f % 4, 0:HALF], Wi[:, c, m * P:(m + 1) * P],
                                                 XT[:, c, h * HALF:(h + 1) * HALF], start=(c == 0), stop=(c == 1))
                            v.inc(last, "f1_ps")
                        for t in range(NT):
                            v.wait("g_act", 2 * NM)
                            for m in range(NM):
                                last = pe.matmul(PS[:, 4 + t // 2, (t % 2) * 256:(t % 2) * 256 + D],
                                                 HT[:, m, t * P:(t + 1) * P], Wo2[:, m, :],
                                                 start=(m == 0), stop=(m == NM - 1))
                            if t % 2:
                                v.inc(last, "y2_ps")
                    v = tail.on(pe, b)
                    transposes(v, A1, lambda pair: v.wait("a_ready", pair + 1))
                    v.wait("tr_dve", 1)
                    v.wait("tr_act", 1)
                    for h in range(2):
                        for c in range(2):
                            last = pe.matmul(PS[:, 4 + h, 0:HALF], W1T[:, c, :], XT[:, c, h * HALF:(h + 1) * HALF],
                                             start=(c == 0), stop=(c == 1))
                    v.inc(last, "f0_ps")
                    v.wait("relu", 1)
                    for m in range(2):
                        for h in range(2):
                            last = pe.matmul(PS[0:FC, 2 * m + h, 0:HALF], W2T[:, m * FC:(m + 1) * FC],
                                             E[:, 0, h * HALF:(h + 1) * HALF], start=True, stop=True)
                        v.inc(last, "pr_ps")
                    v.wait("pr_act", 2)
                    for t in range(NT):
                        for c in range(2):
                            last = pe.matmul(PS[:, 4 + t // 2, (t % 2) * 256:(t % 2) * 256 + D],
                                             Fk[:, c, t * P:(t + 1) * P], WoT[:, c, :], start=(c == 0), stop=(c == 1))
                        if t % 2:
                            v.inc(last, "yo_ps")
                    transposes(v, A1, lambda pair: v.wait("a_ready", 3 + pair + 1))
                    v.wait("tr_dve", 2)
                    v.wait("tr_act", 2)
                    token_product(v, 4, WqkvT[:, :, 2 * D:3 * D], D, "v_ps")
                    for m in range(2):
                        feature_product(v, 0, WqkvT[:, :, 0:D], "f_ps", m)
                    v.wait("v_dve", 3)
                    for m in range(2):
                        feature_product(v, 4, WqkvT[:, :, D:2 * D], "f_ps", m)
                    for t in range(NT):
                        v.wait("f_act", 2 if t < 4 else 3)
                        for c in range(2):
                            last = pe.matmul(PS[:, t, c * 256:c * 256 + 6 * NREL], Fq[:, c, t * P:(t + 1) * P],
                                             EMB[:], start=True, stop=True)
                        v.inc(last, "rr_ps")
                    v.wait("f_act", 4)
                    pe_attention(v, TAIL_ORDER, True)
                    v.wait("m_free", ring_of(TAIL_ORDER, "norm", NG - 1))
                    transposes(v, CTX)
                    v.wait("tr_dve", 3)
                    v.wait("tr_act", 3)
                    token_product(v, 4, WoutT, D, "yo2_ps")
                    transposes(v, A1, lambda pair: v.wait("a_ready", 6 + pair + 1))
                    v.wait("tr_dve", 4)
                    v.wait("tr_act", 4)
                    for t in range(NT):
                        for c in range(2):
                            last = pe.matmul(PS[:, 7, t * E_:(t + 1) * E_], XT[:, c, t * P:(t + 1) * P], Wg[:, c, :],
                                             start=(c == 0), stop=(c == 1))
                    v.inc(last, "lg_ps")

            @block.scalar
            def _(act):
                def first(l):
                    act.dma_start(Wqkcv[:], a["Wqkcv"][l]).then_inc(w_first, 16)
                    act.dma_start(bcol[:], a["bcol"][l]).then_inc(w_first, 16)
                    act.dma_start(brow[:, 0], a["brow"][l, 0].partition_broadcast(P)).then_inc(w_first, 16)

                def rest(l):
                    act.dma_start(Wo[:], a["Wo"][l]).then_inc(w_rest, 16)
                    act.dma_start(Wi[:], a["Wi"][l]).then_inc(w_rest, 16)
                    act.dma_start(Wo2[:], a["Wo2"][l]).then_inc(w_rest, 16)
                    act.dma_start(bicol[:], a["bicol"][l]).then_inc(w_rest, 16)
                    act.dma_start(brow[:, 1:7], a["brow"][l, 1:7].partition_broadcast(P)).then_inc(w_rest, 16)

                act.dma_start(HN, H0[0]).then_inc(h_in, 16)
                first(0)
                rest(0)
                act.wait_ge(w_once, 16 * NW_ONCE)
                with act.Fori(0, B) as b:
                    tv = tail.on(act, b)
                    norm_sd(tv, 1, 0)
                    with act.Fori(0, L) as l:
                        p = b * L + l
                        v = lay.on(act, p)
                        take_transposed(v, 0, 1, True)
                        act.wait_ge(w_first, p * (16 * NW_FIRST) + 16 * NW_FIRST)
                        act.wait_ge(hr_ready, b + 1)
                        for o, f in ((0, Fc), (1, Fk), (2, Fq)):
                            if o == 1:
                                for m in range(2):
                                    v.wait("n_ps", m + 1)
                                    v.inc(act.activation(halves(SQ[:, m, :]), chunk_view(0, m), ACT.Ln), "n_act")
                                for m in range(2):
                                    v.wait("n_act", 2)
                                    v.inc(act.activation(SQ[:, m, :], SQ[:, m, :], ACT.Exp, scale=-0.5), "n_act")
                            for m in range(2):
                                v.wait("f_ps", 2 * o + m + 1)
                                if o == 0:
                                    v.inc(act.activation(halves(SQ[:, m, :]), chunk_view(0, m), ACT.Square,
                                                         bias=bcol[:, o, m:m + 1]), "sq_act")
                                v.inc(act.activation(halves(f[:, m, :]), chunk_view(4 if o else 0, m),
                                                     ACT.Identity, bias=bcol[:, o, m:m + 1]), "f_act")
                        v.wait("v_dve", 3)
                        v.wait("f_act", 6)
                        first(l + 1)
                        act_attention(v, LAYER_ORDER, False)
                        take_transposed(v, 1, 1, True)
                        norm_sd(v, 1, 1)
                        take_transposed(v, 2, 1, True)
                        act.wait_ge(w_rest, p * (16 * NW_REST) + 16 * NW_REST)
                        for f in range(2 * NM):
                            m, h = divmod(f, 2)
                            v.wait("f1_ps", f + 1)
                            v.inc(act.activation(HT[:, m, h * HALF:(h + 1) * HALF], PS[:, 4 + f % 4, 0:HALF],
                                                 ACT.Gelu, bias=bicol[:, m:m + 1]), "g_act")
                        norm_sd(v, 2, 1)
                        act.wait_ge(x_ready, b * XPER + l * 3 + 6)
                        rest(l + 1)
                    v = tv
                    norm_sd(v, 2, 0)
                    take_transposed(v, 0, 1, True)
                    v.wait("f0_ps", 1)
                    v.inc(act.activation(halves(E[:, 0, :]), PS[:, 4:6, 0:HALF], ACT.Relu, bias=fcol[:]), "relu")
                    for m in range(2):
                        v.wait("pr_ps", m + 1)
                        v.inc(act.activation(halves(Fk[:, m, :]), chunk_view(0, m), ACT.Identity,
                                             bias=f2col[:, m:m + 1]), "pr_act")
                    norm_sd(v, 3, 0)
                    norm_sd(v, 4, 0)
                    take_transposed(v, 1, 1, True)
                    for o, f, bank in ((0, Fq, 0), (1, Fk, 4)):
                        for m in range(2):
                            v.wait("f_ps", 2 * o + m + 1)
                            v.inc(act.activation(halves(f[:, m, :]), chunk_view(bank, m), ACT.Identity,
                                                 bias=qkcol[:, o, m:m + 1]), "f_act")
                    for g in range(NG):
                        for t in range(NT):
                            n = g * NT + t
                            if n >= NXS:
                                v.wait(f"xs_w{n % NXS}", 16 * (n // NXS))
                            v.wait("rr_dve", t + 1)
                            xs = XS[n % NXS]
                            for h in range(G):
                                c, hh = divmod(g * G + h, 6)
                                if h and hh:
                                    continue
                                m = min(6 - hh, G - h)
                                r = PS[:, t, c * 256 + hh * NREL:c * 256 + (hh + m) * NREL].rearrange(
                                    "p (h r) -> p h r", h=m)
                                last = act.activation(xs[:, h:h + m, FILL:FILL + NREL], r, ACT.Copy)
                            v.inc(last, "xs_act")
                            for side, lo, hi in ((0, 0, FILL), (1, FILL + NREL, XL)):
                                v.inc(act.activation(
                                    xs[:, :, lo:hi],
                                    RB[:, t, g * G:(g + 1) * G, side:side + 1].broadcast_to([P, G, hi - lo]),
                                    ACT.Copy), "xs_act")
                    for r in range(NXS):
                        v.wait(f"xs_w{r}", 16 * NG * NT // NXS)
                    act_attention(v, TAIL_ORDER, True)
                    v.wait("av_ps", NG * NT)
                    act.dma_start(HN, H0[b + 1]).then_inc(h_in, 16)
                    take_transposed(v, 2, 1, True)
                    norm_sd(v, 5, 0)
                    v.wait("a_ready", 9)
                    act.dma_start(H1[b], HR[:]).then_inc(h_out, 16)
                    act.dma_start(XF[b], A1[:]).then_inc(h_out, 16)
                    take_transposed(v, 3, 1, True)
                    v.wait("out_ready", 1)
                    act.dma_start(LG[b], LGT[:]).then_inc(h_out, 16)
                act.wait_ge(h_in, 16 * (B + 1))
                act.wait_ge(h_out, 48 * B + 1)

            @block.vector
            def _(dve):
                dve.memset(VP[:], 2.0)
                dve.memset(AK[CORE:CORE + MROWS, :, :], 1.0).then_inc(h_out, 1)
                dve.wait_ge(h_out, 1)
                dve.memset(BS[:], 0.0)
                dve.memset(EPS[:, 0:1], 1e-5)
                dve.memset(EPS[:, 1:2], 1e-12)
                dve.wait_ge(w_once, 16 * NW_ONCE)
                dve.tensor_copy(idb[:], idf[:])
                dve.tensor_copy(OHB, OHF).then_inc(onehot_ready, 1)
                dve.tensor_scalar(negI[:], idf[:], -1.0, None, ALU.mult).then_inc(const_ready, 1)
                dve.wait_ge(const_ready, 1)
                with dve.Fori(0, B) as b:
                    tv = tail.on(dve, b)
                    dve.wait_ge(h_in, b * 16 + 16)
                    layer_norm(tv, None, HN, X, 1, lambda ins: ins.then_inc(x_ready, 1))
                    dve.wait_ge(h_out, b * 48 + 1)
                    dve.tensor_copy(HR[:], HN).then_inc(hr_ready, 1)
                    with dve.Fori(0, L) as l:
                        p = b * L + l
                        v = lay.on(dve, p)
                        take_transposed(v, 0, 0, False)
                        dve.wait_ge(w_first, p * (16 * NW_FIRST) + 16 * NW_FIRST)
                        for o, f, m in ((0, Fc, 0), (0, Fc, 1), (1, Fk, 0), (2, Fq, 0), (2, Fq, 1), (1, Fk, 1)):
                            if o == 0:
                                v.wait("n_act", 2 + m + 1)
                                v.link(dve.tensor_tensor(Fc[:, m, :], Fc[:, m, :], SQ[:, m, :], ALU.mult))
                            else:
                                v.wait("f_act", 2 * o + m + 1)
                            split(v, f, o, m, "p_dve")
                            if (o, m) == (2, 0):
                                dve_values(v, 0, brow[:, 0])
                        v.wait("p_dve", 6)
                        dve.wait_ge(w_rest, p * (16 * NW_REST) + 16 * NW_REST)
                        v.link(dve.tensor_tensor(X[:], X[:], row_bc(brow[:, 1], NT), ALU.add))
                        dve_attention(v, LAYER_ORDER, False)
                        take_transposed(v, 1, 0, False)
                        layer_norm(v, product(v, "y_ps", 4, lambda ts: X[:, ts, :], T2), T2, A1, 1,
                                   lambda ins: v.inc(ins, "a1_ready"), brow[:, 2], brow[:, 3])
                        take_transposed(v, 2, 0, False)
                        v.wait("tr_ps", 6)
                        v.link(dve.tensor_tensor(A1[:], A1[:], row_bc(brow[:, 4], NT), ALU.add))
                        layer_norm(v, product(v, "y2_ps", 4, lambda ts: A1[:, ts, :], T2), T2, X, 2,
                                   lambda ins: ins.then_inc(x_ready, 1), brow[:, 5], brow[:, 6])
                        v.close()
                    v = tv
                    dve.wait_ge(x_ready, b * XPER + XPER)
                    dve.wait_ge(hr_ready, b + 1)
                    v.link(dve.tensor_tensor(HR[:], HR[:], X[:], ALU.add))
                    layer_norm(v, None, HR, A1, 2, lambda ins: v.inc(ins, "a_ready"))
                    take_transposed(v, 0, 0, False)
                    layer_norm(v, product(v, "yo_ps", 4, lambda ts: row_bc(frow[:, 0], 2), T2), T2, X, 3,
                               v.link, frow[:, 1], frow[:, 2])
                    v.link(dve.tensor_tensor(HR[:], HR[:], X[:], ALU.add))
                    layer_norm(v, None, HR, A1, 4, lambda ins: v.inc(ins, "a_ready"))
                    take_transposed(v, 1, 0, False)
                    dve_values(v, 4, frow[:, 3])
                    v.wait("f_act", 1)
                    split(v, Fq, 0, 0, "p_dve")
                    for t in range(NT):
                        v.wait("rr_ps", t + 1)
                        r = PS[:, t, :].rearrange("p (c x) -> p c x", c=2)[:, :, 0:6 * NREL].rearrange(
                            "p c (h r) -> p c h r", h=6)
                        v.inc(dve.tensor_copy(RB[:, t].rearrange("p (c h) r -> p c h r", c=2),
                                              r[:, :, :, 0:NREL:NREL - 1]), "rr_dve")
                    for o, f, m in ((1, Fk, 0), (0, Fq, 1), (1, Fk, 1)):
                        v.wait("f_act", 2 * o + m + 1)
                        split(v, f, o, m, "p_dve")
                    v.wait("rr_dve", NT)
                    for t in range(NT):
                        if t:
                            ins = dve.tensor_copy(BS[:, t, :, 0:t], RB[:, t, :, 0:1].broadcast_to([P, H, t]))
                        if t < NT - 1:
                            ins = dve.tensor_copy(BS[:, t, :, t + 1:NT],
                                                  RB[:, t, :, 1:2].broadcast_to([P, H, NT - 1 - t]))
                    v.link(ins)
                    fix_window(v, 0)
                    v.link(dve.tensor_tensor(HR[:], HR[:], row_bc(frow[:, 4], NT), ALU.add))
                    v.wait("p_dve", 4)
                    dve_attention(v, TAIL_ORDER, True)
                    take_transposed(v, 2, 0, False)
                    layer_norm(v, product(v, "yo2_ps", 4, lambda ts: HR[:, ts, :], HR), HR, A1, 5,
                               lambda ins: v.inc(ins, "a_ready"))
                    take_transposed(v, 3, 0, False)
                    v.wait("lg_ps", 1)
                    v.inc(dve.tensor_copy(LGT[:], PS[:, 7, 0:NT * E_].rearrange("p (t e) -> p t e", t=NT)),
                          "out_ready")
                    v.close()

            @block.sync
            def _(sp):
                for dst, src in once:
                    sp.dma_start(dst, src).then_inc(w_once, 16)
                sp.wait_ge(onehot_ready, 1)
                sp.dma_start(ONES, AK[CORE:CORE + MROWS].rearrange("k h s -> k (h s)")).then_inc(ones_in, 16)
                for h in range(H):
                    sp.dma_start(CL[CORE:CORE + RROWS, h, :], OHB).then_inc(onehot_in, 16)
                sp.wait_ge(onehot_in, 16 * H)

                def spread(v, dst, o, part_of, sig, g):
                    hs = slice(g * G, (g + 1) * G)
                    for s_, k in enumerate(part_of):
                        v.inc(sp.dma_start(dst[s_ * DH:(s_ + 1) * DH, hs, :],
                                           PD[o, k].rearrange("(h d) t -> d h t", h=H)[:, hs, :]), sig, 16)

                def to_dram(v, o, m, n):
                    v.wait("p_dve", n + 1)
                    v.inc(sp.dma_start(PD[o].rearrange("k (c f) t -> f k c t", c=2)[:, :, m], parts[:, o, :, m]),
                          f"pd_w{n}", 16)

                with sp.Fori(0, B) as b:
                    with sp.Fori(0, L) as l:
                        v = lay.on(sp, b * L + l)

                        def cosine_operands(g):
                            spread(v, CL, 0, KEY_PARTS, f"c_in{g}", g)
                            spread(v, CR, 0, QRY_PARTS, f"c_in{g}", g)

                        def dot_operands(g):
                            spread(v, AK, 1, KEY_PARTS, f"qk_in{g}", g)
                            spread(v, AQ, 2, QRY_PARTS, f"qk_in{g}", g)

                        to_dram(v, 0, 0, 0)
                        v.wait("pd_w0", 16)
                        cosine_operands(0)
                        to_dram(v, 0, 1, 1)
                        to_dram(v, 1, 0, 2)
                        to_dram(v, 2, 0, 3)
                        v.wait("pd_w2", 16)
                        v.wait("pd_w3", 16)
                        dot_operands(0)
                        to_dram(v, 2, 1, 4)
                        to_dram(v, 1, 1, 5)
                        v.wait("pd_w1", 16)
                        cosine_operands(1)
                        v.wait("pd_w4", 16)
                        v.wait("pd_w5", 16)
                        dot_operands(1)
                        cosine_operands(2)
                        dot_operands(2)
                        for g in range(NG):
                            v.wait("m_free", ring_of(LAYER_ORDER, "bias", g))
                            v.inc(sp.dma_start(MD[:, g * G * NT:(g + 1) * G * NT].rearrange("k r t -> r k t"),
                                               MT[:]), f"md_w{g}", 16)
                            v.wait(f"md_w{g}", 16)
                            v.inc(sp.dma_start(
                                AQ[CORE:CORE + MROWS, g * G:(g + 1) * G, :].rearrange("k h s -> k (h s)"),
                                MD[:, g * G * NT:(g + 1) * G * NT].rearrange("k r t -> k (r t)")), f"md_r{g}", 16)
                    v = tail.on(sp, b)

                    def relative_scores(n0, n1):
                        for n in range(n0, n1):
                            g, t = divmod(n, NT)
                            v.wait("xs_act", 3 * n + 3)
                            v.inc(sp.dma_start(XD[t * P:(t + 1) * P, g * G:(g + 1) * G, :], XS[n % NXS]),
                                  f"xs_w{n % NXS}", 16)

                    def windows(h0, h1):
                        for h in range(h0, h1):
                            src = bass.AP(XD.tensor, h * XL + P - 1, [[H * XL - 1, P], [P * H * XL, NT], [1, WIN]])
                            v.inc(sp.dma_start(window(h), src), f"dw_in{h}", 16)

                    def operands(g):
                        spread(v, CR, 0, QRY_PARTS, f"qk_in{g}", g)
                        spread(v, CL, 1, KEY_PARTS, f"qk_in{g}", g)

                    relative_scores(0, NXS)
                    to_dram(v, 0, 0, 0)
                    to_dram(v, 1, 0, 1)
                    relative_scores(NXS, NT)
                    to_dram(v, 0, 1, 2)
                    to_dram(v, 1, 1, 3)
                    for r in range(NXS):
                        v.wait(f"xs_w{r}", 16 * NT // NXS)
                    windows(0, 1)
                    for n in range(4):
                        v.wait(f"pd_w{n}", 16)
                    operands(0)
                    windows(1, G)
                    relative_scores(NT, 2 * NT)
                    for r in range(NXS):
                        v.wait(f"xs_w{r}", 2 * 16 * NT // NXS)
                    windows(G, 2 * G)
                    operands(1)
                    relative_scores(2 * NT, 3 * NT)
                    for r in range(NXS):
                        v.wait(f"xs_w{r}", 3 * 16 * NT // NXS)
                    windows(2 * G, H)
                    operands(2)
                    for g in range(NG):
                        v.wait("m_free", ring_of(TAIL_ORDER, "bias", g))
                        v.inc(sp.dma_start(RD[:, g * G * NT:(g + 1) * G * NT].rearrange("k r t -> r k t"), MT1),
                              f"md_w{g}", 16)
                        v.wait(f"md_w{g}", 16)
                        for k in range(3):
                            v.inc(sp.dma_start(
                                CR[CORE + k * NT:CORE + (k + 1) * NT, g * G:(g + 1) * G, :],
                                RD[k, g * G * NT:(g + 1) * G * NT].rearrange("(h t) s -> t h s", h=G)), f"md_r{g}", 16)
                    v.wait("sc_ps", 4 * NT * NG)
                    sp.dma_start(AK[CORE:CORE + MROWS].rearrange("k h s -> k (h s)"), ONES).then_inc(ones_in, 16)
                sp.wait_ge(ones_in, 16 * (B + 1))


def experts(nc, a, H1, XF, LG, XG, YD, out):
    with ExitStack() as ctx:
        sb = lambda n, s, d: ctx.enter_context(nc.sbuf_tensor(n, s, d))
        sem = lambda n: ctx.enter_context(nc.semaphore(n))
        T = B * NT
        lg = sb("lg", [P, T, E_], F32)
        xf = sb("xf", [P, T, D], F32)
        h1 = sb("h1", [P, T, D], F32)
        gy = sb("gy", [P, T, TOPK, D], F32)
        v8 = sb("v8", [P, T, 8], F32)
        i8 = sb("i8", [P, T, 8], U32)
        idx = sb("idx", [P, T, TOPK], F32)
        iota = sb("iota", [P, E_], F32)
        oh = sb("oh", [P, T, TOPK, E_], F32)
        ohb = sb("ohb", [P, T, TOPK, E_], BF16)
        trif = sb("trif", [P, P], F32)
        trib = sb("trib", [P, P], BF16)
        oneb = sb("oneb", [P, P], BF16)
        idm = sb("idm", [P, P], F32)
        tot = sb("tot", [P, T, TOPK * E_], F32)
        pre = [sb(f"pre{i}", [P, T, TOPK * E_], F32) for i in range(2)]
        pos = sb("pos", [P, T, TOPK], F32)
        keep = sb("keep", [P, T, TOPK], F32)
        slot = sb("slot", [P, T, TOPK], F32)
        koff = sb("koff", [P, TOPK], F32)
        sidf = sb("sidf", [P, T, TOPK], F32)
        sid = sb("sid", [P, T, TOPK], I32)
        gidf = sb("gidf", [P, T, TOPK], F32)
        gid = sb("gid", [P, T, TOPK], I32)
        dv = sb("dv", [P, T], F32)
        ew = sb("ew", [P, T], F32)
        den = sb("den", [P, T], F32)
        w = sb("w", [P, T, TOPK], F32)
        w1 = sb("w1", [FC, 2, 2, 2 * HID], F32)
        w2 = sb("w2", [P, 2, 4, D], F32)
        xg = sb("xg", [CP, 2, CC, D], F32)
        xgT = sb("xgT", [FC, 2, 2, CAP], F32)
        sg = sb("sg", [P, 2, CAP], F32)
        at = sb("at", [P, 2, 4, CAP], F32)
        ye = sb("ye", [CP, 2, CC, D], F32)
        PS = ctx.enter_context(nc.psum_tensor("PSX", [P, 8, BANK], F32))

        const_in, lg_in, xf_in, h1_in = sem("x_const_in"), sem("lg_in"), sem("xf_in"), sem("h1_in")
        oh_ready, pos_ps, dv_ready, ew_ready = sem("oh_ready"), sem("pos_ps"), sem("dv_ready"), sem("ew_ready")
        sid_ready, gid_ready, step = sem("sid_ready"), sem("gid_ready"), sem("x_step")
        scattered = [sem(f"scattered{k}") for k in range(TOPK)]
        gathered = [sem(f"gathered{k}") for k in range(TOPK)]
        done, stored = sem("x_done"), sem("x_stored")

        U = 2
        PASSES = NBLK // U

        def passes(eng, body):
            body(ex.on(eng, 0), 0)
            with eng.Fori(1, PASSES) as i:
                body(ex.on(eng, i), i)

        ex = Counts(nc, ctx, "e_", dict(w_in0=32, w_in1=32, xg_in0=16, xg_in1=16, y_out0=16, y_out1=16,
                                        xt_ps=2 * U, xt_dve=U, xt_act=U, ug_ps=4 * U, silu=4 * U, at=4 * U,
                                        y_ps=2 * U, ye=2 * U))

        with nc.Block() as block:
            @block.sync
            def _(sp):
                sp.dma_start(lg[:].rearrange("p (b t) e -> p b (t e)", b=B),
                             LG.rearrange("b p t e -> p b (t e)")).then_inc(lg_in, 16)
                sp.dma_start(xf[:].rearrange("p (b t) d -> p b (t d)", b=B),
                             XF.rearrange("b p t d -> p b (t d)")).then_inc(xf_in, 16)
                for dst, src in ((iota[:], a["iota"].partition_broadcast(P)), (koff[:], a["koff"].partition_broadcast(P)),
                                 (trif[:], a["tri"]), (idm[:], a["ident"])):
                    sp.dma_start(dst, src).then_inc(const_in, 16)
                sp.dma_start(h1[:].rearrange("p (b t) d -> p b (t d)", b=B),
                             H1.rearrange("b p t d -> p b (t d)")).then_inc(h1_in, 16)
                def loads(v, i, choice=None):
                    for u in range(U):
                        v.wait("y_ps", 2 * u - 2)
                        sp.wait_ge(const_in, 64)
                        v.inc(sp.dma_start(w1[:, u], a["W1"][U * i + u]), f"w_in{u}", 16)
                        v.inc(sp.dma_start(w2[:, u], a["W2"][U * i + u]), f"w_in{u}", 16)
                        if choice is not None and u == 0:
                            sp.wait_ge(scattered[choice], 16 * T)
                        v.wait("xt_ps", 2 * u - 2)
                        sp.wait_ge(const_in, 64)
                        v.inc(sp.dma_start(xg[:, u], XG[bass.ds((U * i + u) * CAP, CAP), :]
                                           .rearrange("(p c) d -> p c d", c=CC)), f"xg_in{u}", 16)

                loads(ex.on(sp, 0), 0, 0)
                with sp.Fori(1, PASSES // TOPK) as i:
                    loads(ex.on(sp, i), i)
                loads(ex.on(sp, PASSES // TOPK), PASSES // TOPK, 1)
                with sp.Fori(PASSES // TOPK + 1, PASSES) as i:
                    loads(ex.on(sp, i), i)
                sp.wait_ge(done, 1)
                sp.dma_start(out.rearrange("b (t p) d -> p (b t) d", p=P), h1[:]).then_inc(stored, 16)
                sp.wait_ge(stored, 16)

            @block.gpsimd
            def _(pool):
                pool.wait_ge(xf_in, 16)
                pool.wait_ge(sid_ready, 1)
                for k in range(TOPK):
                    for t in range(T):
                        pool.indirect_dma_start(
                            out=XG, out_offset=bass.IndirectOffsetOnAxis(ap=sid[:, t, k:k + 1], axis=0),
                            in_=xf[:, t, :], in_offset=None, bounds_check=SLOTS - 1, oob_is_err=False
                        ).then_inc(scattered[k], 16)
                pool.wait_ge(gid_ready, 1)
                for k in range(TOPK):
                    for u in range(U):
                        pool.wait_ge(ex.sem[f"y_out{u}"], 16 * (k + 1) * PASSES // TOPK)
                    for t in range(T):
                        pool.indirect_dma_start(
                            out=gy[:, t, k, :], out_offset=None, in_=YD[0:(k + 1) * E_ * CAP, :],
                            in_offset=bass.IndirectOffsetOnAxis(ap=gid[:, t, k:k + 1], axis=0)
                        ).then_inc(gathered[k], 16)

            @block.scalar
            def _(act):
                act.wait_ge(dv_ready, 1)
                act.activation(ew[:], dv[:], ACT.Exp).then_inc(ew_ready, 1)

                def store(v, i, u):
                    v.wait("ye", 2 * u + 2)
                    v.inc(act.dma_start(YD[bass.ds((U * i + u) * CAP, CAP), :]
                                        .rearrange("(p c) d -> p c d", c=CC), ye[:, u % 2]), f"y_out{u % 2}", 16)

                def silus(v, i):
                    for u in range(U):
                        v.wait("xt_ps", 2 * u + 2)
                        v.inc(act.activation(xgT[:, u % 2, 1, :], PS[0:FC, 1, 0:CAP], ACT.Copy), "xt_act")
                        for jj in range(4):
                            q = 4 * u + jj
                            v.wait("ug_ps", q + 1)
                            v.wait("at", q - 1)
                            v.inc(act.activation(sg[:, q % 2], PS[:, 3 + 2 * (q % 2), 0:CAP], ACT.Silu), "silu")
                            if u and jj == 1:
                                store(v, i, u - 1)
                    store(v, i, U - 1)

                passes(act, silus)

            @block.tensor
            def _(pe):
                pe.wait_ge(oh_ready, 1)
                ohm = ohb[:].rearrange("p t k e -> p (t k e)")
                pe.matmul(PS[:, 0, 0:T * TOPK * E_], trib[:], ohm, start=True, stop=True)
                pe.matmul(PS[:, 1, 0:T * TOPK * E_], oneb[:], ohm, start=True, stop=True).then_inc(pos_ps, 1)
                pe.wait_ge(sid_ready, 1)
                pe.wait_ge(const_in, 16 * 4)

                def blocks(v, i):
                    for u in range(U):
                        v.wait(f"xg_in{u % 2}", 16)
                        v.wait("xt_dve", u)
                        v.wait("xt_act", u)
                        for c in range(2):
                            for cc in range(CC):
                                last = pe.transpose(PS[0:FC, c, cc * CP:(cc + 1) * CP],
                                                    xg[:, u % 2, cc, c * FC:(c + 1) * FC], idm[0:CP, 0:CP])
                            v.inc(last, "xt_ps")
                        v.wait(f"w_in{u}", 32)
                        v.wait("xt_dve", u + 1)
                        v.wait("xt_act", u + 1)
                        for jj in range(4):
                            q = 4 * u + jj
                            v.wait("at", q - 1)
                            for half in range(2):
                                for c in range(2):
                                    last = pe.matmul(PS[:, 2 + 2 * (q % 2) + half, 0:CAP],
                                                     w1[:, u, c, half * HID + jj * P:half * HID + (jj + 1) * P],
                                                     xgT[:, u % 2, c, :], start=(c == 0), stop=(c == 1))
                            v.inc(last, "ug_ps")
                        v.wait("at", 4 * u + 4)
                        v.wait("ye", 2 * u)
                        for cc in range(CC):
                            for jj in range(4):
                                last = pe.matmul(PS[0:CP, 6 + cc // 2, (cc % 2) * 256:(cc % 2) * 256 + D],
                                                 at[:, u % 2, jj, cc * CP:(cc + 1) * CP], w2[:, u, jj, :],
                                                 start=(jj == 0), stop=(jj == 3))
                            if cc % 2:
                                v.inc(last, "y_ps")

                passes(pe, blocks)

            @block.vector
            def _(dve):
                links = [0]

                def link(ins):
                    links[0] += 1
                    ins.then_inc(step, 1)
                    dve.wait_ge(step, links[0])

                dve.memset(oneb[:], 1.0)
                dve.wait_ge(lg_in, 16)
                dve.wait_ge(const_in, 16 * 4)
                link(dve.tensor_copy(trib[:], trif[:]))
                for t in range(T):
                    ins = dve.max(v8[:, t, :], lg[:, t, :])
                link(ins)
                for t in range(T):
                    ins = dve.max_index(i8[:, t, :], v8[:, t, :], lg[:, t, :])
                link(ins)
                dve.tensor_tensor(dv[:], v8[:, :, 1], v8[:, :, 0], ALU.subtract).then_inc(dv_ready, 1)
                link(dve.tensor_copy(idx[:], i8[:, :, 0:TOPK]))
                for k in range(TOPK):
                    ins = dve.tensor_tensor(oh[:, :, k, :], idx[:, :, k:k + 1].broadcast_to([P, T, E_]),
                                            iota[:].unsqueeze(1).broadcast_to([P, T, E_]), ALU.is_equal)
                link(ins)
                dve.tensor_copy(ohb[:], oh[:]).then_inc(oh_ready, 1)
                dve.wait_ge(pos_ps, 1)
                three = lambda bank: PS[:, bank, 0:T * TOPK * E_].rearrange("p (t x) -> p t x", t=T)
                link(dve.tensor_copy(tot[:], three(1)))
                link(dve.tensor_copy(pre[0][:], tot[:]))
                src, s_ = 0, 1
                while s_ < T:
                    link(dve.tensor_tensor(pre[1 - src][:, s_:T], pre[src][:, s_:T], pre[src][:, 0:T - s_], ALU.add))
                    link(dve.tensor_copy(pre[1 - src][:, 0:s_], pre[src][:, 0:s_]))
                    src, s_ = 1 - src, 2 * s_
                link(dve.tensor_tensor(pre[src][:], pre[src][:], tot[:], ALU.subtract))
                link(dve.tensor_tensor(pre[src][:], pre[src][:], three(0), ALU.add))
                ohv = oh[:].rearrange("p t k e -> p t (k e)")
                link(dve.tensor_tensor(pre[src][:], pre[src][:], ohv, ALU.mult))
                link(dve.tensor_reduce(pos[:], pre[src][:].rearrange("p t (k e) -> p t k e", k=TOPK), AX.X, ALU.add))
                link(dve.tensor_scalar(keep[:], pos[:], float(CAP), None, ALU.is_le))
                link(dve.scalar_tensor_tensor(out=slot[:], in0=idx[:], scalar=float(CAP), in1=pos[:],
                                              op0=ALU.mult, op1=ALU.add))
                link(dve.tensor_tensor(slot[:], slot[:], koff[:].unsqueeze(1).broadcast_to([P, T, TOPK]), ALU.add))
                link(dve.tensor_scalar(sidf[:], keep[:], float(-2 * SLOTS), float(2 * SLOTS), ALU.mult, ALU.add))
                link(dve.tensor_tensor(sidf[:], sidf[:], slot[:], ALU.add))
                dve.tensor_copy(sid[:], sidf[:]).then_inc(sid_ready, 1)
                link(dve.tensor_tensor(gidf[:], slot[:], keep[:], ALU.mult))
                dve.tensor_copy(gid[:], gidf[:]).then_inc(gid_ready, 1)
                dve.wait_ge(ew_ready, 1)
                link(dve.tensor_scalar(den[:], ew[:], 1.0, None, ALU.add))
                link(dve.reciprocal(den[:], den[:]))
                link(dve.tensor_copy(w[:, :, 0], den[:]))
                link(dve.tensor_tensor(w[:, :, 1], den[:], ew[:], ALU.mult))
                link(dve.tensor_tensor(w[:], w[:], keep[:], ALU.mult))

                def products(v, i):
                    for u in range(U):
                        v.wait("xt_ps", 2 * u + 1)
                        v.inc(dve.tensor_copy(xgT[:, u % 2, 0, :], PS[0:FC, 0, 0:CAP]), "xt_dve")
                        for jj in range(4):
                            q = 4 * u + jj
                            v.wait("silu", q + 1)
                            v.wait("y_ps", 2 * u - 2)
                            v.inc(dve.tensor_tensor(at[:, u % 2, jj, :], PS[:, 2 + 2 * (q % 2), 0:CAP], sg[:, q % 2],
                                                    ALU.mult), "at")
                        for c in range(2):
                            v.wait("y_ps", 2 * u + c + 1)
                            v.wait(f"y_out{u}", 0)
                            o = PS[0:CP, 6 + c, :].rearrange("p (t x) -> p t x", t=2)[:, :, 0:D]
                            v.inc(dve.tensor_copy(ye[:, u % 2, 2 * c:2 * c + 2, :], o), "ye")

                passes(dve, products)
                dve.wait_ge(h1_in, 16)
                for k in range(TOPK):
                    dve.wait_ge(gathered[k], 16 * T)
                    for t in range(T):
                        ins = dve.scalar_tensor_tensor(out=h1[:, t, :], in0=gy[:, t, k, :], scalar=w[:, t, k:k + 1],
                                                       in1=h1[:, t, :], op0=ALU.mult, op1=ALU.add)
                    if k < TOPK - 1:
                        link(ins)
                ins.then_inc(done, 1)


def program(nc, a, out, scratch):
    embed(nc, a, scratch["H0"], scratch["XG"])
    layers(nc, a, scratch["H0"], scratch["H1"], scratch["XF"], scratch["LG"], scratch["PD"], scratch["MD"],
           scratch["RD"], scratch["XD"], scratch["ONES"])
    experts(nc, a, scratch["H1"], scratch["XF"], scratch["LG"], scratch["XG"], scratch["YD"], out)


def chunks(w):
    return w.reshape(2, FC, -1).transpose(1, 0, 2)


def kernel(**x):
    import numpy as np
    import concourse.bacc as bacc
    from concourse.bass_utils import run_bass_kernel_spmd as run

    x = {k: np.asarray(v) for k, v in x.items()}
    again = list(range(L)) + [0]
    col = lambda v, n: v.reshape(-1, n).T
    la = {k[8:]: v for k, v in x.items() if k.startswith("L0_attn_")}
    a = {
        "ids": x["x_txt"].reshape(B * 4, P).T,
        "curve": x["L0_tok_curve"].reshape(2, P, 2).transpose(1, 0, 2),
        "tok_w": x["L0_tok_proj_w"].T,
        "tok_b": x["L0_tok_proj_b"],
        "txt_w": x["L0_txt_weights"],
        "colmask": (np.arange(D)[None, :] < np.array([192, 96, 144, 192])[:, None]).astype(np.float32),
        "emb": x["L0_txt_emb_weight"],
        "img": x["x"].reshape(-1, 1),
        "ident": np.eye(P, dtype=np.float32),
        "headblk": np.kron(np.eye(H // 2), np.ones((DH, DH))).astype(np.float32),
        "onehot": np.tile(np.kron(np.eye(NT), np.ones((1, P))), (3, 1)).astype(np.float32),
        "Wqkcv": np.stack([np.concatenate([chunks(la[k][l]) for k in ("Wq", "Wk", "Wc", "Wv")], axis=2)
                           for l in again]),
        "bcol": np.stack([np.stack([col(la[k][l], FC) for k in ("bc", "bk", "bq")], axis=1) for l in again]),
        "Wo": np.stack([chunks(la["Wo"][l]) for l in again]),
        "Wi": np.stack([chunks(la["Wi"][l]) for l in again]),
        "Wo2": np.stack([la["Wo2"][l].reshape(NM, P, D).transpose(1, 0, 2) for l in again]),
        "bicol": np.stack([col(la["bi"][l], P) for l in again]),
        "brow": np.stack([np.stack([la[k][l] for k in ("bv", "bo", "g1", "b1", "bo2", "g2", "b2")])
                          for l in again]),
        "W1T": chunks(x["L0_ffn_W1"].T),
        "W2T": x["L0_ffn_W2"].T,
        "WoT": chunks(x["L0_ffn_Wo"].T),
        "WqkvT": chunks(x["L1_attn_qkv_w"].T),
        "WoutT": chunks(x["L1_attn_out_w"].T),
        "Wg": chunks(x["L1_ffn_Wg"]),
        "relbd": block_diagonal(np, x["L1_attn_rel_pos_emb"].T),
        "fcol": x["L0_ffn_b1"].reshape(P, 1),
        "f2col": col(x["L0_ffn_b2"], FC),
        "qkcol": np.stack([col(x["L1_attn_qkv_b"][i * D:(i + 1) * D], FC) for i in range(2)], axis=1),
        "frow": np.stack([x["L0_ffn_bo"], x["L0_ffn_gamma"], x["L0_ffn_beta"], x["L1_attn_qkv_b"][2 * D:],
                          x["L1_attn_out_b"]]),
        "iota": np.arange(E_, dtype=np.float32),
        "koff": np.array([k * E_ * CAP - 1 for k in range(TOPK)], np.float32),
        "tri": np.triu(np.ones((P, P), np.float32)),
        "W1": np.stack([chunks(w) for w in x["L1_ffn_W1"]] * TOPK),
        "W2": np.tile(x["L1_ffn_W2"].reshape(E_, 4, P, D).transpose(0, 2, 1, 3), (TOPK, 1, 1, 1)),
    }
    a = {k: np.ascontiguousarray(v) for k, v in a.items()}
    nc = bacc.Bacc("TRN2", target_bir_lowering=False, num_devices=1)
    aps = {k: nc.dram_tensor("in_" + k, v.shape, mybir.dt.from_np(v.dtype), kind="ExternalInput").ap()
           for k, v in a.items()}
    out = nc.dram_tensor("out_0", (B, S, D), F32, kind="ExternalOutput").ap()
    scratch = {k: nc.dram_tensor("scratch_" + k, shape, dt).ap() for k, shape, dt in (
        ("H0", (B + 1, P, NT, D), F32), ("H1", (B, P, NT, D), F32), ("XF", (B, P, NT, D), F32),
        ("LG", (B, P, NT, E_), F32), ("XG", (SLOTS, D), F32), ("YD", (SLOTS, D), F32),
        ("PD", (3, 3, D, S), BF16), ("MD", (3, H * NT, P), BF16), ("RD", (3, H * NT, S), BF16),
        ("XD", (S, H, XL), F32), ("ONES", (MROWS, H * S), BF16))}
    program(nc, aps, out, scratch)
    r = run(nc, [{"in_" + k: v for k, v in a.items()}], core_ids=[0])
    return r.results[0]["out_0"]


def block_diagonal(np, w):
    out = np.zeros((FC, (H // 2) * NREL), w.dtype)
    for h in range(H // 2):
        out[h * DH:(h + 1) * DH, h * NREL:(h + 1) * NREL] = w
    return out
```
